# Optimizing a Trainium2 kernel written in Bass

```python
import numpy as np
import jax
import jax.numpy as jnp

def _softmax(x, axis=-1):
    return jax.nn.softmax(x, axis=axis)

def _gelu(x):
    return jax.nn.gelu(x, approximate=True)

def _silu(x):
    return jax.nn.silu(x)

def _sigmoid(x):
    return jax.nn.sigmoid(x)

def _layernorm(x, axis=-1, eps=1e-05):
    m = jnp.mean(x, axis=axis, keepdims=True)
    v = jnp.var(x, axis=axis, keepdims=True)
    return (x - m) / jnp.sqrt(v + eps)

def _scatter_add(tgt, idx, src, axis=0):
    return tgt.at[idx].add(src)

def _segment_sum(src, seg, n):
    return jax.ops.segment_sum(src, seg, n)
kernel_name = 'mk_seq_preln_d2_jaxref_r8_f3012a'

def setup_inputs(seed: int=0):
    np.random.seed(seed)
    _w = jnp.asarray

    def _L0_attn_setup():
        import jax, jax.numpy as jnp
        import numpy as np
        BATCH, T, HID = (4, 256, 128)
        H = P = 128
        EPS = 1e-05
        DISCRETIZATION = 'IM'

        def _linoss(x, B_param, C_param, A_diag, dt_p, D):
            A = jax.nn.relu(A_diag)
            dt = jax.nn.sigmoid(dt_p)
            Bu = jnp.einsum('bth,phc->btpc', x, B_param)
            if DISCRETIZATION == 'IM':
                S = 1.0 / (1.0 + dt * dt * A)
                m11, m12, m21, m22 = (S, -dt * A * S, dt * S, S)
                f1, f2 = (dt * S, dt * dt * S)
            else:
                one = jnp.ones_like(dt)
                m11, m12, m21, m22 = (one, -dt * A, dt, 1.0 - dt * dt * A)
                f1, f2 = (dt, dt * dt)
            c = lambda v: v[None, :, None]

            def step(carry, bu):
                z, y = carry
                z1 = c(m11) * z + c(m12) * y + c(f1) * bu
                y1 = c(m21) * z + c(m22) * y + c(f2) * bu
                return ((z1, y1), y1)
            z0 = jnp.zeros((x.shape[0], A.shape[0], 2), x.dtype)
            _, ys = jax.lax.scan(step, (z0, z0), jnp.swapaxes(Bu, 0, 1))
            ys = jnp.swapaxes(ys, 0, 1)
            o = jnp.einsum('btp,hp->bth', ys[..., 0], C_param[..., 0]) - jnp.einsum('btp,hp->bth', ys[..., 1], C_param[..., 1])
            return o + x * D
        key = jax.random.key(seed)
        ks = jax.random.split(key, 10)
        std_b = 1.0 / np.sqrt(H)
        std_c = 1.0 / np.sqrt(P)
        u = lambda k, s, lo, hi: jax.random.uniform(k, s, jnp.float32, lo, hi)
        return {'hidden_states': jax.random.normal(ks[0], (BATCH, T, HID), jnp.float32), 'Wi': jax.random.normal(ks[1], (H, HID), jnp.float32) / np.sqrt(HID), 'Wg': jax.random.normal(ks[2], (H, HID), jnp.float32) / np.sqrt(HID), 'Wo': jax.random.normal(ks[3], (HID, H), jnp.float32) / np.sqrt(H), 'A_diag': u(ks[4], (P,), 0.0, 1.0), 'B_param': u(ks[5], (P, H, 2), -std_b, std_b), 'C_param': u(ks[6], (H, P, 2), -std_c, std_c), 'D': jax.random.normal(ks[7], (H,), jnp.float32), 'dt': u(ks[8], (P,), 0.0, 1.0), 'norm_weight': jnp.ones((H,), jnp.float32)}
    _L0_attn_in = _L0_attn_setup()

    def _L0_ffn_setup():
        import jax, jax.numpy as jnp
        import numpy as np
        B, S, D, E = (4, 512, 128, 8)
        key = jax.random.key(seed)
        k1, k2, k3, k4, k5 = jax.random.split(key, 5)
        scale = 1.0 / np.sqrt(D)
        return {'x': jax.random.normal(k1, (B, S, D), dtype=jnp.float32), 'Wg': jax.random.normal(k2, (D, D), dtype=jnp.float32) * scale, 'bg': jnp.zeros((D,), dtype=jnp.float32), 'We': jax.random.normal(k3, (E, D, D), dtype=jnp.float32) * scale, 'be': jnp.zeros((E, D), dtype=jnp.float32)}
    _L0_ffn_in = _L0_ffn_setup()

    def _L1_attn_setup():
        import jax, jax.numpy as jnp
        import numpy as np
        B, T, C = (4, 256, 128)
        H = 16
        D = C // H
        key = jax.random.key(seed)
        k1, k2, k3, k4, k5 = jax.random.split(key, 5)
        s = 0.02
        return {'x': jax.random.normal(k1, (B, T, C), dtype=jnp.float32), 'W_qkv': jax.random.normal(k2, (C, 3 * C), dtype=jnp.float32) * s, 'b_qkv': jax.random.normal(k3, (3 * C,), dtype=jnp.float32) * s, 'W_o': jax.random.normal(k4, (C, C), dtype=jnp.float32) * s, 'b_o': jax.random.normal(k5, (C,), dtype=jnp.float32) * s}
    _L1_attn_in = _L1_attn_setup()

    def _L1_ffn_setup():
        import jax, jax.numpy as jnp
        import numpy as np
        DIM = 128
        DEPTH = 6
        HEADS = 16
        DIM_HEAD = 64
        WINDOW = 32
        INNER = HEADS * DIM_HEAD
        DIM_INNER = int(DIM * 4 * 2 / 3)
        QK_SCALE = 8.0

        def shift_tokens(t):
            a, s = jnp.split(t, 2, -1)
            s = jnp.pad(s, ((0, 0), (1, 0), (0, 0)))[:, :-1]
            return jnp.concatenate([a, s], -1)

        def l2norm(t):
            return t / jnp.maximum(jnp.linalg.norm(t, axis=-1, keepdims=True), 1e-12)

        def rotate_half(x):
            x1, x2 = jnp.split(x, 2, -1)
            return jnp.concatenate([-x2, x1], -1)

        def rotary_tables(n):
            half = jnp.arange(0, DIM_HEAD, 2, dtype=jnp.float32)
            inv_freq = 1.0 / 10000.0 ** (half / DIM_HEAD)
            t = jnp.arange(n, dtype=jnp.float32)
            freqs = t[:, None] * inv_freq[None, :]
            freqs = jnp.concatenate([freqs, freqs], -1)
            base_scale = (half + 0.4 * DIM_HEAD) / (1.4 * DIM_HEAD)
            power = (t - n // 2) / (WINDOW // 2)
            scale = base_scale[None, :] ** power[:, None]
            scale = jnp.concatenate([scale, scale], -1)
            return (freqs, scale)

        def local_attention(q, k, v):
            b, h, n, d = q.shape
            w = WINDOW
            nw = n // w
            bq = q.reshape(b, h, nw, w, d)
            bk = k.reshape(b, h, nw, w, d)
            bv = v.reshape(b, h, nw, w, d)

            def look(t):
                p = jnp.pad(t, ((0, 0), (0, 0), (1, 0), (0, 0), (0, 0)))
                return jnp.concatenate([p[:, :, :nw], p[:, :, 1:]], axis=3)
            bk2, bv2 = (look(bk), look(bv))
            seq = jnp.arange(n).reshape(nw, w)
            seq_p = jnp.pad(seq, ((1, 0), (0, 0)), constant_values=-1)
            jt = jnp.concatenate([seq_p[:nw], seq_p[1:]], axis=1)
            it = seq[:, :, None]
            jb = jt[:, None, :]
            mask = (it < jb) | (it > jb + w) | (jb == -1)
            sim = jnp.einsum('bhwie,bhwje->bhwij', bq, bk2) * QK_SCALE
            sim = jnp.where(mask, -jnp.finfo(sim.dtype).max, sim)
            attn = jax.nn.softmax(sim, -1)
            out = jnp.einsum('bhwij,bhwje->bhwie', attn, bv2)
            return out.reshape(b, h, n, d)

        def attn_layer(x, Wqkv, qs, ksc, Wo):
            b, n, _ = x.shape
            qkv = x @ Wqkv
            q, k, v = jnp.split(qkv, 3, -1)
            sh = lambda t: t.reshape(b, n, HEADS, DIM_HEAD).transpose(0, 2, 1, 3)
            q, k, v = (sh(q), sh(k), sh(v))
            q = l2norm(q) * qs
            k = l2norm(k) * ksc
            freqs, scale = rotary_tables(n)
            cos, sin = (jnp.cos(freqs), jnp.sin(freqs))
            q = q * cos * scale + rotate_half(q) * sin * scale
            inv = 1.0 / scale
            k = k * cos * inv + rotate_half(k) * sin * inv
            out = local_attention(q, k, v)
            out = out.transpose(0, 2, 1, 3).reshape(b, n, INNER)
            return out @ Wo

        def ffn_layer(x, g, bln, W1, b1, W2, b2):
            mu = x.mean(-1, keepdims=True)
            var = ((x - mu) ** 2).mean(-1, keepdims=True)
            xn = (x - mu) / jnp.sqrt(var + 1e-05) * g + bln
            hg = xn @ W1 + b1
            a, gate = jnp.split(hg, 2, -1)
            return a * jax.nn.gelu(gate, approximate=False) @ W2 + b2
        key = jax.random.key(seed)
        ks = jax.random.split(key, 8)
        B, N = (2, 256)
        init = lambda k, shape: jax.random.normal(k, shape, jnp.float32) * 0.02
        return {'x': jax.random.normal(ks[0], (B, N, DIM), jnp.float32), 'Wqkv': init(ks[1], (DEPTH, DIM, 3 * INNER)), 'q_scale': jnp.ones((DEPTH, DIM_HEAD), jnp.float32), 'k_scale': jnp.ones((DEPTH, DIM_HEAD), jnp.float32), 'Wo': init(ks[2], (DEPTH, INNER, DIM)), 'ln_g': jnp.ones((DEPTH, DIM), jnp.float32), 'ln_b': jnp.zeros((DEPTH, DIM), jnp.float32), 'W1': init(ks[3], (DEPTH, DIM, 2 * DIM_INNER)), 'b1': jnp.zeros((DEPTH, 2 * DIM_INNER), jnp.float32), 'W2': init(ks[4], (DEPTH, DIM_INNER, DIM)), 'b2': jnp.zeros((DEPTH, DIM), jnp.float32)}
    _L1_ffn_in = _L1_ffn_setup()
    _d = {'L0_attn_hidden_states': _L0_attn_in['hidden_states'], 'L0_attn_Wi': _L0_attn_in['Wi'], 'L0_attn_Wg': _L0_attn_in['Wg'], 'L0_attn_Wo': _L0_attn_in['Wo'], 'L0_attn_A_diag': _L0_attn_in['A_diag'], 'L0_attn_B_param': _L0_attn_in['B_param'], 'L0_attn_C_param': _L0_attn_in['C_param'], 'L0_attn_D': _L0_attn_in['D'], 'L0_attn_dt': _L0_attn_in['dt'], 'L0_attn_norm_weight': _L0_attn_in['norm_weight'], 'L0_ffn_Wg': _L0_ffn_in['Wg'], 'L0_ffn_bg': _L0_ffn_in['bg'], 'L0_ffn_We': _L0_ffn_in['We'], 'L0_ffn_be': _L0_ffn_in['be'], 'L1_attn_W_qkv': _L1_attn_in['W_qkv'], 'L1_attn_b_qkv': _L1_attn_in['b_qkv'], 'L1_attn_W_o': _L1_attn_in['W_o'], 'L1_attn_b_o': _L1_attn_in['b_o'], 'L1_ffn_Wqkv': _L1_ffn_in['Wqkv'], 'L1_ffn_q_scale': _L1_ffn_in['q_scale'], 'L1_ffn_k_scale': _L1_ffn_in['k_scale'], 'L1_ffn_Wo': _L1_ffn_in['Wo'], 'L1_ffn_ln_g': _L1_ffn_in['ln_g'], 'L1_ffn_ln_b': _L1_ffn_in['ln_b'], 'L1_ffn_W1': _L1_ffn_in['W1'], 'L1_ffn_b1': _L1_ffn_in['b1'], 'L1_ffn_W2': _L1_ffn_in['W2'], 'L1_ffn_b2': _L1_ffn_in['b2']}
    _x0 = _d['L0_attn_hidden_states']
    _d['L0_attn_hidden_states'] = jax.random.normal(jax.random.fold_in(jax.random.key(seed), 1), (1, 2048, 128), dtype=_x0.dtype)
    del _x0
    return _d

def reference(L0_attn_hidden_states, L0_attn_Wi, L0_attn_Wg, L0_attn_Wo, L0_attn_A_diag, L0_attn_B_param, L0_attn_C_param, L0_attn_D, L0_attn_dt, L0_attn_norm_weight, L0_ffn_Wg, L0_ffn_bg, L0_ffn_We, L0_ffn_be, L1_attn_W_qkv, L1_attn_b_qkv, L1_attn_W_o, L1_attn_b_o, L1_ffn_Wqkv, L1_ffn_q_scale, L1_ffn_k_scale, L1_ffn_Wo, L1_ffn_ln_g, L1_ffn_ln_b, L1_ffn_W1, L1_ffn_b1, L1_ffn_W2, L1_ffn_b2):

    def _L0_attn_ref(hidden_states, Wi, Wg, Wo, A_diag, B_param, C_param, D, dt, norm_weight):
        import jax, jax.numpy as jnp
        import numpy as np
        BATCH, T, HID = (4, 256, 128)
        H = P = 128
        EPS = 1e-05
        DISCRETIZATION = 'IM'

        def _linoss(x, B_param, C_param, A_diag, dt_p, D):
            A = jax.nn.relu(A_diag)
            dt = jax.nn.sigmoid(dt_p)
            Bu = jnp.einsum('bth,phc->btpc', x, B_param)
            if DISCRETIZATION == 'IM':
                S = 1.0 / (1.0 + dt * dt * A)
                m11, m12, m21, m22 = (S, -dt * A * S, dt * S, S)
                f1, f2 = (dt * S, dt * dt * S)
            else:
                one = jnp.ones_like(dt)
                m11, m12, m21, m22 = (one, -dt * A, dt, 1.0 - dt * dt * A)
                f1, f2 = (dt, dt * dt)
            c = lambda v: v[None, :, None]

            def step(carry, bu):
                z, y = carry
                z1 = c(m11) * z + c(m12) * y + c(f1) * bu
                y1 = c(m21) * z + c(m22) * y + c(f2) * bu
                return ((z1, y1), y1)
            z0 = jnp.zeros((x.shape[0], A.shape[0], 2), x.dtype)
            _, ys = jax.lax.scan(step, (z0, z0), jnp.swapaxes(Bu, 0, 1))
            ys = jnp.swapaxes(ys, 0, 1)
            o = jnp.einsum('btp,hp->bth', ys[..., 0], C_param[..., 0]) - jnp.einsum('btp,hp->bth', ys[..., 1], C_param[..., 1])
            return o + x * D
        x = hidden_states @ Wi.T
        o = _linoss(x, B_param, C_param, A_diag, dt, D)
        g = hidden_states @ Wg.T
        o = o * jax.lax.rsqrt(jnp.mean(o * o, axis=-1, keepdims=True) + EPS) * norm_weight
        o = o * (g * jax.nn.sigmoid(g))
        return o @ Wo.T

    def _L0_ffn_ref(x, Wg, bg, We, be):
        import jax, jax.numpy as jnp
        import numpy as np
        B, S, D, E = (4, 512, 128, 8)
        probs = jax.nn.softmax(x @ Wg + bg, axis=-1)
        idx = jnp.argmax(probs, axis=-1)
        p = jnp.take_along_axis(probs, idx[..., None], axis=-1)[..., 0]
        e_idx = idx % We.shape[0]
        h = jax.nn.relu(jnp.einsum('bsd,edf->besf', x, We) + be[None, :, None, :])
        onehot = jax.nn.one_hot(e_idx, We.shape[0], dtype=x.dtype)
        out = jnp.einsum('besf,bse->bsf', h, onehot) * p[..., None]
        return out

    def _L1_attn_ref(x, W_qkv, b_qkv, W_o, b_o):
        import jax, jax.numpy as jnp
        import numpy as np
        B, T, C = (4, 256, 128)
        H = 16
        D = C // H
        b, t, c = x.shape
        scaling = D ** (-0.5)
        qkv = x @ W_qkv + b_qkv
        q, k, v = jnp.split(qkv, 3, axis=-1)
        q = q.reshape(b, t, H, D).transpose(0, 2, 1, 3)
        k = k.reshape(b, t, H, D).transpose(0, 2, 1, 3)
        v = v.reshape(b, t, H, D).transpose(0, 2, 1, 3)
        scores = jnp.einsum('bhqd,bhkd->bhqk', q, k) * scaling
        mask = jnp.tril(jnp.ones((t, t), dtype=bool))
        scores = jnp.where(mask[None, None, :, :], scores, -jnp.inf)
        probs = jax.nn.softmax(scores, axis=-1)
        out = jnp.einsum('bhqk,bhkd->bhqd', probs, v)
        out = out.transpose(0, 2, 1, 3).reshape(b, t, c)
        return out @ W_o + b_o

    def _L1_ffn_ref(x, Wqkv, q_scale, k_scale, Wo, ln_g, ln_b, W1, b1, W2, b2):
        import jax, jax.numpy as jnp
        import numpy as np
        DIM = 128
        DEPTH = 6
        HEADS = 16
        DIM_HEAD = 64
        WINDOW = 32
        INNER = HEADS * DIM_HEAD
        DIM_INNER = int(DIM * 4 * 2 / 3)
        QK_SCALE = 8.0

        def shift_tokens(t):
            a, s = jnp.split(t, 2, -1)
            s = jnp.pad(s, ((0, 0), (1, 0), (0, 0)))[:, :-1]
            return jnp.concatenate([a, s], -1)

        def l2norm(t):
            return t / jnp.maximum(jnp.linalg.norm(t, axis=-1, keepdims=True), 1e-12)

        def rotate_half(x):
            x1, x2 = jnp.split(x, 2, -1)
            return jnp.concatenate([-x2, x1], -1)

        def rotary_tables(n):
            half = jnp.arange(0, DIM_HEAD, 2, dtype=jnp.float32)
            inv_freq = 1.0 / 10000.0 ** (half / DIM_HEAD)
            t = jnp.arange(n, dtype=jnp.float32)
            freqs = t[:, None] * inv_freq[None, :]
            freqs = jnp.concatenate([freqs, freqs], -1)
            base_scale = (half + 0.4 * DIM_HEAD) / (1.4 * DIM_HEAD)
            power = (t - n // 2) / (WINDOW // 2)
            scale = base_scale[None, :] ** power[:, None]
            scale = jnp.concatenate([scale, scale], -1)
            return (freqs, scale)

        def local_attention(q, k, v):
            b, h, n, d = q.shape
            w = WINDOW
            nw = n // w
            bq = q.reshape(b, h, nw, w, d)
            bk = k.reshape(b, h, nw, w, d)
            bv = v.reshape(b, h, nw, w, d)

            def look(t):
                p = jnp.pad(t, ((0, 0), (0, 0), (1, 0), (0, 0), (0, 0)))
                return jnp.concatenate([p[:, :, :nw], p[:, :, 1:]], axis=3)
            bk2, bv2 = (look(bk), look(bv))
            seq = jnp.arange(n).reshape(nw, w)
            seq_p = jnp.pad(seq, ((1, 0), (0, 0)), constant_values=-1)
            jt = jnp.concatenate([seq_p[:nw], seq_p[1:]], axis=1)
            it = seq[:, :, None]
            jb = jt[:, None, :]
            mask = (it < jb) | (it > jb + w) | (jb == -1)
            sim = jnp.einsum('bhwie,bhwje->bhwij', bq, bk2) * QK_SCALE
            sim = jnp.where(mask, -jnp.finfo(sim.dtype).max, sim)
            attn = jax.nn.softmax(sim, -1)
            out = jnp.einsum('bhwij,bhwje->bhwie', attn, bv2)
            return out.reshape(b, h, n, d)

        def attn_layer(x, Wqkv, qs, ksc, Wo):
            b, n, _ = x.shape
            qkv = x @ Wqkv
            q, k, v = jnp.split(qkv, 3, -1)
            sh = lambda t: t.reshape(b, n, HEADS, DIM_HEAD).transpose(0, 2, 1, 3)
            q, k, v = (sh(q), sh(k), sh(v))
            q = l2norm(q) * qs
            k = l2norm(k) * ksc
            freqs, scale = rotary_tables(n)
            cos, sin = (jnp.cos(freqs), jnp.sin(freqs))
            q = q * cos * scale + rotate_half(q) * sin * scale
            inv = 1.0 / scale
            k = k * cos * inv + rotate_half(k) * sin * inv
            out = local_attention(q, k, v)
            out = out.transpose(0, 2, 1, 3).reshape(b, n, INNER)
            return out @ Wo

        def ffn_layer(x, g, bln, W1, b1, W2, b2):
            mu = x.mean(-1, keepdims=True)
            var = ((x - mu) ** 2).mean(-1, keepdims=True)
            xn = (x - mu) / jnp.sqrt(var + 1e-05) * g + bln
            hg = xn @ W1 + b1
            a, gate = jnp.split(hg, 2, -1)
            return a * jax.nn.gelu(gate, approximate=False) @ W2 + b2
        for i in range(DEPTH):
            x = attn_layer(shift_tokens(x), Wqkv[i], q_scale[i], k_scale[i], Wo[i]) + x
            x = ffn_layer(shift_tokens(x), ln_g[i], ln_b[i], W1[i], b1[i], W2[i], b2[i]) + x
        return x
    x = L0_attn_hidden_states
    x = x + _L0_attn_ref(_layernorm(x, axis=-1), L0_attn_Wi, L0_attn_Wg, L0_attn_Wo, L0_attn_A_diag, L0_attn_B_param, L0_attn_C_param, L0_attn_D, L0_attn_dt, L0_attn_norm_weight)
    x = x + _L0_ffn_ref(_layernorm(x, axis=-1), L0_ffn_Wg, L0_ffn_bg, L0_ffn_We, L0_ffn_be)
    x = x + _L1_attn_ref(_layernorm(x, axis=-1), L1_attn_W_qkv, L1_attn_b_qkv, L1_attn_W_o, L1_attn_b_o)
    x = x + _L1_ffn_ref(_layernorm(x, axis=-1), L1_ffn_Wqkv, L1_ffn_q_scale, L1_ffn_k_scale, L1_ffn_Wo, L1_ffn_ln_g, L1_ffn_ln_b, L1_ffn_W1, L1_ffn_b1, L1_ffn_W2, L1_ffn_b2)
    return x

_drawn_inputs = setup_inputs


def setup_inputs(seed=0):
    import zlib

    import numpy as np

    out = dict(_drawn_inputs(seed))
    spreads = {'L0_attn_norm_weight': (1.0, 0.2),
     'L0_ffn_bg': (0.0, 0.54),
     'L0_ffn_be': (0.0, 0.8),
     'L1_ffn_q_scale': (1.0, 0.6),
     'L1_ffn_k_scale': (1.0, 0.6),
     'L1_ffn_ln_g': (1.0, 0.6),
     'L1_ffn_ln_b': (0.0, 0.8),
     'L1_ffn_b1': (0.0, 0.8),
     'L1_ffn_b2': (0.0, 0.1)}
    factors = {'L1_attn_W_qkv': 8.0,
     'L1_attn_b_qkv': 8.0,
     'L1_attn_W_o': 8.0,
     'L1_attn_b_o': 3.169,
     'L1_ffn_W1': 3.945,
     'L1_ffn_W2': 3.873}
    for name, (base, spread) in spreads.items():
        noise = np.random.default_rng([zlib.crc32(name.encode()), seed]).standard_normal(out[name].shape)
        drawn = base * np.exp(spread * noise) if base else spread * noise
        out[name] = jnp.asarray(drawn.astype(out[name].dtype))
    for name, factor in factors.items():
        out[name] = (out[name] * factor).astype(out[name].dtype)
    return out
```

```python
import concourse.bass as bass
import concourse.mybir as mybir
from contextlib import ExitStack

fp32, bf16, u32 = mybir.dt.float32, mybir.dt.bfloat16, mybir.dt.uint32
ACT = mybir.ActivationFunctionType
ALU = mybir.AluOpType
AX = mybir.AxisListType

P = 128
T = 2048
TILES = T // P
BT = 512
BLOCKS = T // BT
DEPTH = 6
HEADS, DH = 16, 64
INNER = HEADS * DH
GROUPS = 4
GW = 4 * DH
WINDOW = 32
PREV = WINDOW
QC = 64
KC = QC + PREV
QK_SCALE = 8.0
PRIMED = 1
INNER2 = int(P * 4 * 2 / 3)
EPS = 1e-5
PRODUCTS = ((0, 0), (0, 1), (1, 0), (0, 2), (2, 0), (1, 1))
KPROD = 8 * len(PRODUCTS)

CONSTS = (("ident", P), ("ones32", P), ("ones_mean", P), ("mask", 2 * 4 * KC), ("causal", 2 * P), ("iota8", 8),
          ("base_tab", 4 * (BT + PREV)))

INPUTS = ('L0_attn_hidden_states', 'L0_attn_Wi', 'L0_attn_Wg', 'L0_attn_Wo', 'L0_attn_A_diag', 'L0_attn_B_param',
          'L0_attn_C_param', 'L0_attn_D', 'L0_attn_dt', 'L0_attn_norm_weight', 'L0_ffn_Wg', 'L0_ffn_bg', 'L0_ffn_We',
          'L0_ffn_be', 'L1_attn_W_qkv', 'L1_attn_b_qkv', 'L1_attn_W_o', 'L1_attn_b_o', 'L1_ffn_Wqkv', 'L1_ffn_q_scale',
          'L1_ffn_k_scale', 'L1_ffn_Wo', 'L1_ffn_ln_g', 'L1_ffn_ln_b', 'L1_ffn_W1', 'L1_ffn_b1', 'L1_ffn_W2', 'L1_ffn_b2')


class Record:
    pass


def normalise_and_transpose(nc, r, sem, k, to, to_first):
    with nc.Block() as block:

        @block.vector
        def _(dve):
            for t in range(TILES):
                dve.bn_stats(r.stats[:, t, :], r.x[:, t, :]).then_inc(sem.stats, 1)
            dve.wait_ge(sem.stats, (k + 1) * TILES)
            for t in range(TILES):
                dve.bn_aggr(r.moments[:, t, :], r.stats[:, t, :]).then_inc(sem.aggregated, 1)
            dve.wait_ge(sem.std_ready, k + 1)
            dve.reciprocal(r.rstd[:, :], r.std[:, :]).then_inc(sem.rstd_ready, 1)
            dve.wait_ge(sem.rstd_ready, k + 1)
            for t in range(TILES):
                dve.tensor_scalar(r.x_norm[:, t, :], r.x[:, t, :], r.moments[:, t, 0:1], r.rstd[:, t:t + 1],
                                  ALU.subtract, ALU.mult).then_inc(sem.x_normed, 1)

        @block.scalar
        def _(act):
            act.wait_ge(sem.aggregated, (k + 1) * TILES)
            act.activation(r.std[:, :], r.moments[:, :, 1], ACT.Sqrt, bias=r.eps[:, 0:1]).then_inc(sem.std_ready, 1)
            for q in range(TILES // 4):
                act.wait_ge(sem.x_transposed, k * 4 + q + 1)
                act.copy(to[:, to_first + q * BT:to_first + (q + 1) * BT], r.banks[q][:, :]).then_inc(sem.x_copied, 1)

        @block.tensor
        def _(pe):
            for t in range(TILES):
                pe.wait_ge(sem.x_normed, k * TILES + t + 1)
                mm = pe.transpose(r.banks[t // 4][:, (t % 4) * P:(t % 4 + 1) * P], r.x_norm[:, t, :], r.ident[:, :])
                if t % 4 == 3:
                    mm.then_inc(sem.x_transposed, 1)


def oscillators(nc, r, sem):
    CH, ST = r.CH, r.ST
    hT, xiT, bu, ys2 = r.hT, r.xiT, r.bu, r.y_osc
    banks = r.banks

    with nc.Block() as block:

        @block.sync
        def _(sp):
            for i, (dst, src) in enumerate(((r.wA[:, 0, :], r.d['L0_attn_Wi']), (r.wA[:, 1, :], r.d['L0_attn_Wg']),
                                            (r.wA[:, 2, :], r.d['L0_attn_Wo']),
                                            (r.bc_raw[:, 0, :], r.d['L0_attn_B_param'].rearrange("p h c -> p (h c)")),
                                            (r.bc_raw[:, 1, :], r.d['L0_attn_C_param'].rearrange("p h c -> p (h c)")))):
                sp.dma_start(dst, src).then_inc(sem.wA_loaded, 16)
            for i, name in enumerate(('L0_attn_A_diag', 'L0_attn_dt', 'L0_attn_D', 'L0_attn_norm_weight')):
                sp.dma_start(r.colsA[:, i:i + 1], r.d[name].rearrange("(p o) -> p o", o=1)).then_inc(sem.colsA_loaded, 16)

        @block.gpsimd
        def _(pool):
            pool.wait_ge(sem.coefs_ready, 6)
            k = 0
            for s in range(r.N_POW - 1):
                m = r.powers[:, s, :]
                nxt = r.powers[:, s + 1, :]
                pool.tensor_tensor(r.pw_tmp[:, 0:1], m[:, 2:3], m[:, 3:4], ALU.mult).then_inc(sem.powered, 1)
                pool.tensor_tensor(r.pw_tmp[:, 1:2], m[:, 0:1], m[:, 1:2], ALU.add).then_inc(sem.powered, 1)
                pool.tensor_tensor(r.pw_tmp[:, 2:4], m[:, 0:2], m[:, 0:2], ALU.mult).then_inc(sem.powered, 1)
                k += 3
                pool.wait_ge(sem.powered, k)
                pool.tensor_scalar(nxt[:, 0:2], r.pw_tmp[:, 2:4], r.pw_tmp[:, 0:1], None, ALU.add).then_inc(sem.powered, 1)
                pool.tensor_scalar(nxt[:, 2:4], m[:, 2:4], r.pw_tmp[:, 1:2], None, ALU.mult).then_inc(sem.powered, 1)
                k += 2
                pool.wait_ge(sem.powered, k)

        @block.tensor
        def _(pe):
            pe.wait_ge(sem.wA_loaded, 80)
            for i in range(3):
                mm = pe.transpose(banks[4][:, i * P:(i + 1) * P], r.wA[:, i, :], r.ident[:, :])
            mm.then_inc(sem.wA_turned, 1)
            pe.wait_ge(sem.bc_split, 4)
            for i in range(4):
                mm = pe.transpose(banks[5][:, i * P:(i + 1) * P], r.bc[:, i, :], r.ident[:, :])
            mm.then_inc(sem.wA_turned, 1)
            pe.wait_ge(sem.wA_ready, 4)
            for b in range(BLOCKS):
                pe.matmul(banks[b][:, :], r.wAT[:, 0, :], hT[:, b * BT:(b + 1) * BT], start=True, stop=True
                          ).then_inc(sem.xi_made, 1)
            for c in range(2):
                for b in range(BLOCKS):
                    u = c * BLOCKS + b
                    bank = banks[6 + u % 2]
                    pe.wait_ge(sem.xi_copied, b + 1)
                    if u >= 2:
                        pe.wait_ge(sem.bu_copied, u - 1)
                    pe.matmul(bank[:, :], r.bcT[:, c, :], xiT[:, b * BT:(b + 1) * BT], start=True, stop=True
                              ).then_inc(sem.bu_made, 1)
            pe.wait_ge(sem.diag_ready, 1)
            for t in range(TILES + 2):
                if t < TILES:
                    tok = slice(t * P, (t + 1) * P)
                    if t == 0:
                        pe.wait_ge(sem.osc_kept, ST)
                    if t >= 4:
                        pe.wait_ge(sem.o_gated, t - 3)
                    bank = banks[t % 4]
                    pe.matmul(bank[:, 0:P], ys2[:, 0, tok], r.bcT[:, 2, :], start=True, stop=False)
                    pe.matmul(bank[:, 0:P], ys2[:, 1, tok], r.bcT[:, 3, :], start=False, stop=False)
                    pe.matmul(bank[:, 0:P], xiT[:, tok], r.diag_d[:, :], start=False, stop=True)
                    pe.matmul(bank[:, P:2 * P], hT[:, tok], r.wAT[:, 1, :], start=True, stop=True).then_inc(sem.og_made, 1)
                if 1 <= t <= TILES:
                    u = t - 1
                    pe.wait_ge(sem.o_gated, u + 1)
                    if u >= 2:
                        pe.wait_ge(sem.oT_copied, u - 1)
                    pe.transpose(banks[4 + u % 2][:, 0:P], r.gated[:, u % 2, :], r.ident[:, :]).then_inc(sem.o_turned, 1)
                if t >= 2:
                    u = t - 2
                    pe.wait_ge(sem.oT_copied, u + 1)
                    if u >= 2:
                        pe.wait_ge(sem.aT_added, u - 1)
                    pe.matmul(banks[6 + u % 2][:, 0:P], r.gatedT[:, u % 2, :], r.wAT[:, 2, :], start=True, stop=True
                              ).then_inc(sem.aout_made, 1)

        @block.scalar
        def _(act):
            act.wait_ge(sem.colsA_loaded, 64)
            act.activation(r.colt[:, 0:1], r.colsA[:, 1:2], ACT.Exp, scale=-1.0).then_inc(sem.dt_exp, 1)
            act.wait_ge(sem.wA_turned, 1)
            act.copy(r.wAT[:, 0:2, :].rearrange("p a n -> p (a n)"), banks[4][:, 0:2 * P]).then_inc(sem.wA_ready, 1)
            act.mul(r.wAT[:, 2, :], banks[4][:, 2 * P:3 * P], r.colsA[:, 3:4]).then_inc(sem.wA_ready, 1)
            act.wait_ge(sem.wA_turned, 2)
            act.copy(r.bcT[:, 0:3, :].rearrange("p a n -> p (a n)"), banks[5][:, 0:3 * P]).then_inc(sem.wA_ready, 1)
            act.mul(r.bcT[:, 3, :], banks[5][:, 3 * P:4 * P], -1.0).then_inc(sem.wA_ready, 1)
            for b in range(BLOCKS):
                act.wait_ge(sem.xi_made, b + 1)
                act.copy(xiT[:, b * BT:(b + 1) * BT], banks[b][:, :]).then_inc(sem.xi_copied, 1)
            act.wait_ge(sem.coefs_ready, 6)
            for u in range(2 * BLOCKS):
                act.wait_ge(sem.bu_made, u + 1)
                act.mul(bu[:, u // BLOCKS, (u % BLOCKS) * BT:(u % BLOCKS + 1) * BT], banks[6 + u % 2][:, :],
                        r.coef[:, 3:4]).then_inc(sem.bu_copied, 1)
            for t in range(TILES):
                act.wait_ge(sem.og_made, t + 1)
                act.activation(r.sq_junk[:, :], banks[t % 4][:, 0:P], ACT.Square, accum_out=r.o_ss[:, t:t + 1])
                if t >= 2:
                    act.wait_ge(sem.o_gated, t - 1)
                act.activation(r.sig[:, t % 2, :], banks[t % 4][:, P:2 * P], ACT.Sigmoid).then_inc(sem.sig_ready, 1)
                act.wait_ge(sem.o_turned, t + 1)
                if t >= 2:
                    act.wait_ge(sem.aout_made, t - 1)
                act.copy(r.gatedT[:, t % 2, :], banks[4 + t % 2][:, 0:P]).then_inc(sem.oT_copied, 1)

        @block.vector
        def _(dve):
            co, ca, ct = r.coef, r.colsA, r.colt
            dve.wait_ge(sem.dt_exp, 1)
            k = 0

            def link(ins):
                nonlocal k
                k += 1
                ins.then_inc(sem.colchain, 1)
                dve.wait_ge(sem.colchain, k)

            link(dve.tensor_scalar(ct[:, 1:2], ct[:, 0:1], 1.0, None, ALU.add))
            link(dve.reciprocal(co[:, 2:3], ct[:, 1:2]))
            link(dve.tensor_scalar(ct[:, 2:3], ca[:, 0:1], 0.0, co[:, 2:3], ALU.max, ALU.mult))
            link(dve.tensor_scalar(ct[:, 3:4], ct[:, 2:3], co[:, 2:3], 1.0, ALU.mult, ALU.add))
            link(dve.reciprocal(co[:, 0:1], ct[:, 3:4]))
            dve.tensor_scalar(co[:, 3:4], co[:, 0:1], co[:, 2:3], None, ALU.mult).then_inc(sem.coefs_ready, 1)
            dve.tensor_scalar(co[:, 1:2], ct[:, 2:3], co[:, 0:1], -1.0, ALU.mult, ALU.mult).then_inc(sem.coefs_ready, 1)
            dve.tensor_copy(r.powers[:, 0, 0:1], co[:, 0:1]).then_inc(sem.coefs_ready, 1)
            dve.tensor_copy(r.powers[:, 0, 1:2], co[:, 0:1]).then_inc(sem.coefs_ready, 1)
            dve.tensor_scalar(r.powers[:, 0, 2:3], ct[:, 2:3], co[:, 0:1], -1.0, ALU.mult, ALU.mult).then_inc(sem.coefs_ready, 1)
            dve.tensor_scalar(r.powers[:, 0, 3:4], co[:, 0:1], co[:, 2:3], None, ALU.mult).then_inc(sem.coefs_ready, 1)
            dve.tensor_scalar(r.diag_d[:, :], r.ident[:, :], ca[:, 2:3], None, ALU.mult).then_inc(sem.diag_ready, 1)
            dve.wait_ge(sem.wA_loaded, 80)
            for i in range(4):
                dve.tensor_copy(r.bc[:, i, :], r.bc_raw[:, i // 2, :].rearrange("p (h c) -> p h c", c=2)[:, :, i % 2]
                                ).then_inc(sem.bc_split, 1)

            steps = bu[:, :, :].rearrange("p c (n s) -> p c n s", s=ST)
            outs = ys2[:, :, :].rearrange("p c (n s) -> p c n s", s=ST)
            dve.memset(r.state[:, 0, :, :, :], 0.0).then_inc(sem.state_zeroed, 1)
            dve.wait_ge(sem.state_zeroed, 1)
            dve.wait_ge(sem.bu_copied, 2 * BLOCKS)

            def run(z, y, counter, keep):
                with dve.Fori(0, ST // 4) as j4:
                    for i in range(4):
                        done = j4 * 12 + (3 * i + PRIMED)
                        now = steps[:, :, :, bass.ds(j4 * 4 + i, 1)].rearrange("p c n s -> p c (n s)")
                        y_old = y
                        dve.wait_ge(counter, done)
                        dve.scalar_tensor_tensor(r.drive[:, :, :], y_old, co[:, 1:2], now, ALU.mult, ALU.add).then_inc(counter, 1)
                        dve.wait_ge(counter, done + 1)
                        dve.scalar_tensor_tensor(z, z, co[:, 0:1], r.drive[:, :, :], ALU.mult, ALU.add).then_inc(counter, 1)
                        dve.wait_ge(counter, done + 2)
                        dve.scalar_tensor_tensor(y, z, co[:, 2:3], y_old, ALU.mult, ALU.add).then_inc(counter, 1)
                        if keep:
                            dve.wait_ge(counter, done + 3)
                            dve.tensor_copy(outs[:, :, :, bass.ds(j4 * 4 + i, 1)].rearrange("p c n s -> p c (n s)"), y
                                            ).then_inc(sem.osc_kept, 1)

            run(r.state[:, 0, 0, :, :], r.state[:, 0, 1, :, :], sem.osc1, False)
            dve.wait_ge(sem.osc1, 3 * ST + PRIMED)
            dve.wait_ge(sem.powered, 5 * (r.N_POW - 1))
            k2 = 0
            cur = 0
            for s in range(r.LOG_CH):
                d = 1 << s
                g = r.powers[:, r.LOG_ST + s, :]
                src, dst = r.state[:, cur], r.state[:, 1 - cur]
                zs, ysrc = src[:, 0, :, 0:CH - d], src[:, 1, :, 0:CH - d]
                dve.tensor_copy(dst[:, :, :, 0:d], src[:, :, :, 0:d]).then_inc(sem.doubled, 1)
                dve.scalar_tensor_tensor(dst[:, 0, :, d:CH], zs, g[:, 0:1], src[:, 0, :, d:CH], ALU.mult, ALU.add).then_inc(sem.doubled, 1)
                dve.scalar_tensor_tensor(dst[:, 1, :, d:CH], zs, g[:, 3:4], src[:, 1, :, d:CH], ALU.mult, ALU.add).then_inc(sem.doubled, 1)
                k2 += 3
                dve.wait_ge(sem.doubled, k2)
                dve.scalar_tensor_tensor(dst[:, 0, :, d:CH], ysrc, g[:, 2:3], dst[:, 0, :, d:CH], ALU.mult, ALU.add).then_inc(sem.doubled, 1)
                dve.scalar_tensor_tensor(dst[:, 1, :, d:CH], ysrc, g[:, 1:2], dst[:, 1, :, d:CH], ALU.mult, ALU.add).then_inc(sem.doubled, 1)
                k2 += 2
                dve.wait_ge(sem.doubled, k2)
                cur = 1 - cur
            src, dst = r.state[:, cur], r.state[:, 1 - cur]
            dve.memset(dst[:, :, :, 0:1], 0.0).then_inc(sem.doubled, 1)
            dve.tensor_copy(dst[:, 0, :, 1:CH], src[:, 0, :, 0:CH - 1]).then_inc(sem.doubled, 1)
            dve.tensor_copy(dst[:, 1, :, 1:CH], src[:, 1, :, 0:CH - 1]).then_inc(sem.doubled, 1)
            dve.wait_ge(sem.doubled, k2 + 3)
            run(dst[:, 0], dst[:, 1], sem.osc2, True)

            for t in range(TILES + 2):
                if t < TILES:
                    dve.wait_ge(sem.sig_ready, t + 1)
                    if t >= 2:
                        dve.wait_ge(sem.o_turned, t - 1)
                    dve.tensor_tensor(r.silu[:, :], banks[t % 4][:, P:2 * P], r.sig[:, t % 2, :], ALU.mult).then_inc(sem.silu_ready, 1)
                    dve.wait_ge(sem.silu_ready, t + 1)
                    dve.tensor_tensor(r.gated[:, t % 2, :], banks[t % 4][:, 0:P], r.silu[:, :], ALU.mult).then_inc(sem.o_gated, 1)
                if t >= 2:
                    u = t - 2
                    dve.wait_ge(sem.aout_made, u + 1)
                    dve.tensor_copy(r.a_out[:, u, :], banks[6 + u % 2][:, 0:P]).then_inc(sem.aT_added, 1)

    with nc.Block() as block:
        @block.scalar
        def _(act):
            act.activation(r.std[:, :], r.o_ss[:, :], ACT.Sqrt, bias=r.eps[:, 0:1], scale=1.0 / P).then_inc(sem.o_std, 1)

        @block.vector
        def _(dve):
            dve.wait_ge(sem.o_std, 1)
            dve.reciprocal(r.rstd[:, :], r.std[:, :]).then_inc(sem.o_rstd, 1)
            dve.wait_ge(sem.o_rstd, 1)
            for t in range(TILES):
                dve.scalar_tensor_tensor(r.x[:, t, :], r.a_out[:, t, :], r.rstd[:, t:t + 1], r.x[:, t, :], ALU.mult, ALU.add)


def experts(nc, r, sem):
    hT, banks = r.hT, r.banks
    with nc.Block() as block:

        @block.sync
        def _(sp):
            sp.dma_start(r.wgate[:, :], r.d['L0_ffn_Wg']).then_inc(sem.wB_loaded, 16)
            sp.dma_start(r.wexp[:, :, :], r.d['L0_ffn_We'].rearrange("e d f -> d e f")).then_inc(sem.wB_loaded, 16)
            sp.dma_start(r.row_bg[0:1, :], r.d['L0_ffn_bg'].rearrange("(o n) -> o n", o=1)).then_inc(sem.wB_loaded, 16)
            sp.dma_start(r.row_be[0:1, :], r.d['L0_ffn_be'].rearrange("(o e) f -> o (e f)", o=1)).then_inc(sem.wB_loaded, 16)

        @block.tensor
        def _(pe):
            pe.wait_ge(sem.wB_loaded, 64)
            for t in range(TILES):
                tok = slice(t * P, (t + 1) * P)
                if t >= 2:
                    pe.wait_ge(sem.router_exp, t - 1)
                bank = banks[t % 2]
                pe.matmul(bank[:, 0:P], hT[:, tok], r.wgate[:, :], start=True, stop=False)
                pe.matmul(bank[:, 0:P], r.ones_row[0:1, :], r.row_bg[0:1, :], start=False, stop=True).then_inc(sem.routed, 1)
                if t >= 2:
                    pe.wait_ge(sem.experts_scaled, t - 1)
                for h in range(2):
                    bank = banks[2 + 2 * (t % 2) + h]
                    pe.matmul(bank[:, :], hT[:, tok], r.wexp[:, 4 * h:4 * h + 4, :].rearrange("p e f -> p (e f)"), start=True, stop=False)
                    mm = pe.matmul(bank[:, :], r.ones_row[0:1, :], r.row_be[0:1, h * BT:(h + 1) * BT], start=False, stop=True)
                mm.then_inc(sem.experts_made, 1)

        @block.vector
        def _(dve):
            for t in range(TILES + 1):
                if t < TILES:
                    p = t % 2
                    dve.wait_ge(sem.routed, t + 1)
                    dve.max(r.top8[:, p, :], banks[p][:, 0:P]).then_inc(sem.top_found, 1)
                    dve.wait_ge(sem.top_found, t + 1)
                    if t >= 2:
                        dve.wait_ge(sem.router_exp, t - 1)
                    dve.tensor_scalar(r.top_neg[:, p, :], r.top8[:, p, 0:1], -1.0, None, ALU.mult).then_inc(sem.top_neg, 1)
                    dve.max_index(r.top_at[:, p, :], r.top8[:, p, :], banks[p][:, 0:P]).then_inc(sem.index_found, 1)
                    dve.wait_ge(sem.index_found, t + 1)
                    dve.tensor_scalar(r.expert_u[:, p, :], r.top_at[:, p, 0:1], r.N_EXP - 1, None, ALU.bitwise_and).then_inc(sem.expert_found, 1)
                    dve.wait_ge(sem.expert_found, t + 1)
                    dve.tensor_copy(r.expert_f[:, p, :], r.expert_u[:, p, :]).then_inc(sem.expert_cast, 1)
                    dve.wait_ge(sem.router_exp, t + 1)
                    dve.reciprocal(r.top_p[:, p, :], r.router_sum[:, p, :]).then_inc(sem.prob_ready, 1)
                    dve.wait_ge(sem.expert_cast, t + 1)
                    dve.wait_ge(sem.prob_ready, t + 1)
                    if t >= 2:
                        dve.wait_ge(sem.experts_scaled, t - 1)
                    dve.tensor_scalar(r.select[:, p, :], r.iota8[:, :], r.expert_f[:, p, :], r.top_p[:, p, :], ALU.is_equal, ALU.mult
                                      ).then_inc(sem.selected, 1)
                if t >= 1:
                    u = t - 1
                    dve.wait_ge(sem.experts_scaled, u + 1)
                    dve.tensor_reduce(r.moe[:, u % 2, :], r.scaled_exp[:, u % 2, :, :].rearrange("p e f -> p f e"), AX.X, ALU.add
                                      ).then_inc(sem.experts_summed, 1)
                    dve.wait_ge(sem.experts_summed, u + 1)
                    dve.tensor_tensor(r.x[:, u, :], r.x[:, u, :], r.moe[:, u % 2, :], ALU.add).then_inc(sem.moe_added, 1)

        @block.scalar
        def _(act):
            for t in range(TILES):
                p = t % 2
                act.wait_ge(sem.index_found, t + 1)
                act.wait_ge(sem.top_neg, t + 1)
                if t >= 2:
                    act.wait_ge(sem.prob_ready, t - 1)
                act.activation(r.junk[:, :], banks[p][:, 0:P], ACT.Exp, bias=r.top_neg[:, p, :], accum_out=r.router_sum[:, p, :]
                               ).then_inc(sem.router_exp, 1)
                act.wait_ge(sem.selected, t + 1)
                act.wait_ge(sem.experts_made, t + 1)
                if t >= 2:
                    act.wait_ge(sem.experts_summed, t - 1)
                for e in range(r.N_EXP):
                    a = act.activation(r.scaled_exp[:, p, e, :], banks[2 + 2 * p + e // 4][:, (e % 4) * P:(e % 4 + 1) * P], ACT.Relu,
                                       scale=r.select[:, p, e:e + 1])
                a.then_inc(sem.experts_scaled, 1)


def causal_projections(nc, r, sem):
    hT, banks = r.hT, r.banks
    with nc.Block() as block:

        @block.sync
        def _(sp):
            sp.dma_start(r.wqkvC[:, :], r.d['L1_attn_W_qkv']).then_inc(sem.wC_loaded, 16)
            sp.dma_start(r.woC[:, :], r.d['L1_attn_W_o']).then_inc(sem.wC_loaded, 16)
            for i in range(2):
                sp.dma_start(r.cols_bqk[:, i:i + 1], r.d['L1_attn_b_qkv'][i * P:(i + 1) * P].rearrange("(p o) -> p o", o=1)).then_inc(sem.wC_loaded, 16)
            sp.dma_start(r.row_bv[0:1, :], r.d['L1_attn_b_qkv'][2 * P:3 * P].rearrange("(o n) -> o n", o=1)).then_inc(sem.wC_loaded, 16)
            sp.dma_start(r.row_bo[0:1, :], r.d['L1_attn_b_o'].rearrange("(o n) -> o n", o=1)).then_inc(sem.wC_loaded, 16)
            for s in range(2):
                sp.wait_ge(sem.parts_ready, 5 * s + 5)
                for i, pair in enumerate(PRODUCTS):
                    sp.dma_start(r.d_stack[s, :, i],
                                 r.parts[:, s, pair[s], :]).then_inc(sem.stacked, 16)
            sp.wait_ge(sem.stacked, 2 * len(PRODUCTS) * 16)

        @block.tensor
        def _(pe):
            pe.wait_ge(sem.wC_loaded, 96)
            for s in range(2):
                for b in range(BLOCKS):
                    pe.matmul(banks[4 * s + b][:, :], r.wqkvC[:, s * P:(s + 1) * P], hT[:, b * BT:(b + 1) * BT], start=True, stop=True
                              ).then_inc(sem.qkC_made, 1)
            for t in range(TILES):
                if t % 4 == 0:
                    pe.wait_ge(sem.qkC_read, t // 4 + 1)
                bank = banks[t // 4]
                pe.matmul(bank[:, (t % 4) * P:(t % 4 + 1) * P], hT[:, t * P:(t + 1) * P], r.wqkvC[:, 2 * P:3 * P], start=True, stop=False)
                mm = pe.matmul(bank[:, (t % 4) * P:(t % 4 + 1) * P], r.ones_row[0:1, :], r.row_bv[0:1, :], start=False, stop=True)
                if t % 4 == 3:
                    mm.then_inc(sem.vC_made, 1)

        @block.vector
        def _(dve):
            dve.wait_ge(sem.wC_loaded, 96)
            for s in range(2):
                for b in range(BLOCKS):
                    dve.wait_ge(sem.qkC_made, s * BLOCKS + b + 1)
                    dve.tensor_scalar(r.qkf[:, s, b * BT:(b + 1) * BT], banks[4 * s + b][:, :], r.cols_bqk[:, s:s + 1],
                                      8 ** -0.5 if s == 0 else 1.0, ALU.add, ALU.mult).then_inc(sem.qkC_read, 1)
                dve.wait_ge(sem.qkC_read, BLOCKS * (s + 1))
                full, rest = r.qkf[:, s, :], r.rest[:, :]
                hi, mid, lo = (r.parts[:, s, i, :] for i in range(3))
                k = 5 * s
                dve.tensor_copy(hi, full).then_inc(sem.parts_ready, 1)
                dve.wait_ge(sem.parts_ready, k + 1)
                dve.tensor_tensor(rest, full, hi, ALU.subtract).then_inc(sem.parts_ready, 1)
                dve.wait_ge(sem.parts_ready, k + 2)
                dve.tensor_copy(mid, rest).then_inc(sem.parts_ready, 1)
                dve.wait_ge(sem.parts_ready, k + 3)
                dve.tensor_tensor(lo, rest, mid, ALU.subtract).then_inc(sem.parts_ready, 2)
                dve.wait_ge(sem.parts_ready, k + 5)

        @block.scalar
        def _(act):
            act.wait_ge(sem.v_cleared, 2)
            for q in range(4):
                act.wait_ge(sem.vC_made, q + 1)
                for j in range(4):
                    act.copy(r.v_aug[:, 4 * q + j, :, 0:8], banks[q][:, j * P:(j + 1) * P].rearrange("p (h d) -> p h d", d=8)
                             ).then_inc(sem.vC_copied, 1)

        @block.gpsimd
        def _(pool):
            pool.memset(r.v_aug[:, :, :, :], 0.0).then_inc(sem.v_cleared, 1)
            pool.wait_ge(sem.v_cleared, 1)
            pool.memset(r.v_aug[:, :, :, 8:9], 1.0).then_inc(sem.v_cleared, 1)
            pool.memset(r.part_max[:, :, :, :], -3e38).then_inc(sem.v_cleared, 1)
            pool.memset(r.ones3[:, :], 1.0).then_inc(sem.ones3_set, 1)
            pool.wait_ge(sem.ones3_set, 1)
            pool.dma_start(r.k_next[KPROD:KPROD + 3, :, :].rearrange("p a t -> p (a t)"), r.ones3[:, :]).then_inc(sem.ones_placed, 16)
            pool.wait_ge(sem.ones_placed, 16)


def causal_attention(nc, r, sem):
    banks = r.banks
    maxb = (banks[5], banks[6])
    misc, acc = banks[7], banks[4]
    NH = 4
    MAXES = [(a, qt, kb) for qt in range(TILES) for a in range(NH) for kb in range(qt // 4 + 1)]
    STEPS = [(b, kt, pair) for b in range(BLOCKS) for kt in range(4 * b + 4) for pair in range(2)]
    NM, NSTEP = len(MAXES), len(STEPS)
    PER_STEP = -(-NM // NSTEP)

    def at(n, per_group, k):
        return n * per_group + (k + PRIMED)

    def first_query(b, kt):
        return max(0, kt - 4 * b) * P

    with nc.Block() as block:

        @block.sync
        def _(sp):
            def load(m):
                heads = bass.ds(m * NH, NH)
                for s, to in ((0, r.q_next), (1, r.k_next)):
                    sp.dma_start(to[0:KPROD, :, :], r.d_stack[s, heads].rearrange("h i d t -> (i d) h t")).then_inc(sem.stack_loaded, 16)

            def place_maxima(m):
                sp.wait_ge(sem.max_split, at(m, 4, 4))
                for i in range(3):
                    sp.dma_start(r.q_next[KPROD + i:KPROD + i + 1, :, :].rearrange("p a (q t) -> p (a q) t", t=P),
                                 r.max_parts[:, i, :]).then_inc(sem.max_placed, 16)

            load(0)
            place_maxima(0)
            with sp.Fori(0, GROUPS - 1) as n:
                sp.wait_ge(sem.taken, at(n, 2, 2))
                load(n + 1)
                place_maxima(n + 1)

        @block.tensor
        def _(pe):
            def maxima(m, i):
                a, qt, kb = MAXES[i]
                keys = min(BT, (qt + 1) * P - kb * BT)
                bank = maxb[i % 2]
                if i < 2:
                    pe.wait_ge(sem.part_max_done, at(m, NM, 0))
                else:
                    pe.wait_ge(sem.part_max_done, at(m, NM, i - 1))
                diag = kb == qt // 4
                mm = pe.matmul(bank[:, 0:keys], r.q_next[0:KPROD, a, qt * P:(qt + 1) * P], r.k_next[0:KPROD, a, kb * BT:kb * BT + keys],
                               start=True, stop=not diag, skip_group_check=True)
                if diag:
                    mm = pe.matmul(bank[:, keys - P:keys], r.ident_bf[:, :], r.causal_bf[:, 0, :], start=False, stop=True, skip_group_check=True)
                mm.then_inc(sem.max_scored, 1)

            def turn_maxima(m):
                pe.wait_ge(sem.max_ready_c, at(m, 1, 1))
                pe.wait_ge(sem.outputs_taken, at(m, BLOCKS, 0))
                pe.wait_ge(sem.max_split, at(m, 4, 0))
                pe.transpose(misc[:, 0:P], r.neg_max_c[:, :], r.ident[:, :]).then_inc(sem.max_turned, 1)

            def weights(n, i):
                b, kt, pair = STEPS[i]
                q0 = first_query(b, kt)
                if i < 2:
                    pe.wait_ge(sem.exp_done, at(n, NSTEP, 0))
                else:
                    pe.wait_ge(sem.exp_done, at(n, NSTEP, i - 1))
                for h in range(2):
                    a = 2 * pair + h
                    bank = banks[2 * (i % 2) + h]
                    diag = kt >= 4 * b
                    mm = pe.matmul(bank[:, q0:BT], r.k_now[0:KPROD + 3, a, kt * P:(kt + 1) * P], r.q_now[0:KPROD + 3, a, b * BT + q0:(b + 1) * BT],
                                   start=True, stop=not diag, skip_group_check=True)
                    if diag:
                        mm = pe.matmul(bank[:, q0:q0 + P], r.ident_bf[:, :], r.causal_bf[:, 1, :], start=False, stop=True, skip_group_check=True)
                mm.then_inc(sem.weights_scored, 1)

            def values(n, i):
                b, kt, pair = STEPS[i]
                q0 = first_query(b, kt)
                pe.wait_ge(sem.exp_done, at(n, NSTEP, i + 1))
                if kt == 0 and pair == 0:
                    pe.wait_ge(sem.acc_copied, at(n, BLOCKS, b))
                for h in range(2):
                    a = 2 * pair + h
                    mm = pe.matmul(acc[32 * a:32 * a + 32, q0:BT], r.v_now[:, kt, a, :], r.weights[:, i % 2, h, q0:BT],
                                   start=kt == 0, stop=kt == 4 * b + 3, skip_group_check=True)
                mm.then_inc(sem.valued, 1)

            def turn_outputs(n, b):
                pe.wait_ge(sem.acc_copied, at(n, BLOCKS, b + 1))
                pe.wait_ge(sem.outputs_taken, at(n, BLOCKS, b))
                for j in range(4):
                    mm = pe.transpose(misc[:, j * P:(j + 1) * P], r.acc_sb[:, j * P:(j + 1) * P], r.ident[:, :])
                mm.then_inc(sem.outputs_turned, 1)

            pe.wait_ge(sem.stack_loaded, 32 + PRIMED)
            for i in range(NM):
                maxima(0, i)
            turn_maxima(0)

            def body(n, more):
                pe.wait_ge(sem.taken, at(n, 2, 2))
                pe.wait_ge(sem.v_taken, at(n, 1, 1))
                mi = 0
                if more:
                    pe.wait_ge(sem.stack_loaded, at(n, 32, 64))
                for i in range(NSTEP + 1):
                    if i < NSTEP:
                        weights(n, i)
                    if more:
                        while mi < min(NM, PER_STEP * (i + 1)):
                            maxima(n + 1, mi)
                            mi += 1
                    if i >= 1:
                        values(n, i - 1)
                        b, kt, pair = STEPS[i - 1]
                        if b >= 1 and kt == 0 and pair == 1:
                            turn_outputs(n, b - 1)
                turn_outputs(n, BLOCKS - 1)
                if more:
                    turn_maxima(n + 1)

            with pe.Fori(0, GROUPS - 1) as n:
                body(n, True)
            body(GROUPS - 1, False)

        @block.scalar
        def _(act):
            def body(n):
                for i, (b, kt, pair) in enumerate(STEPS):
                    q0 = first_query(b, kt)
                    act.wait_ge(sem.weights_scored, at(n, NSTEP, i + 1))
                    if i >= 2:
                        act.wait_ge(sem.valued, at(n, NSTEP, i - 1))
                    else:
                        act.wait_ge(sem.valued, at(n, NSTEP, 0))
                    act.activation(r.weights[:, i % 2, :, q0:BT], r.pairs[i % 2][:, :, q0:BT], ACT.Exp).then_inc(sem.exp_done, 1)
            with act.Fori(0, GROUPS) as n:
                body(n)

        @block.vector
        def _(dve):
            def part_maxima(m, i):
                a, qt, kb = MAXES[i]
                keys = min(BT, (qt + 1) * P - kb * BT)
                dve.wait_ge(sem.max_scored, at(m, NM, i + 1))
                dve.tensor_reduce(r.part_max[:, a, qt, kb:kb + 1], maxb[i % 2][:, 0:keys], AX.X, ALU.max).then_inc(sem.part_max_done, 1)

            def finish_maxima(m):
                dve.wait_ge(sem.part_max_done, at(m, NM, NM))
                dve.tensor_reduce(r.max_c[:, :], r.part_max[:, :, :, :].rearrange("p a q k -> p (a q) k"), AX.X, ALU.max
                                  ).then_inc(sem.max_reduced, 1)
                dve.wait_ge(sem.max_reduced, at(m, 1, 1))
                dve.tensor_scalar(r.neg_max_c[:, 0:NH * TILES], r.max_c[:, :], -1.0, None, ALU.mult).then_inc(sem.max_ready_c, 1)
                dve.wait_ge(sem.max_turned, at(m, 1, 1))
                dve.wait_ge(sem.max_placed, at(m, 48, 0))
                full, rest = r.max_rows[:, 0, :], r.max_rows[:, 1, :]
                dve.tensor_copy(full, misc[0:NH * TILES, 0:P]).then_inc(sem.max_split, 1)
                dve.wait_ge(sem.max_split, at(m, 4, 1))
                dve.tensor_copy(r.max_parts[:, 0, :], full).then_inc(sem.max_cut, 1)
                dve.wait_ge(sem.max_cut, at(m, 2, 1))
                dve.tensor_tensor(rest, full, r.max_parts[:, 0, :], ALU.subtract).then_inc(sem.max_split, 1)
                dve.wait_ge(sem.max_split, at(m, 4, 2))
                dve.tensor_copy(r.max_parts[:, 1, :], rest).then_inc(sem.max_cut, 1)
                dve.wait_ge(sem.max_cut, at(m, 2, 2))
                dve.tensor_tensor(r.max_parts[:, 2, :], rest, r.max_parts[:, 1, :], ALU.subtract).then_inc(sem.max_split, 2)

            def take(n):
                dve.wait_ge(sem.max_placed, at(n, 48, 48))
                dve.wait_ge(sem.valued, at(n, NSTEP, 0))
                dve.tensor_copy(r.q_now[0:KPROD + 3, :, :], r.q_next[0:KPROD + 3, :, :]).then_inc(sem.taken, 1)
                dve.tensor_copy(r.k_now[0:KPROD + 3, :, :], r.k_next[0:KPROD + 3, :, :]).then_inc(sem.taken, 1)
                dve.tensor_copy(r.v_now[:, :, :, :], r.v_aug[:, :, bass.ds(n * NH, NH), :]).then_inc(sem.v_taken, 1)

            def copy_sums(n, b):
                dve.wait_ge(sem.valued, at(n, NSTEP, 4 * (b + 1) * (b + 2)))
                dve.wait_ge(sem.outputs_turned, at(n, BLOCKS, b))
                dve.tensor_copy(r.acc_sb[:, :], acc[:, :]).then_inc(sem.acc_copied, 1)

            def take_outputs(n, b):
                dve.wait_ge(sem.outputs_turned, at(n, BLOCKS, b + 1))
                v = misc[:, :].rearrange("p (j a c) -> p j a c", j=4, a=NH)
                dve.reciprocal(r.inv_den[:, :, :], v[:, :, :, 8]).then_inc(sem.den_inverted, 1)
                dve.wait_ge(sem.den_inverted, at(n, BLOCKS, b + 1))
                for j in range(4):
                    o = dve.tensor_tensor(r.attn_tok[:, 4 * b + j, bass.ds(n * 4 * 8, 32)].rearrange("p (a d) -> p a d", d=8),
                                          v[:, j, :, 0:8], r.inv_den[:, j, :].unsqueeze(2).to_broadcast([P, NH, 8]), ALU.mult)
                o.then_inc(sem.outputs_taken, 1)

            dve.wait_ge(sem.v_cleared, 3)
            dve.memset(r.neg_max_c[:, NH * TILES:P], 0.0)
            for i in range(NM):
                part_maxima(0, i)
            finish_maxima(0)

            def body(n, more):
                take(n)
                mi = 0
                for i in range(NSTEP + 1):
                    if more:
                        while mi < min(NM, PER_STEP * (i + 1)):
                            part_maxima(n + 1, mi)
                            mi += 1
                    if i >= 1:
                        b, kt, pair = STEPS[i - 1]
                        if kt == 4 * b + 3 and pair == 1:
                            copy_sums(n, b)
                        if b >= 1 and kt == 1 and pair == 0:
                            take_outputs(n, b - 1)
                take_outputs(n, BLOCKS - 1)
                if more:
                    finish_maxima(n + 1)

            with dve.Fori(0, GROUPS - 1) as n:
                body(n, True)
            body(GROUPS - 1, False)


def causal_output(nc, r, sem):
    banks = r.banks
    with nc.Block() as block:

        @block.tensor
        def _(pe):
            for t in range(TILES + 1):
                if t < TILES:
                    if t >= 2:
                        pe.wait_ge(sem.aC_copied, t - 1)
                    pe.transpose(banks[t % 2][:, 0:P], r.attn_tok[:, t, :], r.ident[:, :]).then_inc(sem.aC_turned, 1)
                if t >= 1:
                    u = t - 1
                    pe.wait_ge(sem.aC_copied, u + 1)
                    if u >= 2:
                        pe.wait_ge(sem.c_added, u - 1)
                    pe.matmul(banks[2 + u % 2][:, 0:P], r.aC_T[:, u % 2, :], r.woC[:, :], start=True, stop=False)
                    pe.matmul(banks[2 + u % 2][:, 0:P], r.ones_row[0:1, :], r.row_bo[0:1, :], start=False, stop=True).then_inc(sem.c_out, 1)

        @block.scalar
        def _(act):
            for t in range(TILES):
                act.wait_ge(sem.aC_turned, t + 1)
                if t >= 2:
                    act.wait_ge(sem.c_out, t - 1)
                act.copy(r.aC_T[:, t % 2, :], banks[t % 2][:, 0:P]).then_inc(sem.aC_copied, 1)

        @block.vector
        def _(dve):
            for t in range(TILES):
                dve.wait_ge(sem.c_out, t + 1)
                dve.tensor_tensor(r.x[:, t, :], r.x[:, t, :], banks[2 + t % 2][:, 0:P], ALU.add).then_inc(sem.c_added, 1)
def windowed_attention(nc, L, r, sem):
    ys, raw_q, raw_k, squares = r.ys, r.raw_q, r.raw_k, r.squares
    work, scores, pt_ps, out_ps = r.work_ps, r.scores_ps, r.pt_ps, r.out_ps

    def at(n, per_block, b, k):
        return n * (BLOCKS * per_block) + (b * per_block + k + PRIMED)

    with nc.Block() as block:

        @block.sync
        def _(sp):
            lay = bass.ds(L, 1)
            sp.dma_start(r.wo[:, :, :], r.d_wo[lay].rearrange("l (c p) n -> p (l c) n", p=P)).then_inc(sem.ffn_loaded, 16)
            sp.dma_start(r.w1[:, :], r.d_w1[lay].rearrange("l p n -> p (l n)")).then_inc(sem.ffn_loaded, 16)
            sp.dma_start(r.w2[:, 0:2, :], r.d_w2[lay, 0:2 * P].rearrange("l (c p) n -> p (l c) n", p=P)).then_inc(sem.ffn_loaded, 16)
            sp.dma_start(r.w2[0:INNER2 - 2 * P, 2, :], r.d_w2[lay, 2 * P:INNER2].rearrange("l p n -> p (l n)")).then_inc(sem.ffn_loaded, 16)
            with sp.Fori(0, GROUPS) as g:
                n = L * GROUPS + g
                sp.wait_ge(sem.weights_copied, n * 3 + PRIMED)
                for s in range(3):
                    sp.dma_start(r.w_stage[:, s, :],
                                 r.d_wqkv[lay, :, bass.ds(g * GW + s * INNER, GW)].rearrange("l p n -> p (l n)")
                                 ).then_inc(sem.weights_loaded, 16)

        @block.tensor
        def _(pe):
            with pe.Fori(0, GROUPS) as g:
                n = L * GROUPS + g

                def work_use(b, u):
                    if b == 0 and u < 2:
                        pe.wait_ge(sem.work_read, at(n, 10, 0, 0))
                    else:
                        pe.wait_ge(sem.work_read, at(n, 10, b, u - 1))
                    return work[u % 2]

                def project(b):
                    tokens = slice(PREV + b * BT, PREV + (b + 1) * BT)
                    if b == 0:
                        pe.wait_ge(sem.weights_copied, n * 3 + (3 + PRIMED))
                    for u in range(4):
                        pe.matmul(work_use(b, u)[:, :], r.w_qk[:, u, :], ys[:, tokens],
                                  start=True, stop=True).then_inc(sem.work_written, 1)
                    for v in range(4):
                        bank = work_use(b, 4 + v)
                        for half in range(2):
                            c = 2 * v + half
                            first = b * BT + c * QC
                            mm = pe.matmul(bank[0:KC, half * GW:(half + 1) * GW], ys[:, first:first + KC], r.w_v[:, :],
                                           start=True, stop=True)
                        mm.then_inc(sem.work_written, 1)

                def norms(b):
                    for s in range(2):
                        bank = work_use(b, 8 + s)
                        pe.wait_ge(sem.squared, at(n, 4, b, 2 * s + 2))
                        pe.matmul(bank[:, :], r.ones32[:, :], squares[:, 2 * s, :], start=True, stop=False)
                        pe.matmul(bank[:, :], r.ones32[:, :], squares[:, 2 * s + 1, :],
                                  start=False, stop=True).then_inc(sem.work_written, 1)

                def score(b):
                    pe.wait_ge(sem.rotated, at(n, 4, b, 4))
                    for a in range(4):
                        rows = slice(32 * a, 32 * a + 32)
                        bank = scores[a]
                        pe.matmul(bank[:, 0:4 * KC], r.ident_bf[:, :], r.mask_bf[:, 0 if b == 0 else 1, :],
                                  start=True, stop=False, skip_group_check=True)
                        for c in range(8):
                            for half in range(2):
                                mm = pe.matmul(bank[64 * (c % 2):64 * (c % 2) + 64, (c // 2) * KC:(c // 2 + 1) * KC],
                                               r.rot_q[rows, half, c * QC:(c + 1) * QC],
                                               r.rot_k[rows, half, c * QC:c * QC + KC],
                                               start=False, stop=half == 1, skip_group_check=True)
                        mm.then_inc(sem.scored, 1)

                def turn(b, a):
                    pe.wait_ge(sem.normalised, at(n, 4, b, a + 1))
                    if b or a:
                        pe.wait_ge(sem.turned_copied, at(n, 4, b, a))
                    else:
                        pe.wait_ge(sem.turned_copied, at(n, 4, 0, 0))
                    for j in range(4):
                        mm = pe.transpose(pt_ps[0:KC, j * P:(j + 1) * P], r.probs[:, a, j * KC:(j + 1) * KC], r.ident[:, :])
                    mm.then_inc(sem.turned, 1)

                def attend(b, a):
                    pe.wait_ge(sem.turned_copied, at(n, 4, b, a + 1))
                    if a % 2 == 0:
                        pe.wait_ge(sem.out_copied, at(n, 2, b, a // 2))
                    for c in range(8):
                        mm = pe.matmul(out_ps[64 * (a % 2):64 * (a % 2) + 64, c * QC:(c + 1) * QC],
                                       r.v_win[0:KC, b % 2, c, a * DH:(a + 1) * DH],
                                       r.turned_sb[0:KC, a % 2, c * QC:(c + 1) * QC],
                                       start=True, stop=True)
                    mm.then_inc(sem.attended, 1)

                project(0)
                norms(0)
                for b in range(BLOCKS):
                    score(b)
                    if b + 1 < BLOCKS:
                        project(b + 1)
                        norms(b + 1)
                    turn(b, 0)
                    for a in range(1, 4):
                        turn(b, a)
                        attend(b, a - 1)
                    attend(b, 3)

        @block.scalar
        def _(act):
            with act.Fori(0, GROUPS) as g:
                n = L * GROUPS + g

                def copy_raw(b, u):
                    if u == 0:
                        act.wait_ge(sem.multiplied, at(n, 8, b, 0))
                        act.wait_ge(sem.tail_copied, at(n, 2, b, 0))
                    act.wait_ge(sem.work_written, at(n, 10, b, u + 1))
                    to = raw_q[:, u, :] if u < 2 else raw_k[:, u - 2, PREV:]
                    act.copy(to, work[u % 2][:, :]).then_inc(sem.work_read, 1)

                def square(b, u):
                    act.wait_ge(sem.work_read, at(n, 10, b, u + 1))
                    src = raw_q[:, u, :] if u < 2 else raw_k[:, u - 2, PREV:]
                    act.activation(squares[:, u, :], src, ACT.Square).then_inc(sem.squared, 1)

                def copy_v(b, v):
                    act.wait_ge(sem.work_written, at(n, 10, b, 5 + v))
                    act.copy(r.v_win[0:KC, b % 2, 2 * v:2 * v + 2, :].rearrange("p c n -> p (c n)"),
                             work[v % 2][0:KC, :]).then_inc(sem.work_read, 1)

                def inverse_norms(b):
                    act.wait_ge(sem.rotated, at(n, 4, b, 0))
                    act.wait_ge(sem.tail_copied, at(n, 2, b, 0))
                    to = (r.inv_q[:, :], r.inv_k[:, PREV:])
                    for s in range(2):
                        act.wait_ge(sem.work_written, at(n, 10, b, 9 + s))
                        act.activation(to[s], work[s][:, :], ACT.Ln, bias=r.tiny[:, 0:1],
                                       scale=float(2 ** 20)).then_inc(sem.work_read, 1)
                    for s in range(2):
                        act.wait_ge(sem.work_read, at(n, 10, b, 9 + s))
                        act.activation(to[s], to[s], ACT.Exp, bias=r.half_shift[:, 0:1], scale=-0.5
                                       ).then_inc(sem.inverted_norms, 1)

                def exponentials(b, a):
                    act.wait_ge(sem.neg_max_ready, at(n, 4, b, a + 1))
                    for j in range(4):
                        e = act.activation(r.probs[:, a, j * KC:(j + 1) * KC], scores[a][:, j * KC:(j + 1) * KC], ACT.Exp,
                                           bias=r.neg_max[:, a, j:j + 1], scale=QK_SCALE,
                                           accum_out=r.sums[:, a, j:j + 1])
                    e.then_inc(sem.exponentiated, 1)

                def copy_out(b, pair):
                    act.wait_ge(sem.attended, at(n, 4, b, 2 * pair + 2))
                    act.copy(r.attn[:, bass.ds(g * 2 + pair, 1), b * BT:(b + 1) * BT].rearrange("p c n -> p (c n)"),
                             out_ps[:, :]).then_inc(sem.out_copied, 1)

                for u in range(4):
                    copy_raw(0, u)
                for u in range(4):
                    square(0, u)
                for v in range(4):
                    copy_v(0, v)
                inverse_norms(0)
                for b in range(BLOCKS):
                    more = b + 1 < BLOCKS
                    exponentials(b, 0)
                    exponentials(b, 1)
                    if more:
                        copy_raw(b + 1, 0)
                        copy_raw(b + 1, 1)
                    exponentials(b, 2)
                    if more:
                        copy_raw(b + 1, 2)
                        copy_raw(b + 1, 3)
                    exponentials(b, 3)
                    if more:
                        for u in range(4):
                            square(b + 1, u)
                        for v in range(4):
                            copy_v(b + 1, v)
                        inverse_norms(b + 1)
                    copy_out(b, 0)
                    copy_out(b, 1)

        @block.vector
        def _(dve):
            dve.memset(raw_k[:, :, 0:PREV], 0.0).then_inc(sem.tables_ready, 1)
            dve.memset(r.inv_k[:, 0:PREV], 0.0).then_inc(sem.tables_ready, 1)
            lay = bass.ds(L, 1)
            for s, (tab, col) in enumerate(((0, 0), (1, 1), (0, 1), (1, 0))):
                dve.tensor_scalar(r.tab_q[:, s, :], r.base_tab[:, tab, PREV:], r.qk_scale[:, lay, col], None, ALU.mult
                                  ).then_inc(sem.tables_ready, 1)
                dve.tensor_scalar(r.tab_k[:, s, :], r.base_tab[:, 2 + tab, :], r.qk_scale[:, lay, 2 + col], None, ALU.mult
                                  ).then_inc(sem.tables_ready, 1)
            with dve.Fori(0, GROUPS) as g:
                n = L * GROUPS + g
                dve.wait_ge(sem.tables_ready, L * 10 + 10)

                def take_weights():
                    dve.wait_ge(sem.weights_loaded, n * 48 + 48)
                    dve.wait_ge(sem.work_read, at(n, 10, 0, 0))
                    for s in range(2):
                        dve.tensor_copy(r.w_qk[:, 2 * s:2 * s + 2, :].rearrange("p h (a d) -> p h a d", a=4),
                                        r.w_stage[:, s, :].rearrange("p (a h d) -> p h a d", a=4, h=2)
                                        ).then_inc(sem.weights_copied, 1)
                    dve.tensor_copy(r.w_v[:, :], r.w_stage[:, 2, :]).then_inc(sem.weights_copied, 1)

                def multiply(b):
                    dve.wait_ge(sem.summed, at(n, 4, b, 0))
                    for s, plane in enumerate((0, 1, 1, 0)):
                        dve.wait_ge(sem.work_read, at(n, 10, b, plane + 1))
                        dve.tensor_tensor(r.prod_q[:, s, :], raw_q[:, plane, :], r.tab_q[:, s, :], ALU.mult
                                          ).then_inc(sem.multiplied, 1)
                    dve.wait_ge(sem.tail_copied, at(n, 2, b, 0))
                    for s, plane in enumerate((0, 1, 1, 0)):
                        dve.wait_ge(sem.work_read, at(n, 10, b, plane + 3))
                        dve.tensor_tensor(r.prod_k[:, s, :], raw_k[:, plane, :], r.tab_k[:, s, :], ALU.mult
                                          ).then_inc(sem.multiplied, 1)

                def finish_rotation(b):
                    dve.wait_ge(sem.inverted_norms, at(n, 2, b, 2))
                    dve.wait_ge(sem.tail_copied, at(n, 2, b, 0))
                    for half in range(2):
                        dve.wait_ge(sem.summed, at(n, 4, b, half + 1))
                        dve.scalar_tensor_tensor(r.rot_q[:, half, :], r.inv_q[:, :], 1e12,
                                                 r.prod_q[:, 2 * half, :], ALU.min, ALU.mult).then_inc(sem.rotated, 1)
                    for half in range(2):
                        dve.wait_ge(sem.summed, at(n, 4, b, half + 3))
                        dve.scalar_tensor_tensor(r.rot_k[:, half, :], r.inv_k[:, :], 1e12,
                                                 r.prod_k[:, 2 * half, :], ALU.min, ALU.mult).then_inc(sem.rotated, 1)

                def maximum(b, a):
                    dve.wait_ge(sem.scored, at(n, 4, b, a + 1))
                    dve.tensor_reduce(r.row_max[:, a, :], scores[a][:, 0:4 * KC].rearrange("p (j k) -> p j k", j=4),
                                      AX.X, ALU.max).then_inc(sem.max_ready, 1)
                    dve.wait_ge(sem.max_ready, at(n, 4, b, a + 1))
                    dve.tensor_scalar(r.neg_max[:, a, :], r.row_max[:, a, :], -QK_SCALE, None, ALU.mult
                                      ).then_inc(sem.neg_max_ready, 1)

                def invert_sums(b, a):
                    dve.wait_ge(sem.exponentiated, at(n, 4, b, a + 1))
                    dve.reciprocal(r.inv_sums[:, a, :], r.sums[:, a, :]).then_inc(sem.sums_inverted, 1)

                def copy_turned(b, a):
                    dve.wait_ge(sem.turned, at(n, 4, b, a + 1))
                    if a >= 2:
                        dve.wait_ge(sem.attended, at(n, 4, b, a - 1))
                    else:
                        dve.wait_ge(sem.attended, at(n, 4, b, 0))
                    dve.tensor_copy(r.turned_sb[0:KC, a % 2, :], pt_ps[0:KC, :]).then_inc(sem.turned_copied, 1)

                take_weights()
                multiply(0)
                finish_rotation(0)
                for b in range(BLOCKS):
                    for a in range(4):
                        maximum(b, a)
                    invert_sums(b, 0)
                    invert_sums(b, 1)
                    if b + 1 < BLOCKS:
                        multiply(b + 1)
                    invert_sums(b, 2)
                    invert_sums(b, 3)
                    for a in range(4):
                        copy_turned(b, a)
                    if b + 1 < BLOCKS:
                        finish_rotation(b + 1)

        @block.gpsimd
        def _(pool):
            with pool.Fori(0, GROUPS) as g:
                n = L * GROUPS + g

                def sum_products(b):
                    for x, prod in enumerate((r.prod_q, r.prod_k)):
                        for half, op in ((0, ALU.subtract), (1, ALU.add)):
                            pool.wait_ge(sem.multiplied, at(n, 8, b, 4 * x + 2 * half + 2))
                            pool.tensor_tensor(prod[:, 2 * half, :], prod[:, 2 * half, :], prod[:, 2 * half + 1, :], op
                                               ).then_inc(sem.summed, 1)

                def copy_tails(b):
                    pool.wait_ge(sem.multiplied, at(n, 8, b, 8))
                    pool.wait_ge(sem.work_read, at(n, 10, b, 4))
                    tail = raw_k[:, :, BT:BT + PREV]
                    pool.tensor_tensor(raw_k[:, :, 0:PREV], tail, r.zeros[:, :, :], ALU.add).then_inc(sem.tail_copied, 1)
                    pool.wait_ge(sem.inverted_norms, at(n, 2, b, 2))
                    pool.wait_ge(sem.rotated, at(n, 4, b, 4))
                    tail = r.inv_k[:, BT:BT + PREV]
                    pool.tensor_tensor(r.inv_k[:, 0:PREV], tail, r.zeros[:, 0, :], ALU.add).then_inc(sem.tail_copied, 1)

                def normalise(b, a):
                    pool.wait_ge(sem.sums_inverted, at(n, 4, b, a + 1))
                    probs = r.probs[:, a, :].rearrange("p (j k) -> p j k", j=4)
                    pool.tensor_tensor(probs, probs, r.inv_sums[:, a, :].unsqueeze(2).to_broadcast([P, 4, KC]), ALU.mult
                                       ).then_inc(sem.normalised, 1)

                sum_products(0)
                copy_tails(0)
                for b in range(BLOCKS):
                    for a in range(4):
                        normalise(b, a)
                    if b + 1 < BLOCKS:
                        sum_products(b + 1)
                        copy_tails(b + 1)


def output_and_ffn(nc, L, r, sem):
    banks = r.banks
    y = r.y
    lay = bass.ds(L, 1)
    MID = ((0, P), (P, P), (2 * P, INNER2 - 2 * P))

    def at(per_block, b, k):
        return L * (BLOCKS * per_block) + (b * per_block + k + PRIMED)

    with nc.Block() as block:

        def moments(pe, b):
            pe.wait_ge(sem.ffn_shifted, at(2, b, 2))
            pe.matmul(banks[2 + b % 2][:, :], r.ones_mean[:, :], r.shifted[:, b % 2, :], start=True, stop=True
                      ).then_inc(sem.mean_made, 1)
            pe.wait_ge(sem.centred_squared, at(1, b, 1))
            if b >= 2:
                pe.wait_ge(sem.logged, at(1, b, -1))
            pe.matmul(banks[4 + b % 2][:, :], r.ones_mean[:, :], r.centred_sq[:, b % 2, :], start=True, stop=True
                      ).then_inc(sem.variance_made, 1)

        def down(pe, b):
            pe.wait_ge(sem.gate_applied, at(3, b, 3))
            if b >= 1:
                pe.wait_ge(sem.ffn_added, at(1, b, 0))
            for m, (first, size) in enumerate(MID):
                mm = pe.matmul(banks[6][:, :], r.w2[0:size, m, :], r.inner[0:size, b % 2, m, :], start=m == 0, stop=m == 2)
            mm.then_inc(sem.ffn_made, 1)

        @block.tensor
        def _(pe):
            pe.wait_ge(sem.ffn_loaded, L * 64 + 64)
            for b in range(BLOCKS):
                cols = slice(b * BT, (b + 1) * BT)
                if b >= 2:
                    pe.wait_ge(sem.residual_added, at(1, b, -1))
                for c in range(8):
                    mm = pe.matmul(banks[b % 2][:, :], r.wo[:, c, :], r.attn[:, c, cols], start=c == 0, stop=c == 7)
                mm.then_inc(sem.projected_out, 1)
                if b >= 1:
                    moments(pe, b - 1)
            moments(pe, BLOCKS - 1)
            for b in range(BLOCKS):
                pe.wait_ge(sem.ffn_normed, at(1, b, 1))
                if b == 0:
                    pe.wait_ge(sem.residual_added, at(1, 0, BLOCKS))
                    pe.wait_ge(sem.centred, at(1, 0, BLOCKS))
                    pe.wait_ge(sem.logged, at(1, 0, BLOCKS))
                for m, (first, size) in enumerate(MID):
                    for gate in (1, 0):
                        u = 6 * b + 2 * m + (1 - gate)
                        if b >= 1 and gate:
                            pe.wait_ge(sem.gated, at(3, b, m - 2))
                        elif b >= 1:
                            pe.wait_ge(sem.gate_applied, at(3, b, m - 2))
                        bank = banks[2 * m + gate]
                        pe.matmul(bank[0:size, :], r.w1[:, gate * INNER2 + first:gate * INNER2 + first + size],
                                  r.normed[:, b, :], start=True, stop=True).then_inc(sem.gate_made if gate else sem.value_made, 1)
                if b >= 1:
                    down(pe, b - 1)
            down(pe, BLOCKS - 1)

        def add_ffn(dve, b):
            cols = slice(1 + b * BT, 1 + (b + 1) * BT)
            dve.wait_ge(sem.ffn_made, at(1, b, 1))
            dve.scalar_tensor_tensor(y[:, cols], banks[6][:, :], r.b2[:, lay], y[:, cols], ALU.add, ALU.add
                                     ).then_inc(sem.ffn_added, 1)

        @block.vector
        def _(dve):
            for b in range(BLOCKS + 1):
                if b < BLOCKS:
                    cols = slice(1 + b * BT, 1 + (b + 1) * BT)
                    dve.wait_ge(sem.projected_out, at(1, b, 1))
                    dve.tensor_tensor(y[:, cols], banks[b % 2][:, :], y[:, cols], ALU.add).then_inc(sem.residual_added, 1)
                    dve.wait_ge(sem.residual_added, at(1, b, 1))
                    if b >= 2:
                        dve.wait_ge(sem.mean_made, at(1, b, -1))
                    dve.tensor_copy(r.shifted[0:64, b % 2, :], y[0:64, cols]).then_inc(sem.ffn_shifted, 1)
                    dve.tensor_copy(r.shifted[64:128, b % 2, :], y[64:128, b * BT:(b + 1) * BT]).then_inc(sem.ffn_shifted, 1)
                    dve.wait_ge(sem.ffn_shifted, at(2, b, 2))
                    dve.wait_ge(sem.mean_made, at(1, b, 1))
                    dve.tensor_tensor(r.centred[:, b % 2, :], r.shifted[:, b % 2, :], banks[2 + b % 2][:, :], ALU.subtract
                                      ).then_inc(sem.centred, 1)
                if b >= 1:
                    c = b - 1
                    dve.wait_ge(sem.inverse_std, at(1, c, 1))
                    dve.tensor_tensor(r.scaled[:, c % 2, :], r.centred[:, c % 2, :], r.inv_std[:, :], ALU.mult).then_inc(sem.scaled, 1)
                    dve.wait_ge(sem.scaled, at(1, c, 1))
                    dve.tensor_scalar(r.normed[:, c, :], r.scaled[:, c % 2, :], r.ln_gb[:, lay, 0], r.ln_gb[:, lay, 1],
                                      ALU.mult, ALU.add).then_inc(sem.ffn_normed, 1)
            for b in range(BLOCKS):
                for m, (first, size) in enumerate(MID):
                    dve.wait_ge(sem.gated, at(3, b, m + 1))
                    dve.wait_ge(sem.value_made, at(3, b, m + 1))
                    if b >= 2:
                        dve.wait_ge(sem.ffn_made, at(1, b, -1))
                    dve.scalar_tensor_tensor(r.inner[0:size, b % 2, m, :], banks[2 * m][0:size, :], r.b1_now[0:size, m:m + 1],
                                             r.gate[0:size, m, :], ALU.add, ALU.mult).then_inc(sem.gate_applied, 1)
                if b >= 1:
                    add_ffn(dve, b - 1)
            add_ffn(dve, BLOCKS - 1)
            dve.wait_ge(sem.ffn_added, at(1, 3, 1))
            dve.tensor_copy(r.ys[0:64, PREV:], y[0:64, 1:]).then_inc(sem.attn_shifted, 1)
            dve.tensor_copy(r.ys[64:128, PREV:], y[64:128, 0:T]).then_inc(sem.attn_shifted, 1)

        @block.scalar
        def _(act):
            act.copy(r.b1_now[:, :], r.b1[:, lay, :].rearrange("p l n -> p (l n)")).then_inc(sem.b1_copied, 1)
            for b in range(BLOCKS):
                act.wait_ge(sem.centred, at(1, b, 1))
                if b >= 2:
                    act.wait_ge(sem.variance_made, at(1, b, -1))
                act.activation(r.centred_sq[:, b % 2, :], r.centred[:, b % 2, :], ACT.Square).then_inc(sem.centred_squared, 1)
                act.wait_ge(sem.variance_made, at(1, b, 1))
                act.activation(r.log_var[:, :], banks[4 + b % 2][:, :], ACT.Ln, bias=r.eps[:, 0:1]).then_inc(sem.logged, 1)
                act.wait_ge(sem.logged, at(1, b, 1))
                if b >= 1:
                    act.wait_ge(sem.scaled, at(1, b, 0))
                act.activation(r.inv_std[:, :], r.log_var[:, :], ACT.Exp, scale=-0.5).then_inc(sem.inverse_std, 1)
            for b in range(BLOCKS):
                for m, (first, size) in enumerate(MID):
                    if b == 0 and m == 0:
                        act.wait_ge(sem.b1_copied, L + 1)
                    act.wait_ge(sem.gate_made, at(3, b, m + 1))
                    if b >= 1:
                        act.wait_ge(sem.gate_applied, at(3, b, m - 2))
                    act.activation(r.gate[0:size, m, :], banks[2 * m + 1][0:size, :], ACT.Gelu,
                                   bias=r.b1_now[0:size, 3 + m:4 + m]).then_inc(sem.gated, 1)
def semaphores(nc, ctx):
    sem = Record()
    sem.consts_loaded = ctx.enter_context(nc.semaphore("consts_loaded"))
    sem.x_loaded = ctx.enter_context(nc.semaphore("x_loaded"))
    sem.small_loaded = ctx.enter_context(nc.semaphore("small_loaded"))
    sem.cleared = ctx.enter_context(nc.semaphore("cleared"))
    sem.stats = ctx.enter_context(nc.semaphore("stats"))
    sem.aggregated = ctx.enter_context(nc.semaphore("aggregated"))
    sem.std_ready = ctx.enter_context(nc.semaphore("std_ready"))
    sem.rstd_ready = ctx.enter_context(nc.semaphore("rstd_ready"))
    sem.x_normed = ctx.enter_context(nc.semaphore("x_normed"))
    sem.x_transposed = ctx.enter_context(nc.semaphore("x_transposed"))
    sem.x_copied = ctx.enter_context(nc.semaphore("x_copied"))
    sem.wA_loaded = ctx.enter_context(nc.semaphore("wA_loaded"))
    sem.colsA_loaded = ctx.enter_context(nc.semaphore("colsA_loaded"))
    sem.powered = ctx.enter_context(nc.semaphore("powered"))
    sem.wA_turned = ctx.enter_context(nc.semaphore("wA_turned"))
    sem.bc_split = ctx.enter_context(nc.semaphore("bc_split"))
    sem.wA_ready = ctx.enter_context(nc.semaphore("wA_ready"))
    sem.xi_made = ctx.enter_context(nc.semaphore("xi_made"))
    sem.xi_copied = ctx.enter_context(nc.semaphore("xi_copied"))
    sem.bu_made = ctx.enter_context(nc.semaphore("bu_made"))
    sem.bu_copied = ctx.enter_context(nc.semaphore("bu_copied"))
    sem.diag_ready = ctx.enter_context(nc.semaphore("diag_ready"))
    sem.og_made = ctx.enter_context(nc.semaphore("og_made"))
    sem.o_gated = ctx.enter_context(nc.semaphore("o_gated"))
    sem.oT_copied = ctx.enter_context(nc.semaphore("oT_copied"))
    sem.aT_added = ctx.enter_context(nc.semaphore("aT_added"))
    sem.o_turned = ctx.enter_context(nc.semaphore("o_turned"))
    sem.aout_made = ctx.enter_context(nc.semaphore("aout_made"))
    sem.dt_exp = ctx.enter_context(nc.semaphore("dt_exp"))
    sem.sig_ready = ctx.enter_context(nc.semaphore("sig_ready"))
    sem.colchain = ctx.enter_context(nc.semaphore("colchain"))
    sem.coefs_ready = ctx.enter_context(nc.semaphore("coefs_ready"))
    sem.state_zeroed = ctx.enter_context(nc.semaphore("state_zeroed"))
    sem.osc1 = ctx.enter_context(nc.semaphore("osc1"))
    sem.osc2 = ctx.enter_context(nc.semaphore("osc2"))
    sem.osc_kept = ctx.enter_context(nc.semaphore("osc_kept"))
    sem.doubled = ctx.enter_context(nc.semaphore("doubled"))
    sem.silu_ready = ctx.enter_context(nc.semaphore("silu_ready"))
    sem.o_std = ctx.enter_context(nc.semaphore("o_std"))
    sem.o_rstd = ctx.enter_context(nc.semaphore("o_rstd"))
    sem.wB_loaded = ctx.enter_context(nc.semaphore("wB_loaded"))
    sem.router_exp = ctx.enter_context(nc.semaphore("router_exp"))
    sem.routed = ctx.enter_context(nc.semaphore("routed"))
    sem.experts_scaled = ctx.enter_context(nc.semaphore("experts_scaled"))
    sem.experts_made = ctx.enter_context(nc.semaphore("experts_made"))
    sem.top_found = ctx.enter_context(nc.semaphore("top_found"))
    sem.top_neg = ctx.enter_context(nc.semaphore("top_neg"))
    sem.index_found = ctx.enter_context(nc.semaphore("index_found"))
    sem.expert_found = ctx.enter_context(nc.semaphore("expert_found"))
    sem.expert_cast = ctx.enter_context(nc.semaphore("expert_cast"))
    sem.prob_ready = ctx.enter_context(nc.semaphore("prob_ready"))
    sem.selected = ctx.enter_context(nc.semaphore("selected"))
    sem.experts_summed = ctx.enter_context(nc.semaphore("experts_summed"))
    sem.moe_added = ctx.enter_context(nc.semaphore("moe_added"))
    sem.wC_loaded = ctx.enter_context(nc.semaphore("wC_loaded"))
    sem.parts_ready = ctx.enter_context(nc.semaphore("parts_ready"))
    sem.stacked = ctx.enter_context(nc.semaphore("stacked"))
    sem.qkC_made = ctx.enter_context(nc.semaphore("qkC_made"))
    sem.qkC_read = ctx.enter_context(nc.semaphore("qkC_read"))
    sem.vC_made = ctx.enter_context(nc.semaphore("vC_made"))
    sem.v_cleared = ctx.enter_context(nc.semaphore("v_cleared"))
    sem.vC_copied = ctx.enter_context(nc.semaphore("vC_copied"))
    sem.ones3_set = ctx.enter_context(nc.semaphore("ones3_set"))
    sem.ones_placed = ctx.enter_context(nc.semaphore("ones_placed"))
    sem.stack_loaded = ctx.enter_context(nc.semaphore("stack_loaded"))
    sem.max_split = ctx.enter_context(nc.semaphore("max_split"))
    sem.max_placed = ctx.enter_context(nc.semaphore("max_placed"))
    sem.taken = ctx.enter_context(nc.semaphore("taken"))
    sem.v_taken = ctx.enter_context(nc.semaphore("v_taken"))
    sem.part_max_done = ctx.enter_context(nc.semaphore("part_max_done"))
    sem.max_scored = ctx.enter_context(nc.semaphore("max_scored"))
    sem.max_ready_c = ctx.enter_context(nc.semaphore("max_ready_c"))
    sem.outputs_taken = ctx.enter_context(nc.semaphore("outputs_taken"))
    sem.max_turned = ctx.enter_context(nc.semaphore("max_turned"))
    sem.exp_done = ctx.enter_context(nc.semaphore("exp_done"))
    sem.weights_scored = ctx.enter_context(nc.semaphore("weights_scored"))
    sem.acc_copied = ctx.enter_context(nc.semaphore("acc_copied"))
    sem.valued = ctx.enter_context(nc.semaphore("valued"))
    sem.outputs_turned = ctx.enter_context(nc.semaphore("outputs_turned"))
    sem.max_reduced = ctx.enter_context(nc.semaphore("max_reduced"))
    sem.max_cut = ctx.enter_context(nc.semaphore("max_cut"))
    sem.den_inverted = ctx.enter_context(nc.semaphore("den_inverted"))
    sem.aC_copied = ctx.enter_context(nc.semaphore("aC_copied"))
    sem.aC_turned = ctx.enter_context(nc.semaphore("aC_turned"))
    sem.c_added = ctx.enter_context(nc.semaphore("c_added"))
    sem.c_out = ctx.enter_context(nc.semaphore("c_out"))
    sem.ffn_loaded = ctx.enter_context(nc.semaphore("ffn_loaded"))
    sem.weights_copied = ctx.enter_context(nc.semaphore("weights_copied"))
    sem.weights_loaded = ctx.enter_context(nc.semaphore("weights_loaded"))
    sem.work_read = ctx.enter_context(nc.semaphore("work_read"))
    sem.work_written = ctx.enter_context(nc.semaphore("work_written"))
    sem.squared = ctx.enter_context(nc.semaphore("squared"))
    sem.rotated = ctx.enter_context(nc.semaphore("rotated"))
    sem.scored = ctx.enter_context(nc.semaphore("scored"))
    sem.normalised = ctx.enter_context(nc.semaphore("normalised"))
    sem.turned_copied = ctx.enter_context(nc.semaphore("turned_copied"))
    sem.turned = ctx.enter_context(nc.semaphore("turned"))
    sem.out_copied = ctx.enter_context(nc.semaphore("out_copied"))
    sem.attended = ctx.enter_context(nc.semaphore("attended"))
    sem.multiplied = ctx.enter_context(nc.semaphore("multiplied"))
    sem.tail_copied = ctx.enter_context(nc.semaphore("tail_copied"))
    sem.inverted_norms = ctx.enter_context(nc.semaphore("inverted_norms"))
    sem.neg_max_ready = ctx.enter_context(nc.semaphore("neg_max_ready"))
    sem.max_ready = ctx.enter_context(nc.semaphore("max_ready"))
    sem.exponentiated = ctx.enter_context(nc.semaphore("exponentiated"))
    sem.tables_ready = ctx.enter_context(nc.semaphore("tables_ready"))
    sem.summed = ctx.enter_context(nc.semaphore("summed"))
    sem.sums_inverted = ctx.enter_context(nc.semaphore("sums_inverted"))
    sem.residual_added = ctx.enter_context(nc.semaphore("residual_added"))
    sem.projected_out = ctx.enter_context(nc.semaphore("projected_out"))
    sem.ffn_normed = ctx.enter_context(nc.semaphore("ffn_normed"))
    sem.gated = ctx.enter_context(nc.semaphore("gated"))
    sem.gate_applied = ctx.enter_context(nc.semaphore("gate_applied"))
    sem.gate_made = ctx.enter_context(nc.semaphore("gate_made"))
    sem.value_made = ctx.enter_context(nc.semaphore("value_made"))
    sem.ffn_shifted = ctx.enter_context(nc.semaphore("ffn_shifted"))
    sem.mean_made = ctx.enter_context(nc.semaphore("mean_made"))
    sem.centred_squared = ctx.enter_context(nc.semaphore("centred_squared"))
    sem.variance_made = ctx.enter_context(nc.semaphore("variance_made"))
    sem.ffn_added = ctx.enter_context(nc.semaphore("ffn_added"))
    sem.ffn_made = ctx.enter_context(nc.semaphore("ffn_made"))
    sem.centred = ctx.enter_context(nc.semaphore("centred"))
    sem.inverse_std = ctx.enter_context(nc.semaphore("inverse_std"))
    sem.scaled = ctx.enter_context(nc.semaphore("scaled"))
    sem.attn_shifted = ctx.enter_context(nc.semaphore("attn_shifted"))
    sem.logged = ctx.enter_context(nc.semaphore("logged"))
    sem.b1_copied = ctx.enter_context(nc.semaphore("b1_copied"))
    sem.b1_cleared = ctx.enter_context(nc.semaphore("b1_cleared"))
    sem.y_turned = ctx.enter_context(nc.semaphore("y_turned"))
    sem.out_summed = ctx.enter_context(nc.semaphore("out_summed"))
    sem.out_stored = ctx.enter_context(nc.semaphore("out_stored"))
    sem.y_shifted = ctx.enter_context(nc.semaphore("y_shifted"))
    return sem


def looped(sem):
    return (sem.acc_copied, sem.attended, sem.centred, sem.centred_squared, sem.den_inverted, sem.exp_done,
            sem.exponentiated, sem.ffn_added, sem.ffn_made, sem.ffn_normed, sem.ffn_shifted, sem.gate_applied,
            sem.gate_made, sem.gated, sem.inverse_std, sem.inverted_norms, sem.logged, sem.max_cut, sem.max_placed,
            sem.max_ready, sem.max_ready_c, sem.max_reduced, sem.max_scored, sem.max_split, sem.max_turned,
            sem.mean_made, sem.multiplied, sem.neg_max_ready, sem.normalised, sem.osc1, sem.osc2, sem.out_copied,
            sem.outputs_taken, sem.outputs_turned, sem.part_max_done, sem.projected_out, sem.residual_added,
            sem.rotated, sem.scaled, sem.scored, sem.squared, sem.stack_loaded, sem.summed, sem.sums_inverted,
            sem.tail_copied, sem.taken, sem.turned, sem.turned_copied, sem.v_taken, sem.value_made, sem.valued,
            sem.variance_made, sem.weights_copied, sem.weights_scored, sem.work_read, sem.work_written)



def program(nc, ins, const, out):
    ctx = ExitStack()
    with ctx:
        r = Record()
        sem = semaphores(nc, ctx)

        def sb(name, shape, dt=fp32, within=None):
            return (within or ctx).enter_context(nc.sbuf_tensor(name, shape, dt))

        psum = ctx.enter_context(nc.psum_tensor("psum", [P, 8, BT], fp32))
        r.banks = [psum[:, i, :] for i in range(8)]
        r.pairs = [psum[:, 0:2, :], psum[:, 2:4, :]]
        r.d = ins

        r.x = sb("x", [P, TILES, P])
        r.ident = sb("ident", [P, P])
        r.ones32 = sb("ones32", [P, P])
        r.ones_mean = sb("ones_mean", [P, P])
        r.iota8 = sb("iota8", [P, 8])
        r.ident_bf = sb("ident_bf", [P, P], bf16)
        r.mask_bf = sb("mask_bf", [P, 2, 4 * KC], bf16)
        r.causal_bf = sb("causal_bf", [P, 2, P], bf16)
        r.ones_row = sb("ones_row", [1, P])
        r.eps = sb("eps", [P, 1])
        r.tiny = sb("tiny", [P, 1])
        r.half_shift = sb("half_shift", [P, 1])
        r.stats = sb("stats", [P, TILES, 6])
        r.moments = sb("moments", [P, TILES, 2])
        r.std = sb("std", [P, TILES])
        r.rstd = sb("rstd", [P, TILES])
        r.base_tab = sb("base_tab", [P, 4, BT + PREV])
        first = {}
        k = 0
        for name, cols in CONSTS:
            first[name] = k
            k += cols

        with ExitStack() as own:
            mask_f = sb("mask_f", [P, 2, 4 * KC], within=own)
            causal_f = sb("causal_f", [P, 2, P], within=own)
            with nc.Block() as block:

                @block.sync
                def _(sp):
                    sp.dma_start(r.x[:, :, :], ins['L0_attn_hidden_states'].rearrange("o (t p) c -> p (o t) c", p=P)).then_inc(sem.x_loaded, 16)
                    for name, to in (("ident", r.ident[:, :]), ("ones32", r.ones32[:, :]), ("ones_mean", r.ones_mean[:, :]),
                                     ("mask", mask_f[:, :, :].rearrange("p a n -> p (a n)")),
                                     ("causal", causal_f[:, :, :].rearrange("p a n -> p (a n)")), ("iota8", r.iota8[:, :]),
                                     ("base_tab", r.base_tab[:, :, :].rearrange("p a n -> p (a n)"))):
                        n = dict(CONSTS)[name]
                        sp.dma_start(to, const[:, first[name]:first[name] + n]).then_inc(sem.consts_loaded, 16)
                    for semaphore in looped(sem):
                        sp.sem_inc(semaphore, PRIMED)
                    sp.wait_ge(sem.x_loaded, 16)

                @block.vector
                def _(dve):
                    dve.memset(r.ones_row[:, :], 1.0)
                    dve.memset(r.eps[:, :], EPS)
                    dve.memset(r.tiny[:, :], 2.0 ** -64)
                    dve.memset(r.half_shift[:, :], LN_2_10)
                    dve.wait_ge(sem.consts_loaded, 16 * len(CONSTS))
                    dve.tensor_copy(r.ident_bf[:, :], r.ident[:, :])
                    dve.tensor_copy(r.mask_bf[:, :, :], mask_f[:, :, :])
                    dve.tensor_copy(r.causal_bf[:, :, :], causal_f[:, :, :])

        with ExitStack() as own:
            r.x_norm = sb("x_norm", [P, TILES, P], within=own)
            r.hT = sb("hT", [P, T], within=own)

            with ExitStack() as a:
                r.ST, r.CH, r.LOG_ST, r.LOG_CH = 32, T // 32, 5, 6
                r.N_POW = r.LOG_ST + r.LOG_CH
                r.wA = sb("wA", [P, 3, P], within=a)
                r.wAT = sb("wAT", [P, 3, P], within=a)
                r.bc_raw = sb("bc_raw", [P, 2, 2 * P], within=a)
                r.bc = sb("bc", [P, 4, P], within=a)
                r.bcT = sb("bcT", [P, 4, P], within=a)
                r.colsA = sb("colsA", [P, 4], within=a)
                r.colt = sb("colt", [P, 4], within=a)
                r.coef = sb("coef", [P, 4], within=a)
                r.powers = sb("powers", [P, r.N_POW, 4], within=a)
                r.pw_tmp = sb("pw_tmp", [P, 4], within=a)
                r.diag_d = sb("diag_d", [P, P], within=a)
                r.xiT = sb("xiT", [P, T], within=a)
                r.bu = sb("bu", [P, 2, T], within=a)
                r.y_osc = sb("y_osc", [P, 2, T], within=a)
                r.state = sb("state", [P, 2, 2, 2, r.CH], within=a)
                r.drive = sb("drive", [P, 2, r.CH], within=a)
                r.sq_junk = sb("sq_junk", [P, P], within=a)
                r.o_ss = sb("o_ss", [P, TILES], within=a)
                r.sig = sb("sig", [P, 2, P], within=a)
                r.silu = sb("silu", [P, P], within=a)
                r.gated = sb("gated", [P, 2, P], within=a)
                r.gatedT = sb("gatedT", [P, 2, P], within=a)
                r.a_out = sb("a_out", [P, TILES, P], within=a)
                normalise_and_transpose(nc, r, sem, 0, r.hT, 0)
                oscillators(nc, r, sem)

            with ExitStack() as b:
                r.N_EXP = 8
                r.wgate = sb("wgate", [P, P], within=b)
                r.wexp = sb("wexp", [P, r.N_EXP, P], within=b)
                r.row_bg = sb("row_bg", [1, P], within=b)
                r.row_be = sb("row_be", [1, r.N_EXP * P], within=b)
                r.top8 = sb("top8", [P, 2, 8], within=b)
                r.top_neg = sb("top_neg", [P, 2, 1], within=b)
                r.top_at = sb("top_at", [P, 2, 8], u32, within=b)
                r.expert_u = sb("expert_u", [P, 2, 1], u32, within=b)
                r.expert_f = sb("expert_f", [P, 2, 1], within=b)
                r.top_p = sb("top_p", [P, 2, 1], within=b)
                r.router_sum = sb("router_sum", [P, 2, 1], within=b)
                r.select = sb("select", [P, 2, 8], within=b)
                r.junk = sb("junk", [P, P], within=b)
                r.scaled_exp = sb("scaled_exp", [P, 2, r.N_EXP, P], within=b)
                r.moe = sb("moe", [P, 2, P], within=b)
                normalise_and_transpose(nc, r, sem, 1, r.hT, 0)
                experts(nc, r, sem)

            with ExitStack() as c:
                d_stack = nc.dram_tensor("stacks", (2, HEADS, len(PRODUCTS), 8, T), bf16, kind="Internal").ap()
                r.d_stack = d_stack
                r.woC = sb("woC", [P, P], within=c)
                r.row_bo = sb("row_bo", [1, P], within=c)
                r.v_aug = sb("v_aug", [P, TILES, HEADS, 32], within=c)
                r.part_max = sb("part_max", [P, 4, TILES, BLOCKS], within=c)
                r.k_next = sb("k_next", [KPROD + 3, 4, T], bf16, within=c)
                r.ones3 = sb("ones3", [3, 4 * T], bf16, within=c)
                r.attn_tok = sb("attn_tok", [P, TILES, P], within=c)
                r.aC_T = sb("aC_T", [P, 2, P], within=c)
                normalise_and_transpose(nc, r, sem, 2, r.hT, 0)
                with ExitStack() as proj:
                    r.wqkvC = sb("wqkvC", [P, 3 * P], within=proj)
                    r.cols_bqk = sb("cols_bqk", [P, 2], within=proj)
                    r.row_bv = sb("row_bv", [1, P], within=proj)
                    r.qkf = sb("qkf", [P, 2, T], within=proj)
                    r.rest = sb("rest", [P, T], within=proj)
                    r.parts = sb("parts", [P, 2, 3, T], bf16, within=proj)
                    causal_projections(nc, r, sem)
                with ExitStack() as att:
                    r.q_next = sb("q_next", [KPROD + 3, 4, T], bf16, within=att)
                    r.q_now = sb("q_now", [KPROD + 3, 4, T], bf16, within=att)
                    r.k_now = sb("k_now", [KPROD + 3, 4, T], bf16, within=att)
                    r.v_now = sb("v_now", [P, TILES, 4, 32], within=att)
                    r.weights = sb("weights", [P, 2, 2, BT], within=att)
                    r.max_c = sb("max_c", [P, 4 * TILES], within=att)
                    r.neg_max_c = sb("neg_max_c", [P, P], within=att)
                    r.max_rows = sb("max_rows", [4 * TILES, 2, P], within=att)
                    r.max_parts = sb("max_parts", [4 * TILES, 3, P], bf16, within=att)
                    r.acc_sb = sb("acc_sb", [P, BT], within=att)
                    r.inv_den = sb("inv_den", [P, 4, 4], within=att)
                    causal_attention(nc, r, sem)
                causal_output(nc, r, sem)

        r.y = sb("y", [P, 1 + T])
        with ExitStack() as d:
            r.ys = sb("ys", [P, PREV + T], within=d)
            r.attn = sb("attn", [P, 8, T], within=d)
            r.wo = sb("wo", [P, 8, P], within=d)
            r.w1 = sb("w1", [P, 2 * INNER2], within=d)
            r.w2 = sb("w2", [P, 3, P], within=d)
            r.b1 = sb("b1", [P, DEPTH, 6], within=d)
            r.zeros = sb("zeros", [P, 2, PREV], within=d)
            r.b1_now = sb("b1_now", [P, 6], within=d)
            r.b2 = sb("b2", [P, DEPTH], within=d)
            r.ln_gb = sb("ln_gb", [P, DEPTH, 2], within=d)
            r.qk_scale = sb("qk_scale", [P, DEPTH, 4], within=d)
            r.d_wqkv, r.d_wo, r.d_w1, r.d_w2 = (ins['L1_ffn_' + w] for w in ('Wqkv', 'Wo', 'W1', 'W2'))
            with ExitStack() as own:
                r.x_norm = sb("x_norm_d", [P, TILES, P], within=own)
                normalise_and_transpose(nc, r, sem, 3, r.y, 1)
            with nc.Block() as block:

                @block.sync
                def _(sp):
                  with nc.allow_non_contiguous_dma(reason="columns of parameters, a few thousand elements"):
                    for h in range(2):
                        for a in range(4):
                            rows = slice(32 * a, 32 * a + 32)
                            for s, name in enumerate(('L1_ffn_q_scale', 'L1_ffn_k_scale')):
                                sp.dma_start(r.qk_scale[rows, :, 2 * s + h],
                                             ins[name][:, 32 * h:32 * h + 32].rearrange("l d -> d l")).then_inc(sem.small_loaded, 16)
                    for i, name in enumerate(('L1_ffn_ln_g', 'L1_ffn_ln_b')):
                        sp.dma_start(r.ln_gb[:, :, i], ins[name].rearrange("l d -> d l")).then_inc(sem.small_loaded, 16)
                    sp.dma_start(r.b2[:, :], ins['L1_ffn_b2'].rearrange("l d -> d l")).then_inc(sem.small_loaded, 16)
                    sp.wait_ge(sem.b1_cleared, 1)
                    for h in range(2):
                        for m in range(3):
                            size = min(P, INNER2 - m * P)
                            f = h * INNER2 + m * P
                            sp.dma_start(r.b1[0:size, :, 3 * h + m], ins['L1_ffn_b1'][:, f:f + size].rearrange("l d -> d l")).then_inc(sem.small_loaded, 16)
                    sp.wait_ge(sem.small_loaded, 16 * (16 + 3 + 6))

                @block.vector
                def _(dve):
                    dve.memset(r.b1[:, :, :], 0.0).then_inc(sem.b1_cleared, 1)
                    dve.memset(r.y[:, 0:1], 0.0).then_inc(sem.cleared, 1)
                    dve.memset(r.ys[:, 0:PREV], 0.0)
                    dve.memset(r.zeros[:, :, :], 0.0)
                    dve.wait_ge(sem.cleared, 1)
                    dve.tensor_copy(r.ys[0:64, PREV:], r.y[0:64, 1:]).then_inc(sem.y_shifted, 1)
                    dve.tensor_copy(r.ys[64:128, PREV:], r.y[64:128, 0:T]).then_inc(sem.y_shifted, 1)

            layers(nc, r, sem, sb)

        with ExitStack() as own:
            out_sb = sb("out_sb", [P, TILES, P], within=own)
            with nc.Block() as block:

                @block.tensor
                def _(pe):
                    for t in range(TILES):
                        mm = pe.transpose(r.banks[t // 4][:, (t % 4) * P:(t % 4 + 1) * P], r.y[:, 1 + t * P:1 + (t + 1) * P], r.ident[:, :])
                        if t % 4 == 3:
                            mm.then_inc(sem.y_turned, 1)

                @block.vector
                def _(dve):
                    for q in range(4):
                        dve.wait_ge(sem.y_turned, q + 1)
                        dve.tensor_tensor(out_sb[:, 4 * q:4 * q + 4, :].rearrange("p t c -> p (t c)"),
                                          r.x[:, 4 * q:4 * q + 4, :].rearrange("p t c -> p (t c)"), r.banks[q][:, :], ALU.add
                                          ).then_inc(sem.out_summed, 1)

                @block.sync
                def _(sp):
                    to = out.rearrange("o (t p) c -> p (o t) c", p=P)
                    for q in range(4):
                        sp.wait_ge(sem.out_summed, q + 1)
                        sp.dma_start(to[:, 4 * q:4 * q + 4, :], out_sb[:, 4 * q:4 * q + 4, :]).then_inc(sem.out_stored, 16)
                    sp.wait_ge(sem.out_stored, 64)


LN_2_10 = 6.931471805599453


def layers(nc, r, sem, sb):
    r.work_ps = [r.banks[4], r.banks[5]]
    r.scores_ps = r.banks[0:4]
    r.pt_ps, r.out_ps = r.banks[6], r.banks[7]
    with nc.Fori(0, DEPTH) as L:
        with ExitStack() as a:
            r.w_stage = sb("w_stage", [P, 3, GW], within=a)
            r.w_qk = sb("w_qk", [P, 4, P], within=a)
            r.w_v = sb("w_v", [P, GW], within=a)
            r.tab_q = sb("tab_q", [P, 4, BT], within=a)
            r.tab_k = sb("tab_k", [P, 4, BT + PREV], within=a)
            r.raw_q = sb("raw_q", [P, 2, BT], within=a)
            r.raw_k = sb("raw_k", [P, 2, BT + PREV], within=a)
            r.squares = sb("squares", [P, 4, BT], within=a)
            r.inv_q = sb("inv_q", [P, BT], within=a)
            r.inv_k = sb("inv_k", [P, BT + PREV], within=a)
            r.prod_q = sb("prod_q", [P, 4, BT], within=a)
            r.prod_k = sb("prod_k", [P, 4, BT + PREV], within=a)
            r.rot_q = sb("rot_q", [P, 2, BT], within=a)
            r.rot_k = sb("rot_k", [P, 2, BT + PREV], within=a)
            r.v_win = sb("v_win", [P, 2, 8, GW], within=a)
            r.probs = sb("probs", [P, 4, 4 * KC], within=a)
            r.turned_sb = sb("turned_sb", [P, 2, BT], within=a)
            r.row_max = sb("row_max", [P, 4, 4], within=a)
            r.neg_max = sb("neg_max", [P, 4, 4], within=a)
            r.sums = sb("sums", [P, 4, 4], within=a)
            r.inv_sums = sb("inv_sums", [P, 4, 4], within=a)
            windowed_attention(nc, L, r, sem)
        with ExitStack() as f:
            r.shifted = sb("shifted", [P, 2, BT], within=f)
            r.centred = sb("centred", [P, 2, BT], within=f)
            r.centred_sq = sb("centred_sq", [P, 2, BT], within=f)
            r.log_var = sb("log_var", [P, BT], within=f)
            r.inv_std = sb("inv_std", [P, BT], within=f)
            r.scaled = sb("scaled", [P, 2, BT], within=f)
            r.normed = sb("normed", [P, BLOCKS, BT], within=f)
            r.gate = sb("gate", [P, 3, BT], within=f)
            r.inner = sb("inner", [P, 2, 3, BT], within=f)
            output_and_ffn(nc, L, r, sem)


def constants():
    import numpy as np
    c = {}
    c["ident"] = np.eye(P)
    c["ones32"] = np.kron(np.eye(4), np.ones((32, 32)))
    c["ones_mean"] = np.full((P, P), 1.0 / P)
    q = np.arange(P)[:, None] % QC
    key = np.arange(KC)[None, :] - PREV
    allowed = (key <= q) & (q <= key + WINDOW)
    mask = np.where(allowed, 0.0, -1e30)
    later = np.tile(mask, (1, 4))
    first = later.copy()
    first[:QC, :PREV] = -1e30
    c["mask"] = np.concatenate([first, later], 1)
    tri = np.where(np.arange(P)[None, :] > np.arange(P)[:, None], -1e30, 0.0)
    c["causal"] = np.concatenate([tri, tri.T], 1)
    c["iota8"] = np.tile(np.arange(8.0), (P, 1))
    half = np.arange(0, DH, 2, dtype=np.float64)[:, None]
    pos = np.arange(-PREV, BT, dtype=np.float64)[None, :]
    angle = pos / 10000.0 ** (half / DH)
    scale = ((half + 0.4 * DH) / (1.4 * DH)) ** ((pos - BT // 2) / (WINDOW // 2))
    tabs = [np.cos(angle) * scale, np.sin(angle) * scale, np.cos(angle) / scale, np.sin(angle) / scale]
    c["base_tab"] = np.concatenate([np.tile(t, (4, 1)) for t in tabs], 1)
    return np.concatenate([c[n] for n, _ in CONSTS], 1).astype(np.float32)


def kernel(**inputs):
    import numpy as np
    import concourse.bacc as bacc
    from concourse.bass_utils import run_bass_kernel_spmd
    nc = bacc.Bacc("TRN2", target_bir_lowering=False, num_devices=1)
    arrays, aps = {}, {}
    for name in INPUTS:
        a = np.ascontiguousarray(inputs[name])
        arrays["in_" + name] = a
        aps[name] = nc.dram_tensor("in_" + name, a.shape, mybir.dt.from_np(a.dtype), kind="ExternalInput").ap()
    arrays["constants"] = constants()
    const = nc.dram_tensor("constants", arrays["constants"].shape, fp32, kind="ExternalInput").ap()
    out = nc.dram_tensor("out", (1, T, P), fp32, kind="ExternalOutput").ap()
    program(nc, aps, const, out)
    got = run_bass_kernel_spmd(nc, [arrays], core_ids=[0])
    return got.results[0]["out"]
```

```python
import concourse.bass as bass
import concourse.mybir as mybir
from contextlib import ExitStack

fp32, bf16, u32 = mybir.dt.float32, mybir.dt.bfloat16, mybir.dt.uint32
ACT = mybir.ActivationFunctionType
ALU = mybir.AluOpType
AX = mybir.AxisListType

P = 128
T = 2048
TILES = T // P
BT = 512
BLOCKS = T // BT
DEPTH = 6
HEADS, DH = 16, 64
INNER = HEADS * DH
GROUPS = 4
GW = 4 * DH
WINDOW = 32
PREV = WINDOW
QC = 64
KC = QC + PREV
QK_SCALE = 8.0
PRIMED = 1
INNER2 = int(P * 4 * 2 / 3)
EPS = 1e-5
PRODUCTS = ((0, 0), (0, 1), (1, 0), (0, 2), (2, 0), (1, 1))
KPROD = 8 * len(PRODUCTS)

CONSTS = (("ident", P), ("ones32", P), ("ones_mean", P), ("mask", 2 * 4 * KC), ("causal", 2 * P), ("iota8", 8),
          ("base_tab", 4 * (BT + PREV)))

INPUTS = ('L0_attn_hidden_states', 'L0_attn_Wi', 'L0_attn_Wg', 'L0_attn_Wo', 'L0_attn_A_diag', 'L0_attn_B_param',
          'L0_attn_C_param', 'L0_attn_D', 'L0_attn_dt', 'L0_attn_norm_weight', 'L0_ffn_Wg', 'L0_ffn_bg', 'L0_ffn_We',
          'L0_ffn_be', 'L1_attn_W_qkv', 'L1_attn_b_qkv', 'L1_attn_W_o', 'L1_attn_b_o', 'L1_ffn_Wqkv', 'L1_ffn_q_scale',
          'L1_ffn_k_scale', 'L1_ffn_Wo', 'L1_ffn_ln_g', 'L1_ffn_ln_b', 'L1_ffn_W1', 'L1_ffn_b1', 'L1_ffn_W2', 'L1_ffn_b2')


class Record:
    pass


def normalise_and_transpose(nc, r, sem, k, to, to_first):
    with nc.Block() as block:

        @block.vector
        def _(dve):
            for t in range(TILES):
                dve.bn_stats(r.stats[:, t, :], r.x[:, t, :]).then_inc(sem.stats, 1)
            dve.wait_ge(sem.stats, (k + 1) * TILES)
            for t in range(TILES):
                dve.bn_aggr(r.moments[:, t, :], r.stats[:, t, :]).then_inc(sem.aggregated, 1)
            dve.wait_ge(sem.std_ready, k + 1)
            dve.reciprocal(r.rstd[:, :], r.std[:, :]).then_inc(sem.rstd_ready, 1)
            dve.wait_ge(sem.rstd_ready, k + 1)
            for t in range(TILES):
                dve.tensor_scalar(r.x_norm[:, t, :], r.x[:, t, :], r.moments[:, t, 0:1], r.rstd[:, t:t + 1],
                                  ALU.subtract, ALU.mult).then_inc(sem.x_normed, 1)

        @block.scalar
        def _(act):
            act.wait_ge(sem.aggregated, (k + 1) * TILES)
            act.activation(r.std[:, :], r.moments[:, :, 1], ACT.Sqrt, bias=r.eps[:, 0:1]).then_inc(sem.std_ready, 1)
            for q in range(TILES // 4):
                act.wait_ge(sem.x_transposed, k * 4 + q + 1)
                act.copy(to[:, to_first + q * BT:to_first + (q + 1) * BT], r.banks[q][:, :]).then_inc(sem.x_copied, 1)

        @block.tensor
        def _(pe):
            for t in range(TILES):
                pe.wait_ge(sem.x_normed, k * TILES + t + 1)
                mm = pe.transpose(r.banks[t // 4][:, (t % 4) * P:(t % 4 + 1) * P], r.x_norm[:, t, :], r.ident[:, :])
                if t % 4 == 3:
                    mm.then_inc(sem.x_transposed, 1)


def oscillators(nc, r, sem):
    CH, ST = r.CH, r.ST
    hT, xiT, bu, ys2 = r.hT, r.xiT, r.bu, r.y_osc
    banks = r.banks

    with nc.Block() as block:

        @block.sync
        def _(sp):
            for i, (dst, src) in enumerate(((r.wA[:, 0, :], r.d['L0_attn_Wi']), (r.wA[:, 1, :], r.d['L0_attn_Wg']),
                                            (r.wA[:, 2, :], r.d['L0_attn_Wo']),
                                            (r.bc_raw[:, 0, :], r.d['L0_attn_B_param'].rearrange("p h c -> p (h c)")),
                                            (r.bc_raw[:, 1, :], r.d['L0_attn_C_param'].rearrange("p h c -> p (h c)")))):
                sp.dma_start(dst, src).then_inc(sem.wA_loaded, 16)
            for i, name in enumerate(('L0_attn_A_diag', 'L0_attn_dt', 'L0_attn_D', 'L0_attn_norm_weight')):
                sp.dma_start(r.colsA[:, i:i + 1], r.d[name].rearrange("(p o) -> p o", o=1)).then_inc(sem.colsA_loaded, 16)

        @block.gpsimd
        def _(pool):
            pool.wait_ge(sem.coefs_ready, 6)
            k = 0
            for s in range(r.N_POW - 1):
                m = r.powers[:, s, :]
                nxt = r.powers[:, s + 1, :]
                pool.tensor_tensor(r.pw_tmp[:, 0:1], m[:, 2:3], m[:, 3:4], ALU.mult).then_inc(sem.powered, 1)
                pool.tensor_tensor(r.pw_tmp[:, 1:2], m[:, 0:1], m[:, 1:2], ALU.add).then_inc(sem.powered, 1)
                pool.tensor_tensor(r.pw_tmp[:, 2:4], m[:, 0:2], m[:, 0:2], ALU.mult).then_inc(sem.powered, 1)
                k += 3
                pool.wait_ge(sem.powered, k)
                pool.tensor_scalar(nxt[:, 0:2], r.pw_tmp[:, 2:4], r.pw_tmp[:, 0:1], None, ALU.add).then_inc(sem.powered, 1)
                pool.tensor_scalar(nxt[:, 2:4], m[:, 2:4], r.pw_tmp[:, 1:2], None, ALU.mult).then_inc(sem.powered, 1)
                k += 2
                pool.wait_ge(sem.powered, k)

        @block.tensor
        def _(pe):
            pe.wait_ge(sem.wA_loaded, 80)
            for i in range(3):
                mm = pe.transpose(banks[4][:, i * P:(i + 1) * P], r.wA[:, i, :], r.ident[:, :])
            mm.then_inc(sem.wA_turned, 1)
            pe.wait_ge(sem.bc_split, 4)
            for i in range(4):
                mm = pe.transpose(banks[5][:, i * P:(i + 1) * P], r.bc[:, i, :], r.ident[:, :])
            mm.then_inc(sem.wA_turned, 1)
            pe.wait_ge(sem.wA_ready, 4)
            for b in range(BLOCKS):
                pe.matmul(banks[b][:, :], r.wAT[:, 0, :], hT[:, b * BT:(b + 1) * BT], start=True, stop=True
                          ).then_inc(sem.xi_made, 1)
            for c in range(2):
                for b in range(BLOCKS):
                    u = c * BLOCKS + b
                    bank = banks[6 + u % 2]
                    pe.wait_ge(sem.xi_copied, b + 1)
                    if u >= 2:
                        pe.wait_ge(sem.bu_copied, u - 1)
                    pe.matmul(bank[:, :], r.bcT[:, c, :], xiT[:, b * BT:(b + 1) * BT], start=True, stop=True
                              ).then_inc(sem.bu_made, 1)
            pe.wait_ge(sem.diag_ready, 1)
            for t in range(TILES + 2):
                if t < TILES:
                    tok = slice(t * P, (t + 1) * P)
                    if t == 0:
                        pe.wait_ge(sem.osc_kept, ST)
                    if t >= 4:
                        pe.wait_ge(sem.o_gated, t - 3)
                    bank = banks[t % 4]
                    pe.matmul(bank[:, 0:P], ys2[:, 0, tok], r.bcT[:, 2, :], start=True, stop=False)
                    pe.matmul(bank[:, 0:P], ys2[:, 1, tok], r.bcT[:, 3, :], start=False, stop=False)
                    pe.matmul(bank[:, 0:P], xiT[:, tok], r.diag_d[:, :], start=False, stop=True)
                    pe.matmul(bank[:, P:2 * P], hT[:, tok], r.wAT[:, 1, :], start=True, stop=True).then_inc(sem.og_made, 1)
                if 1 <= t <= TILES:
                    u = t - 1
                    pe.wait_ge(sem.o_gated, u + 1)
                    if u >= 2:
                        pe.wait_ge(sem.oT_copied, u - 1)
                    pe.transpose(banks[4 + u % 2][:, 0:P], r.gated[:, u % 2, :], r.ident[:, :]).then_inc(sem.o_turned, 1)
                if t >= 2:
                    u = t - 2
                    pe.wait_ge(sem.oT_copied, u + 1)
                    if u >= 2:
                        pe.wait_ge(sem.aT_added, u - 1)
                    pe.matmul(banks[6 + u % 2][:, 0:P], r.gatedT[:, u % 2, :], r.wAT[:, 2, :], start=True, stop=True
                              ).then_inc(sem.aout_made, 1)

        @block.scalar
        def _(act):
            act.wait_ge(sem.colsA_loaded, 64)
            act.activation(r.colt[:, 0:1], r.colsA[:, 1:2], ACT.Exp, scale=-1.0).then_inc(sem.dt_exp, 1)
            act.wait_ge(sem.wA_turned, 1)
            act.copy(r.wAT[:, 0:2, :].rearrange("p a n -> p (a n)"), banks[4][:, 0:2 * P]).then_inc(sem.wA_ready, 1)
            act.mul(r.wAT[:, 2, :], banks[4][:, 2 * P:3 * P], r.colsA[:, 3:4]).then_inc(sem.wA_ready, 1)
            act.wait_ge(sem.wA_turned, 2)
            act.copy(r.bcT[:, 0:3, :].rearrange("p a n -> p (a n)"), banks[5][:, 0:3 * P]).then_inc(sem.wA_ready, 1)
            act.mul(r.bcT[:, 3, :], banks[5][:, 3 * P:4 * P], -1.0).then_inc(sem.wA_ready, 1)
            for b in range(BLOCKS):
                act.wait_ge(sem.xi_made, b + 1)
                act.copy(xiT[:, b * BT:(b + 1) * BT], banks[b][:, :]).then_inc(sem.xi_copied, 1)
            act.wait_ge(sem.coefs_ready, 6)
            for u in range(2 * BLOCKS):
                act.wait_ge(sem.bu_made, u + 1)
                act.mul(bu[:, u // BLOCKS, (u % BLOCKS) * BT:(u % BLOCKS + 1) * BT], banks[6 + u % 2][:, :],
                        r.coef[:, 3:4]).then_inc(sem.bu_copied, 1)
            for t in range(TILES):
                act.wait_ge(sem.og_made, t + 1)
                act.activation(r.sq_junk[:, :], banks[t % 4][:, 0:P], ACT.Square, accum_out=r.o_ss[:, t:t + 1])
                if t >= 2:
                    act.wait_ge(sem.o_gated, t - 1)
                act.activation(r.sig[:, t % 2, :], banks[t % 4][:, P:2 * P], ACT.Sigmoid).then_inc(sem.sig_ready, 1)
                act.wait_ge(sem.o_turned, t + 1)
                if t >= 2:
                    act.wait_ge(sem.aout_made, t - 1)
                act.copy(r.gatedT[:, t % 2, :], banks[4 + t % 2][:, 0:P]).then_inc(sem.oT_copied, 1)

        @block.vector
        def _(dve):
            co, ca, ct = r.coef, r.colsA, r.colt
            dve.wait_ge(sem.dt_exp, 1)
            k = 0

            def link(ins):
                nonlocal k
                k += 1
                ins.then_inc(sem.colchain, 1)
                dve.wait_ge(sem.colchain, k)

            link(dve.tensor_scalar(ct[:, 1:2], ct[:, 0:1], 1.0, None, ALU.add))
            link(dve.reciprocal(co[:, 2:3], ct[:, 1:2]))
            link(dve.tensor_scalar(ct[:, 2:3], ca[:, 0:1], 0.0, co[:, 2:3], ALU.max, ALU.mult))
            link(dve.tensor_scalar(ct[:, 3:4], ct[:, 2:3], co[:, 2:3], 1.0, ALU.mult, ALU.add))
            link(dve.reciprocal(co[:, 0:1], ct[:, 3:4]))
            dve.tensor_scalar(co[:, 3:4], co[:, 0:1], co[:, 2:3], None, ALU.mult).then_inc(sem.coefs_ready, 1)
            dve.tensor_scalar(co[:, 1:2], ct[:, 2:3], co[:, 0:1], -1.0, ALU.mult, ALU.mult).then_inc(sem.coefs_ready, 1)
            dve.tensor_copy(r.powers[:, 0, 0:1], co[:, 0:1]).then_inc(sem.coefs_ready, 1)
            dve.tensor_copy(r.powers[:, 0, 1:2], co[:, 0:1]).then_inc(sem.coefs_ready, 1)
            dve.tensor_scalar(r.powers[:, 0, 2:3], ct[:, 2:3], co[:, 0:1], -1.0, ALU.mult, ALU.mult).then_inc(sem.coefs_ready, 1)
            dve.tensor_scalar(r.powers[:, 0, 3:4], co[:, 0:1], co[:, 2:3], None, ALU.mult).then_inc(sem.coefs_ready, 1)
            dve.tensor_scalar(r.diag_d[:, :], r.ident[:, :], ca[:, 2:3], None, ALU.mult).then_inc(sem.diag_ready, 1)
            dve.wait_ge(sem.wA_loaded, 80)
            for i in range(4):
                dve.tensor_copy(r.bc[:, i, :], r.bc_raw[:, i // 2, :].rearrange("p (h c) -> p h c", c=2)[:, :, i % 2]
                                ).then_inc(sem.bc_split, 1)

            steps = bu[:, :, :].rearrange("p c (n s) -> p c n s", s=ST)
            outs = ys2[:, :, :].rearrange("p c (n s) -> p c n s", s=ST)
            dve.memset(r.state[:, 0, :, :, :], 0.0).then_inc(sem.state_zeroed, 1)
            dve.wait_ge(sem.state_zeroed, 1)
            dve.wait_ge(sem.bu_copied, 2 * BLOCKS)

            def run(z, y, counter, keep):
                with dve.Fori(0, ST // 4) as j4:
                    for i in range(4):
                        done = j4 * 12 + (3 * i + PRIMED)
                        now = steps[:, :, :, bass.ds(j4 * 4 + i, 1)].rearrange("p c n s -> p c (n s)")
                        y_old = y
                        dve.wait_ge(counter, done)
                        dve.scalar_tensor_tensor(r.drive[:, :, :], y_old, co[:, 1:2], now, ALU.mult, ALU.add).then_inc(counter, 1)
                        dve.wait_ge(counter, done + 1)
                        dve.scalar_tensor_tensor(z, z, co[:, 0:1], r.drive[:, :, :], ALU.mult, ALU.add).then_inc(counter, 1)
                        dve.wait_ge(counter, done + 2)
                        dve.scalar_tensor_tensor(y, z, co[:, 2:3], y_old, ALU.mult, ALU.add).then_inc(counter, 1)
                        if keep:
                            dve.wait_ge(counter, done + 3)
                            dve.tensor_copy(outs[:, :, :, bass.ds(j4 * 4 + i, 1)].rearrange("p c n s -> p c (n s)"), y
                                            ).then_inc(sem.osc_kept, 1)

            run(r.state[:, 0, 0, :, :], r.state[:, 0, 1, :, :], sem.osc1, False)
            dve.wait_ge(sem.osc1, 3 * ST + PRIMED)
            dve.wait_ge(sem.powered, 5 * (r.N_POW - 1))
            k2 = 0
            cur = 0
            for s in range(r.LOG_CH):
                d = 1 << s
                g = r.powers[:, r.LOG_ST + s, :]
                src, dst = r.state[:, cur], r.state[:, 1 - cur]
                zs, ysrc = src[:, 0, :, 0:CH - d], src[:, 1, :, 0:CH - d]
                dve.tensor_copy(dst[:, :, :, 0:d], src[:, :, :, 0:d]).then_inc(sem.doubled, 1)
                dve.scalar_tensor_tensor(dst[:, 0, :, d:CH], zs, g[:, 0:1], src[:, 0, :, d:CH], ALU.mult, ALU.add).then_inc(sem.doubled, 1)
                dve.scalar_tensor_tensor(dst[:, 1, :, d:CH], zs, g[:, 3:4], src[:, 1, :, d:CH], ALU.mult, ALU.add).then_inc(sem.doubled, 1)
                k2 += 3
                dve.wait_ge(sem.doubled, k2)
                dve.scalar_tensor_tensor(dst[:, 0, :, d:CH], ysrc, g[:, 2:3], dst[:, 0, :, d:CH], ALU.mult, ALU.add).then_inc(sem.doubled, 1)
                dve.scalar_tensor_tensor(dst[:, 1, :, d:CH], ysrc, g[:, 1:2], dst[:, 1, :, d:CH], ALU.mult, ALU.add).then_inc(sem.doubled, 1)
                k2 += 2
                dve.wait_ge(sem.doubled, k2)
                cur = 1 - cur
            src, dst = r.state[:, cur], r.state[:, 1 - cur]
            dve.memset(dst[:, :, :, 0:1], 0.0).then_inc(sem.doubled, 1)
            dve.tensor_copy(dst[:, 0, :, 1:CH], src[:, 0, :, 0:CH - 1]).then_inc(sem.doubled, 1)
            dve.tensor_copy(dst[:, 1, :, 1:CH], src[:, 1, :, 0:CH - 1]).then_inc(sem.doubled, 1)
            dve.wait_ge(sem.doubled, k2 + 3)
            run(dst[:, 0], dst[:, 1], sem.osc2, True)

            for t in range(TILES + 2):
                if t < TILES:
                    dve.wait_ge(sem.sig_ready, t + 1)
                    if t >= 2:
                        dve.wait_ge(sem.o_turned, t - 1)
                    dve.tensor_tensor(r.silu[:, :], banks[t % 4][:, P:2 * P], r.sig[:, t % 2, :], ALU.mult).then_inc(sem.silu_ready, 1)
                    dve.wait_ge(sem.silu_ready, t + 1)
                    dve.tensor_tensor(r.gated[:, t % 2, :], banks[t % 4][:, 0:P], r.silu[:, :], ALU.mult).then_inc(sem.o_gated, 1)
                if t >= 2:
                    u = t - 2
                    dve.wait_ge(sem.aout_made, u + 1)
                    dve.tensor_copy(r.a_out[:, u, :], banks[6 + u % 2][:, 0:P]).then_inc(sem.aT_added, 1)

    with nc.Block() as block:
        @block.scalar
        def _(act):
            act.activation(r.std[:, :], r.o_ss[:, :], ACT.Sqrt, bias=r.eps[:, 0:1], scale=1.0 / P).then_inc(sem.o_std, 1)

        @block.vector
        def _(dve):
            dve.wait_ge(sem.o_std, 1)
            dve.reciprocal(r.rstd[:, :], r.std[:, :]).then_inc(sem.o_rstd, 1)
            dve.wait_ge(sem.o_rstd, 1)
            for t in range(TILES):
                dve.scalar_tensor_tensor(r.x[:, t, :], r.a_out[:, t, :], r.rstd[:, t:t + 1], r.x[:, t, :], ALU.mult, ALU.add)


def experts(nc, r, sem):
    hT, banks = r.hT, r.banks
    with nc.Block() as block:

        @block.sync
        def _(sp):
            sp.dma_start(r.wgate[:, :], r.d['L0_ffn_Wg']).then_inc(sem.wB_loaded, 16)
            sp.dma_start(r.wexp[:, :, :], r.d['L0_ffn_We'].rearrange("e d f -> d e f")).then_inc(sem.wB_loaded, 16)
            sp.dma_start(r.row_bg[0:1, :], r.d['L0_ffn_bg'].rearrange("(o n) -> o n", o=1)).then_inc(sem.wB_loaded, 16)
            sp.dma_start(r.row_be[0:1, :], r.d['L0_ffn_be'].rearrange("(o e) f -> o (e f)", o=1)).then_inc(sem.wB_loaded, 16)

        @block.tensor
        def _(pe):
            pe.wait_ge(sem.wB_loaded, 64)
            for t in range(TILES):
                tok = slice(t * P, (t + 1) * P)
                if t >= 2:
                    pe.wait_ge(sem.router_exp, t - 1)
                bank = banks[t % 2]
                pe.matmul(bank[:, 0:P], hT[:, tok], r.wgate[:, :], start=True, stop=False)
                pe.matmul(bank[:, 0:P], r.ones_row[0:1, :], r.row_bg[0:1, :], start=False, stop=True).then_inc(sem.routed, 1)
                if t >= 2:
                    pe.wait_ge(sem.experts_scaled, t - 1)
                for h in range(2):
                    bank = banks[2 + 2 * (t % 2) + h]
                    pe.matmul(bank[:, :], hT[:, tok], r.wexp[:, 4 * h:4 * h + 4, :].rearrange("p e f -> p (e f)"), start=True, stop=False)
                    mm = pe.matmul(bank[:, :], r.ones_row[0:1, :], r.row_be[0:1, h * BT:(h + 1) * BT], start=False, stop=True)
                mm.then_inc(sem.experts_made, 1)

        @block.vector
        def _(dve):
            for t in range(TILES + 1):
                if t < TILES:
                    p = t % 2
                    dve.wait_ge(sem.routed, t + 1)
                    dve.max(r.top8[:, p, :], banks[p][:, 0:P]).then_inc(sem.top_found, 1)
                    dve.wait_ge(sem.top_found, t + 1)
                    if t >= 2:
                        dve.wait_ge(sem.router_exp, t - 1)
                    dve.tensor_scalar(r.top_neg[:, p, :], r.top8[:, p, 0:1], -1.0, None, ALU.mult).then_inc(sem.top_neg, 1)
                    dve.max_index(r.top_at[:, p, :], r.top8[:, p, :], banks[p][:, 0:P]).then_inc(sem.index_found, 1)
                    dve.wait_ge(sem.index_found, t + 1)
                    dve.tensor_scalar(r.expert_u[:, p, :], r.top_at[:, p, 0:1], r.N_EXP - 1, None, ALU.bitwise_and).then_inc(sem.expert_found, 1)
                    dve.wait_ge(sem.expert_found, t + 1)
                    dve.tensor_copy(r.expert_f[:, p, :], r.expert_u[:, p, :]).then_inc(sem.expert_cast, 1)
                    dve.wait_ge(sem.router_exp, t + 1)
                    dve.reciprocal(r.top_p[:, p, :], r.router_sum[:, p, :]).then_inc(sem.prob_ready, 1)
                    dve.wait_ge(sem.expert_cast, t + 1)
                    dve.wait_ge(sem.prob_ready, t + 1)
                    if t >= 2:
                        dve.wait_ge(sem.experts_scaled, t - 1)
                    dve.tensor_scalar(r.select[:, p, :], r.iota8[:, :], r.expert_f[:, p, :], r.top_p[:, p, :], ALU.is_equal, ALU.mult
                                      ).then_inc(sem.selected, 1)
                if t >= 1:
                    u = t - 1
                    dve.wait_ge(sem.experts_scaled, u + 1)
                    dve.tensor_reduce(r.moe[:, u % 2, :], r.scaled_exp[:, u % 2, :, :].rearrange("p e f -> p f e"), AX.X, ALU.add
                                      ).then_inc(sem.experts_summed, 1)
                    dve.wait_ge(sem.experts_summed, u + 1)
                    dve.tensor_tensor(r.x[:, u, :], r.x[:, u, :], r.moe[:, u % 2, :], ALU.add).then_inc(sem.moe_added, 1)

        @block.scalar
        def _(act):
            for t in range(TILES):
                p = t % 2
                act.wait_ge(sem.index_found, t + 1)
                act.wait_ge(sem.top_neg, t + 1)
                if t >= 2:
                    act.wait_ge(sem.prob_ready, t - 1)
                act.activation(r.junk[:, :], banks[p][:, 0:P], ACT.Exp, bias=r.top_neg[:, p, :], accum_out=r.router_sum[:, p, :]
                               ).then_inc(sem.router_exp, 1)
                act.wait_ge(sem.selected, t + 1)
                act.wait_ge(sem.experts_made, t + 1)
                if t >= 2:
                    act.wait_ge(sem.experts_summed, t - 1)
                for e in range(r.N_EXP):
                    a = act.activation(r.scaled_exp[:, p, e, :], banks[2 + 2 * p + e // 4][:, (e % 4) * P:(e % 4 + 1) * P], ACT.Relu,
                                       scale=r.select[:, p, e:e + 1])
                a.then_inc(sem.experts_scaled, 1)


def causal_projections(nc, r, sem):
    hT, banks = r.hT, r.banks
    with nc.Block() as block:

        @block.sync
        def _(sp):
            sp.dma_start(r.wqkvC[:, :], r.d['L1_attn_W_qkv']).then_inc(sem.wC_loaded, 16)
            sp.dma_start(r.woC[:, :], r.d['L1_attn_W_o']).then_inc(sem.wC_loaded, 16)
            for i in range(2):
                sp.dma_start(r.cols_bqk[:, i:i + 1], r.d['L1_attn_b_qkv'][i * P:(i + 1) * P].rearrange("(p o) -> p o", o=1)).then_inc(sem.wC_loaded, 16)
            sp.dma_start(r.row_bv[0:1, :], r.d['L1_attn_b_qkv'][2 * P:3 * P].rearrange("(o n) -> o n", o=1)).then_inc(sem.wC_loaded, 16)
            sp.dma_start(r.row_bo[0:1, :], r.d['L1_attn_b_o'].rearrange("(o n) -> o n", o=1)).then_inc(sem.wC_loaded, 16)
            for s in range(2):
                sp.wait_ge(sem.parts_ready, 5 * s + 5)
                for i, pair in enumerate(PRODUCTS):
                    sp.dma_start(r.d_stack[s, :, i],
                                 r.parts[:, s, pair[s], :]).then_inc(sem.stacked, 16)
            sp.wait_ge(sem.stacked, 2 * len(PRODUCTS) * 16)

        @block.tensor
        def _(pe):
            pe.wait_ge(sem.wC_loaded, 96)
            for s in range(2):
                for b in range(BLOCKS):
                    pe.matmul(banks[4 * s + b][:, :], r.wqkvC[:, s * P:(s + 1) * P], hT[:, b * BT:(b + 1) * BT], start=True, stop=True
                              ).then_inc(sem.qkC_made, 1)
            for t in range(TILES):
                if t % 4 == 0:
                    pe.wait_ge(sem.qkC_read, t // 4 + 1)
                bank = banks[t // 4]
                pe.matmul(bank[:, (t % 4) * P:(t % 4 + 1) * P], hT[:, t * P:(t + 1) * P], r.wqkvC[:, 2 * P:3 * P], start=True, stop=False)
                mm = pe.matmul(bank[:, (t % 4) * P:(t % 4 + 1) * P], r.ones_row[0:1, :], r.row_bv[0:1, :], start=False, stop=True)
                if t % 4 == 3:
                    mm.then_inc(sem.vC_made, 1)

        @block.vector
        def _(dve):
            dve.wait_ge(sem.wC_loaded, 96)
            for s in range(2):
                for b in range(BLOCKS):
                    dve.wait_ge(sem.qkC_made, s * BLOCKS + b + 1)
                    dve.tensor_scalar(r.qkf[:, s, b * BT:(b + 1) * BT], banks[4 * s + b][:, :], r.cols_bqk[:, s:s + 1],
                                      8 ** -0.5 if s == 0 else 1.0, ALU.add, ALU.mult).then_inc(sem.qkC_read, 1)
                dve.wait_ge(sem.qkC_read, BLOCKS * (s + 1))
                full, rest = r.qkf[:, s, :], r.rest[:, :]
                hi, mid, lo = (r.parts[:, s, i, :] for i in range(3))
                k = 5 * s
                dve.tensor_copy(hi, full).then_inc(sem.parts_ready, 1)
                dve.wait_ge(sem.parts_ready, k + 1)
                dve.tensor_tensor(rest, full, hi, ALU.subtract).then_inc(sem.parts_ready, 1)
                dve.wait_ge(sem.parts_ready, k + 2)
                dve.tensor_copy(mid, rest).then_inc(sem.parts_ready, 1)
                dve.wait_ge(sem.parts_ready, k + 3)
                dve.tensor_tensor(lo, rest, mid, ALU.subtract).then_inc(sem.parts_ready, 2)
                dve.wait_ge(sem.parts_ready, k + 5)

        @block.scalar
        def _(act):
            act.wait_ge(sem.v_cleared, 2)
            for q in range(4):
                act.wait_ge(sem.vC_made, q + 1)
                for j in range(4):
                    act.copy(r.v_aug[:, 4 * q + j, :, 0:8], banks[q][:, j * P:(j + 1) * P].rearrange("p (h d) -> p h d", d=8)
                             ).then_inc(sem.vC_copied, 1)

        @block.gpsimd
        def _(pool):
            pool.memset(r.v_aug[:, :, :, :], 0.0).then_inc(sem.v_cleared, 1)
            pool.wait_ge(sem.v_cleared, 1)
            pool.memset(r.v_aug[:, :, :, 8:9], 1.0).then_inc(sem.v_cleared, 1)
            pool.memset(r.part_max[:, :, :, :], -3e38).then_inc(sem.v_cleared, 1)
            pool.memset(r.ones3[:, :], 1.0).then_inc(sem.ones3_set, 1)
            pool.wait_ge(sem.ones3_set, 1)
            pool.dma_start(r.k_next[KPROD:KPROD + 3, :, :].rearrange("p a t -> p (a t)"), r.ones3[:, :]).then_inc(sem.ones_placed, 16)
            pool.wait_ge(sem.ones_placed, 16)


def causal_attention(nc, r, sem):
    banks = r.banks
    maxb = (banks[5], banks[6])
    misc, acc = banks[7], banks[4]
    NH = 4
    MAXES = [(a, qt, kb) for qt in range(TILES) for a in range(NH) for kb in range(qt // 4 + 1)]
    STEPS = [(b, kt, pair) for b in range(BLOCKS) for kt in range(4 * b + 4) for pair in range(2)]
    NM, NSTEP = len(MAXES), len(STEPS)
    PER_STEP = -(-NM // NSTEP)

    def at(n, per_group, k):
        return n * per_group + (k + PRIMED)

    def first_query(b, kt):
        return max(0, kt - 4 * b) * P

    with nc.Block() as block:

        @block.sync
        def _(sp):
            def load(m):
                heads = bass.ds(m * NH, NH)
                for s, to in ((0, r.q_next), (1, r.k_next)):
                    sp.dma_start(to[0:KPROD, :, :], r.d_stack[s, heads].rearrange("h i d t -> (i d) h t")).then_inc(sem.stack_loaded, 16)

            def place_maxima(m):
                sp.wait_ge(sem.max_split, at(m, 4, 4))
                for i in range(3):
                    sp.dma_start(r.q_next[KPROD + i:KPROD + i + 1, :, :].rearrange("p a (q t) -> p (a q) t", t=P),
                                 r.max_parts[:, i, :]).then_inc(sem.max_placed, 16)

            load(0)
            place_maxima(0)
            with sp.Fori(0, GROUPS - 1) as n:
                sp.wait_ge(sem.taken, at(n, 2, 2))
                load(n + 1)
                place_maxima(n + 1)

        @block.tensor
        def _(pe):
            def maxima(m, i):
                a, qt, kb = MAXES[i]
                keys = min(BT, (qt + 1) * P - kb * BT)
                bank = maxb[i % 2]
                if i < 2:
                    pe.wait_ge(sem.part_max_done, at(m, NM, 0))
                else:
                    pe.wait_ge(sem.part_max_done, at(m, NM, i - 1))
                diag = kb == qt // 4
                mm = pe.matmul(bank[:, 0:keys], r.q_next[0:KPROD, a, qt * P:(qt + 1) * P], r.k_next[0:KPROD, a, kb * BT:kb * BT + keys],
                               start=True, stop=not diag, skip_group_check=True)
                if diag:
                    mm = pe.matmul(bank[:, keys - P:keys], r.ident_bf[:, :], r.causal_bf[:, 0, :], start=False, stop=True, skip_group_check=True)
                mm.then_inc(sem.max_scored, 1)

            def turn_maxima(m):
                pe.wait_ge(sem.max_ready_c, at(m, 1, 1))
                pe.wait_ge(sem.outputs_taken, at(m, BLOCKS, 0))
                pe.wait_ge(sem.max_split, at(m, 4, 0))
                pe.transpose(misc[:, 0:P], r.neg_max_c[:, :], r.ident[:, :]).then_inc(sem.max_turned, 1)

            def weights(n, i):
                b, kt, pair = STEPS[i]
                q0 = first_query(b, kt)
                if i < 2:
                    pe.wait_ge(sem.exp_done, at(n, NSTEP, 0))
                else:
                    pe.wait_ge(sem.exp_done, at(n, NSTEP, i - 1))
                for h in range(2):
                    a = 2 * pair + h
                    bank = banks[2 * (i % 2) + h]
                    diag = kt >= 4 * b
                    mm = pe.matmul(bank[:, q0:BT], r.k_now[0:KPROD + 3, a, kt * P:(kt + 1) * P], r.q_now[0:KPROD + 3, a, b * BT + q0:(b + 1) * BT],
                                   start=True, stop=not diag, skip_group_check=True)
                    if diag:
                        mm = pe.matmul(bank[:, q0:q0 + P], r.ident_bf[:, :], r.causal_bf[:, 1, :], start=False, stop=True, skip_group_check=True)
                mm.then_inc(sem.weights_scored, 1)

            def values(n, i):
                b, kt, pair = STEPS[i]
                q0 = first_query(b, kt)
                pe.wait_ge(sem.exp_done, at(n, NSTEP, i + 1))
                if kt == 0 and pair == 0:
                    pe.wait_ge(sem.acc_copied, at(n, BLOCKS, b))
                for h in range(2):
                    a = 2 * pair + h
                    mm = pe.matmul(acc[32 * a:32 * a + 32, q0:BT], r.v_now[:, kt, a, :], r.weights[:, i % 2, h, q0:BT],
                                   start=kt == 0, stop=kt == 4 * b + 3, skip_group_check=True)
                mm.then_inc(sem.valued, 1)

            def turn_outputs(n, b):
                pe.wait_ge(sem.acc_copied, at(n, BLOCKS, b + 1))
                pe.wait_ge(sem.outputs_taken, at(n, BLOCKS, b))
                for j in range(4):
                    mm = pe.transpose(misc[:, j * P:(j + 1) * P], r.acc_sb[:, j * P:(j + 1) * P], r.ident[:, :])
                mm.then_inc(sem.outputs_turned, 1)

            pe.wait_ge(sem.stack_loaded, 32 + PRIMED)
            for i in range(NM):
                maxima(0, i)
            turn_maxima(0)

            def body(n, more):
                pe.wait_ge(sem.taken, at(n, 2, 2))
                pe.wait_ge(sem.v_taken, at(n, 1, 1))
                mi = 0
                if more:
                    pe.wait_ge(sem.stack_loaded, at(n, 32, 64))
                for i in range(NSTEP + 1):
                    if i < NSTEP:
                        weights(n, i)
                    if more:
                        while mi < min(NM, PER_STEP * (i + 1)):
                            maxima(n + 1, mi)
                            mi += 1
                    if i >= 1:
                        values(n, i - 1)
                        b, kt, pair = STEPS[i - 1]
                        if b >= 1 and kt == 0 and pair == 1:
                            turn_outputs(n, b - 1)
                turn_outputs(n, BLOCKS - 1)
                if more:
                    turn_maxima(n + 1)

            with pe.Fori(0, GROUPS - 1) as n:
                body(n, True)
            body(GROUPS - 1, False)

        @block.scalar
        def _(act):
            def body(n):
                for i, (b, kt, pair) in enumerate(STEPS):
                    q0 = first_query(b, kt)
                    act.wait_ge(sem.weights_scored, at(n, NSTEP, i + 1))
                    if i >= 2:
                        act.wait_ge(sem.valued, at(n, NSTEP, i - 1))
                    else:
                        act.wait_ge(sem.valued, at(n, NSTEP, 0))
                    act.activation(r.weights[:, i % 2, :, q0:BT], r.pairs[i % 2][:, :, q0:BT], ACT.Exp).then_inc(sem.exp_done, 1)
            with act.Fori(0, GROUPS) as n:
                body(n)

        @block.vector
        def _(dve):
            def part_maxima(m, i):
                a, qt, kb = MAXES[i]
                keys = min(BT, (qt + 1) * P - kb * BT)
                dve.wait_ge(sem.max_scored, at(m, NM, i + 1))
                dve.tensor_reduce(r.part_max[:, a, qt, kb:kb + 1], maxb[i % 2][:, 0:keys], AX.X, ALU.max).then_inc(sem.part_max_done, 1)

            def finish_maxima(m):
                dve.wait_ge(sem.part_max_done, at(m, NM, NM))
                dve.tensor_reduce(r.max_c[:, :], r.part_max[:, :, :, :].rearrange("p a q k -> p (a q) k"), AX.X, ALU.max
                                  ).then_inc(sem.max_reduced, 1)
                dve.wait_ge(sem.max_reduced, at(m, 1, 1))
                dve.tensor_scalar(r.neg_max_c[:, 0:NH * TILES], r.max_c[:, :], -1.0, None, ALU.mult).then_inc(sem.max_ready_c, 1)
                dve.wait_ge(sem.max_turned, at(m, 1, 1))
                dve.wait_ge(sem.max_placed, at(m, 48, 0))
                full, rest = r.max_rows[:, 0, :], r.max_rows[:, 1, :]
                dve.tensor_copy(full, misc[0:NH * TILES, 0:P]).then_inc(sem.max_split, 1)
                dve.wait_ge(sem.max_split, at(m, 4, 1))
                dve.tensor_copy(r.max_parts[:, 0, :], full).then_inc(sem.max_cut, 1)
                dve.wait_ge(sem.max_cut, at(m, 2, 1))
                dve.tensor_tensor(rest, full, r.max_parts[:, 0, :], ALU.subtract).then_inc(sem.max_split, 1)
                dve.wait_ge(sem.max_split, at(m, 4, 2))
                dve.tensor_copy(r.max_parts[:, 1, :], rest).then_inc(sem.max_cut, 1)
                dve.wait_ge(sem.max_cut, at(m, 2, 2))
                dve.tensor_tensor(r.max_parts[:, 2, :], rest, r.max_parts[:, 1, :], ALU.subtract).then_inc(sem.max_split, 2)

            def take(n):
                dve.wait_ge(sem.max_placed, at(n, 48, 48))
                dve.wait_ge(sem.valued, at(n, NSTEP, 0))
                dve.tensor_copy(r.q_now[0:KPROD + 3, :, :], r.q_next[0:KPROD + 3, :, :]).then_inc(sem.taken, 1)
                dve.tensor_copy(r.k_now[0:KPROD + 3, :, :], r.k_next[0:KPROD + 3, :, :]).then_inc(sem.taken, 1)
                dve.tensor_copy(r.v_now[:, :, :, :], r.v_aug[:, :, bass.ds(n * NH, NH), :]).then_inc(sem.v_taken, 1)

            def copy_sums(n, b):
                dve.wait_ge(sem.valued, at(n, NSTEP, 4 * (b + 1) * (b + 2)))
                dve.wait_ge(sem.outputs_turned, at(n, BLOCKS, b))
                dve.tensor_copy(r.acc_sb[:, :], acc[:, :]).then_inc(sem.acc_copied, 1)

            def take_outputs(n, b):
                dve.wait_ge(sem.outputs_turned, at(n, BLOCKS, b + 1))
                v = misc[:, :].rearrange("p (j a c) -> p j a c", j=4, a=NH)
                dve.reciprocal(r.inv_den[:, :, :], v[:, :, :, 8]).then_inc(sem.den_inverted, 1)
                dve.wait_ge(sem.den_inverted, at(n, BLOCKS, b + 1))
                for j in range(4):
                    o = dve.tensor_tensor(r.attn_tok[:, 4 * b + j, bass.ds(n * 4 * 8, 32)].rearrange("p (a d) -> p a d", d=8),
                                          v[:, j, :, 0:8], r.inv_den[:, j, :].unsqueeze(2).to_broadcast([P, NH, 8]), ALU.mult)
                o.then_inc(sem.outputs_taken, 1)

            dve.wait_ge(sem.v_cleared, 3)
            dve.memset(r.neg_max_c[:, NH * TILES:P], 0.0)
            for i in range(NM):
                part_maxima(0, i)
            finish_maxima(0)

            def body(n, more):
                take(n)
                mi = 0
                for i in range(NSTEP + 1):
                    if more:
                        while mi < min(NM, PER_STEP * (i + 1)):
                            part_maxima(n + 1, mi)
                            mi += 1
                    if i >= 1:
                        b, kt, pair = STEPS[i - 1]
                        if kt == 4 * b + 3 and pair == 1:
                            copy_sums(n, b)
                        if b >= 1 and kt == 1 and pair == 0:
                            take_outputs(n, b - 1)
                take_outputs(n, BLOCKS - 1)
                if more:
                    finish_maxima(n + 1)

            with dve.Fori(0, GROUPS - 1) as n:
                body(n, True)
            body(GROUPS - 1, False)


def causal_output(nc, r, sem):
    banks = r.banks
    with nc.Block() as block:

        @block.tensor
        def _(pe):
            for t in range(TILES + 1):
                if t < TILES:
                    if t >= 2:
                        pe.wait_ge(sem.aC_copied, t - 1)
                    pe.transpose(banks[t % 2][:, 0:P], r.attn_tok[:, t, :], r.ident[:, :]).then_inc(sem.aC_turned, 1)
                if t >= 1:
                    u = t - 1
                    pe.wait_ge(sem.aC_copied, u + 1)
                    if u >= 2:
                        pe.wait_ge(sem.c_added, u - 1)
                    pe.matmul(banks[2 + u % 2][:, 0:P], r.aC_T[:, u % 2, :], r.woC[:, :], start=True, stop=False)
                    pe.matmul(banks[2 + u % 2][:, 0:P], r.ones_row[0:1, :], r.row_bo[0:1, :], start=False, stop=True).then_inc(sem.c_out, 1)

        @block.scalar
        def _(act):
            for t in range(TILES):
                act.wait_ge(sem.aC_turned, t + 1)
                if t >= 2:
                    act.wait_ge(sem.c_out, t - 1)
                act.copy(r.aC_T[:, t % 2, :], banks[t % 2][:, 0:P]).then_inc(sem.aC_copied, 1)

        @block.vector
        def _(dve):
            for t in range(TILES):
                dve.wait_ge(sem.c_out, t + 1)
                dve.tensor_tensor(r.x[:, t, :], r.x[:, t, :], banks[2 + t % 2][:, 0:P], ALU.add).then_inc(sem.c_added, 1)
def windowed_attention(nc, L, r, sem):
    ys, raw_q, raw_k, squares = r.ys, r.raw_q, r.raw_k, r.squares
    work, scores, pt_ps, out_ps = r.work_ps, r.scores_ps, r.pt_ps, r.out_ps

    def at(n, per_block, b, k):
        return n * (BLOCKS * per_block) + (b * per_block + k + PRIMED)

    PLACED = 16 * 12

    def exists(c, last):
        return c < BLOCKS or not last

    def run(engine, heads):
        first_blocks, _ = heads(L * GROUPS, 0, False)
        first_blocks()
        with engine.Fori(0, GROUPS - 1) as g:
            _, step = heads(L * GROUPS + g, g, False)
            for b in range(BLOCKS):
                step(b)
        _, step = heads(L * GROUPS + (GROUPS - 1), GROUPS - 1, True)
        for b in range(BLOCKS):
            step(b)

    def place_heads(sp, n, b):
        for half in range(2):
            sp.wait_ge(sem.rotated, at(n, 4, b, half + 1))
            for a in range(4):
                to = 64 * half + 32 * (a % 2)
                sp.dma_start(r.k_pair[to:to + 32, a // 2, a % 2, :], r.rot_k[32 * a:32 * a + 32, half, :]
                             ).then_inc(sem.placed, 16)
        for half in range(2):
            sp.wait_ge(sem.rotated, at(n, 4, b, half + 3))
            for hp in range(2):
                sp.dma_start(r.q_pair[64 * half:64 * half + 64, hp, :], r.rot_q[64 * hp:64 * hp + 64, half, :]
                             ).then_inc(sem.placed, 16)

    with nc.Block() as block:

        @block.sync
        def _(sp):
            base = r.d_tab.rearrange("p (a n) -> p a n", a=4)
            for twice in range(2):
                sp.dma_start(r.tab_q[:, 2 * twice:2 * twice + 2, :], base[:, 0:2, PREV:]).then_inc(sem.tables_loaded, 16)
                sp.dma_start(r.tab_k[:, 2 * twice:2 * twice + 2, :], base[:, 2:4, :]).then_inc(sem.tables_loaded, 16)
            lay = bass.ds(L, 1)
            sp.dma_start(r.wo[:, :, :], r.d_wo[lay].rearrange("l (c p) n -> p (l c) n", p=P)).then_inc(sem.ffn_loaded, 16)
            sp.dma_start(r.w1[:, :], r.d_w1[lay].rearrange("l p n -> p (l n)")).then_inc(sem.ffn_loaded, 16)
            sp.dma_start(r.w2[:, 0:2, :], r.d_w2[lay, 0:2 * P].rearrange("l (c p) n -> p (l c) n", p=P)).then_inc(sem.ffn_loaded, 16)
            sp.dma_start(r.w2[0:INNER2 - 2 * P, 2, :], r.d_w2[lay, 2 * P:INNER2].rearrange("l p n -> p (l n)")).then_inc(sem.ffn_loaded, 16)

            def load_weights(n, g):
                sp.wait_ge(sem.weights_copied, n * 3 + PRIMED)
                for s in range(3):
                    sp.dma_start(r.w_stage[:, s, :],
                                 r.d_wqkv[lay, :, bass.ds(g * GW + s * INNER, GW)].rearrange("l p n -> p (l n)")
                                 ).then_inc(sem.weights_loaded, 16)

            load_weights(L * GROUPS, 0)
            place_heads(sp, L * GROUPS, 0)
            with sp.Fori(0, GROUPS - 1) as g:
                n = L * GROUPS + g
                load_weights(n + 1, g + 1)
                for b in range(BLOCKS):
                    place_heads(sp, n, b + 1)
            for b in range(BLOCKS - 1):
                place_heads(sp, L * GROUPS + (GROUPS - 1), b + 1)

        @block.tensor
        def _(pe):
            def heads(n, g, last):
                def project(c):
                    tokens = slice(PREV + c % BLOCKS * BT, PREV + (c % BLOCKS + 1) * BT)
                    if c % BLOCKS == 0:
                        pe.wait_ge(sem.weights_copied, (n + c // BLOCKS) * 3 + (2 + PRIMED))
                    for u in range(4):
                        if u < 2:
                            pe.wait_ge(sem.norm_read, at(n, 2, c, 0))
                        else:
                            pe.wait_ge(sem.qk_read, at(n, 4, c, u - 1))
                        pe.matmul(work[u % 2][:, :], r.w_qk[:, u, :], ys[:, tokens],
                                  start=True, stop=True).then_inc(sem.qk_made, 1)

                def project_v(c, v):
                    if c % BLOCKS == 0 and v == 0:
                        pe.wait_ge(sem.weights_copied, (n + c // BLOCKS) * 3 + (3 + PRIMED))
                    if v >= 2:
                        pe.wait_ge(sem.v_read, at(n, 4, c, v - 1))
                    elif last and c == BLOCKS - 1:
                        pe.wait_ge(sem.norm_read, at(n, 2, c, 2))
                    else:
                        pe.wait_ge(sem.qk_read, at(n, 4, c + 1, v + 3))
                    for half in range(2):
                        chunk = 2 * v + half
                        first = c % BLOCKS * BT + chunk * QC
                        mm = pe.matmul(work[v % 2][0:KC, half * GW:(half + 1) * GW], ys[:, first:first + KC], r.w_v[:, :],
                                       start=True, stop=True)
                    mm.then_inc(sem.v_made, 1)

                def norms(b):
                    for s in range(2):
                        if b == 0:
                            pe.wait_ge(sem.qk_read, at(n, 4, b, s + 3))
                        else:
                            pe.wait_ge(sem.v_read, at(n, 4, b - 1, s + 3))
                        pe.wait_ge(sem.squares_summed, at(n, 2, b, s + 1))
                        pe.matmul(work[s][:, :], r.ones32[:, :], squares[:, 2 * s, :], start=True, stop=True
                                  ).then_inc(sem.norm_made, 1)

                def score(b):
                    pe.wait_ge(sem.placed, at(n, PLACED, b, PLACED))
                    for u in range(4):
                        hp, jh = u // 2, u % 2
                        bank = scores[u]
                        pe.matmul(bank[:, 0:4 * KC], r.ident_bf[:, :], r.mask_bf[:, 0 if b == 0 and jh == 0 else 1, :],
                                  start=True, stop=False, skip_group_check=True)
                        for jj in range(2):
                            for odd in range(2):
                                c = 4 * jh + 2 * jj + odd
                                mm = pe.matmul(bank[64 * odd:64 * odd + 64, jj * 2 * KC:(jj + 1) * 2 * KC],
                                               r.q_pair[:, hp, c * QC:(c + 1) * QC],
                                               r.k_pair[:, hp, :, c * QC:c * QC + KC],
                                               start=False, stop=True, skip_group_check=True)
                        mm.then_inc(sem.scored, 1)

                def turn(b, a):
                    pe.wait_ge(sem.normalised, at(n, 4, b, a + 1))
                    if b or a:
                        pe.wait_ge(sem.turned_copied, at(n, 4, b, a))
                    else:
                        pe.wait_ge(sem.turned_copied, at(n, 4, 0, 0))
                    for j in range(4):
                        mm = pe.transpose(pt_ps[0:KC, j * P:(j + 1) * P], r.probs[:, a, j * KC:(j + 1) * KC], r.ident[:, :])
                    mm.then_inc(sem.turned, 1)

                def attend(b, a):
                    pe.wait_ge(sem.turned_copied, at(n, 4, b, a + 1))
                    if a % 2 == 0:
                        pe.wait_ge(sem.out_copied, at(n, 2, b, a // 2))
                    hp, jh = a // 2, a % 2
                    for jj in range(2):
                        for odd in range(2):
                            c = 4 * jh + 2 * jj + odd
                            for hh in range(2):
                                first = (2 * jj + hh) * P + odd * QC
                                head = 2 * hp + hh
                                mm = pe.matmul(out_ps[64 * hh:64 * hh + 64, c * QC:(c + 1) * QC],
                                               r.v_win[0:KC, b % 2, c, head * DH:(head + 1) * DH],
                                               r.turned_sb[0:KC, a % 2, first:first + QC],
                                               start=True, stop=True)
                    mm.then_inc(sem.attended, 1)

                def first_blocks():
                    project(0)
                    norms(0)
                    project(1)
                    for v in range(4):
                        project_v(0, v)
                    norms(1)

                def step(b):
                    score(b)
                    if exists(b + 2, last):
                        project(b + 2)
                    turn(b, 0)
                    for a in range(4):
                        if exists(b + 1, last):
                            project_v(b + 1, a)
                        if a < 3:
                            turn(b, a + 1)
                        elif exists(b + 2, last):
                            norms(b + 2)
                        attend(b, a)

                return first_blocks, step

            run(pe, heads)

        @block.scalar
        def _(act):
            act.preload_act_table_set("natural_log_exp_and_others")

            def heads(n, g, last):
                def copy_raw(b, u):
                    if u == 0:
                        act.wait_ge(sem.multiplied, at(n, 8, b, 0))
                        act.wait_ge(sem.tail_copied, at(n, 1, b, 0))
                    act.wait_ge(sem.qk_made, at(n, 4, b, u + 1))
                    to = raw_q[:, u, :] if u < 2 else raw_k[:, u - 2, PREV:]
                    act.copy(to, work[u % 2][:, :]).then_inc(sem.qk_read, 1)

                def square(b, u):
                    act.wait_ge(sem.qk_read, at(n, 4, b, u + 1))
                    src = raw_q[:, u, :] if u < 2 else raw_k[:, u - 2, PREV:]
                    act.activation(squares[:, u, :], src, ACT.Square).then_inc(sem.squared, 1)

                def copy_v(b, v):
                    act.wait_ge(sem.v_made, at(n, 4, b, v + 1))
                    act.copy(r.v_win[0:KC, b % 2, 2 * v:2 * v + 2, :].rearrange("p c n -> p (c n)"),
                             work[v % 2][0:KC, :]).then_inc(sem.v_read, 1)

                def inverse_norms(b):
                    act.wait_ge(sem.rotated, at(n, 4, b, 0))
                    act.wait_ge(sem.norm_tail_copied, at(n, 1, b, 0))
                    to = (r.inv_q[:, :], r.inv_k[:, PREV:])
                    for s in range(2):
                        act.wait_ge(sem.norm_made, at(n, 2, b, s + 1))
                        act.activation(to[s], work[s][:, :], ACT.Ln, bias=r.tiny[:, 0:1],
                                       scale=float(2 ** 20)).then_inc(sem.norm_read, 1)
                    for s in range(2):
                        act.wait_ge(sem.norm_read, at(n, 2, b, s + 1))
                        act.activation(to[s], to[s], ACT.Exp, bias=r.half_shift[:, 0:1], scale=-0.5
                                       ).then_inc(sem.inverted_norms, 1)

                def exponentials(b, a):
                    act.wait_ge(sem.neg_max_ready, at(n, 4, b, a + 1))
                    for j in range(4):
                        e = act.activation(r.probs[:, a, j * KC:(j + 1) * KC], scores[a][:, j * KC:(j + 1) * KC], ACT.Exp,
                                           bias=r.neg_max[:, a, j:j + 1], scale=QK_SCALE,
                                           accum_out=r.sums[:, a, j:j + 1])
                    e.then_inc(sem.exponentiated, 1)

                def copy_out(b, pair):
                    act.wait_ge(sem.attended, at(n, 4, b, 2 * pair + 2))
                    act.copy(r.attn[:, bass.ds(g * 2 + pair, 1), b * BT:(b + 1) * BT].rearrange("p c n -> p (c n)"),
                             out_ps[:, :]).then_inc(sem.out_copied, 1)

                def first_blocks():
                    for u in range(4):
                        copy_raw(0, u)
                    for u in range(4):
                        square(0, u)
                    inverse_norms(0)
                    for u in range(4):
                        copy_raw(1, u)
                    for v in range(4):
                        copy_v(0, v)
                    for u in range(4):
                        square(1, u)
                    inverse_norms(1)

                def step(b):
                    for a in range(4):
                        exponentials(b, a)
                        if exists(b + 2, last):
                            copy_raw(b + 2, a)
                    if exists(b + 2, last):
                        for u in range(4):
                            square(b + 2, u)
                    if exists(b + 1, last):
                        for v in range(3):
                            copy_v(b + 1, v)
                    copy_out(b, 0)
                    if exists(b + 1, last):
                        copy_v(b + 1, 3)
                    if exists(b + 2, last):
                        inverse_norms(b + 2)
                    copy_out(b, 1)

                return first_blocks, step

            run(act, heads)

        @block.vector
        def _(dve):
            dve.memset(raw_k[:, :, 0:PREV], 0.0).then_inc(sem.tables_ready, 1)
            dve.memset(r.inv_k[:, 0:PREV], 0.0).then_inc(sem.tables_ready, 1)
            dve.memset(r.k_pair[:, :, :, :], 0.0).then_inc(sem.tables_ready, 1)
            lay = bass.ds(L, 1)
            dve.wait_ge(sem.tables_loaded, L * 64 + 64)
            for s, col in enumerate((0, 1, 1, 0)):
                dve.tensor_scalar(r.tab_q[:, s, :], r.tab_q[:, s, :], r.qk_scale[:, lay, col], None, ALU.mult
                                  ).then_inc(sem.tables_ready, 1)
                dve.tensor_scalar(r.tab_k[:, s, :], r.tab_k[:, s, :], r.qk_scale[:, lay, 2 + col], None, ALU.mult
                                  ).then_inc(sem.tables_ready, 1)
            dve.wait_ge(sem.tables_ready, L * 11 + 11)

            def heads(n, g, last):
                def take_weights(m):
                    dve.wait_ge(sem.weights_loaded, m * 48 + 48)
                    dve.wait_ge(sem.qk_read, at(m, 4, 0, 0))
                    for s in range(2):
                        dve.tensor_copy(r.w_qk[:, 2 * s:2 * s + 2, :].rearrange("p h (a d) -> p h a d", a=4),
                                        r.w_stage[:, s, :].rearrange("p (a h d) -> p h a d", a=4, h=2)
                                        ).then_inc(sem.weights_copied, 1)

                def take_v_weights(m):
                    dve.wait_ge(sem.v_read, at(m, 4, 0, 0))
                    dve.tensor_copy(r.w_v[:, :], r.w_stage[:, 2, :]).then_inc(sem.weights_copied, 1)

                def multiply(b, steps):
                    for step in steps:
                        s, plane = step % 4, (0, 1, 1, 0)[step % 4]
                        if step == 0:
                            dve.wait_ge(sem.summed, at(n, 4, b, 0))
                            dve.wait_ge(sem.rotated, at(n, 4, b, 0))
                        if step < 4:
                            dve.wait_ge(sem.qk_read, at(n, 4, b, plane + 1))
                            dve.tensor_tensor(r.prod_q[:, s, :], raw_q[:, plane, :], r.tab_q[:, s, :], ALU.mult
                                              ).then_inc(sem.multiplied, 1)
                        else:
                            if step == 4:
                                dve.wait_ge(sem.tail_copied, at(n, 1, b, 0))
                            dve.wait_ge(sem.qk_read, at(n, 4, b, plane + 3))
                            dve.tensor_tensor(r.prod_k[:, s, :], raw_k[:, plane, :], r.tab_k[:, s, :], ALU.mult
                                              ).then_inc(sem.multiplied, 1)

                def finish_rotation(b, half):
                    if half == 0:
                        dve.wait_ge(sem.placed, at(n, PLACED, b, 0))
                        dve.wait_ge(sem.inverted_norms, at(n, 2, b, 2))
                        dve.wait_ge(sem.norm_tail_copied, at(n, 1, b, 0))
                        dve.wait_ge(sem.summed, at(n, 4, b, 4))
                    to, inv, prod = (r.rot_k, r.inv_k, r.prod_k) if half < 2 else (r.rot_q, r.inv_q, r.prod_q)
                    dve.scalar_tensor_tensor(to[:, half % 2, :], inv[:, :], 1e12, prod[:, 2 * (half % 2), :],
                                             ALU.min, ALU.mult).then_inc(sem.rotated, 1)

                def maximum(b, a):
                    dve.wait_ge(sem.scored, at(n, 4, b, a + 1))
                    dve.tensor_reduce(r.row_max[:, a, :], scores[a][:, 0:4 * KC].rearrange("p (j k) -> p j k", j=4),
                                      AX.X, ALU.max).then_inc(sem.max_ready, 1)
                    dve.wait_ge(sem.max_ready, at(n, 4, b, a + 1))
                    dve.tensor_scalar(r.neg_max[:, a, :], r.row_max[:, a, :], -QK_SCALE, None, ALU.mult
                                      ).then_inc(sem.neg_max_ready, 1)

                def invert_sums(b, a):
                    dve.wait_ge(sem.exponentiated, at(n, 4, b, a + 1))
                    dve.reciprocal(r.inv_sums[:, a, :], r.sums[:, a, :]).then_inc(sem.sums_inverted, 1)

                def copy_turned(b, a):
                    dve.wait_ge(sem.turned, at(n, 4, b, a + 1))
                    if a >= 2:
                        dve.wait_ge(sem.attended, at(n, 4, b, a - 1))
                    else:
                        dve.wait_ge(sem.attended, at(n, 4, b, 0))
                    dve.tensor_copy(r.turned_sb[0:KC, a % 2, :], pt_ps[0:KC, :]).then_inc(sem.turned_copied, 1)

                def first_blocks():
                    take_weights(n)
                    take_v_weights(n)
                    multiply(0, range(8))
                    for half in range(4):
                        finish_rotation(0, half)
                    multiply(1, range(8))

                def step(b):
                    maximum(b, 0)
                    maximum(b, 1)
                    maximum(b, 2)
                    invert_sums(b, 0)
                    maximum(b, 3)
                    for a in range(4):
                        if exists(b + 1, last):
                            finish_rotation(b + 1, a)
                        if a < 3:
                            invert_sums(b, a + 1)
                        if a == 3 and exists(b + 2, last):
                            multiply(b + 2, range(0, 2))
                        copy_turned(b, a)
                    if exists(b + 2, last):
                        multiply(b + 2, range(2, 8))
                    if not last and b == 1:
                        take_weights(n + 1)
                    if not last and b == 2:
                        take_v_weights(n + 1)

                return first_blocks, step

            run(dve, heads)

        @block.gpsimd
        def _(pool):
            def heads(n, g, last):
                def sum_products(b):
                    for x, prod in enumerate((r.prod_q, r.prod_k)):
                        for half, op in ((0, ALU.subtract), (1, ALU.add)):
                            pool.wait_ge(sem.multiplied, at(n, 8, b, 4 * x + 2 * half + 2))
                            pool.tensor_tensor(prod[:, 2 * half, :], prod[:, 2 * half, :], prod[:, 2 * half + 1, :], op
                                               ).then_inc(sem.summed, 1)

                def sum_squares(b):
                    for s in range(2):
                        pool.wait_ge(sem.squared, at(n, 4, b, 2 * s + 2))
                        pool.tensor_tensor(squares[:, 2 * s, :], squares[:, 2 * s, :], squares[:, 2 * s + 1, :], ALU.add
                                           ).then_inc(sem.squares_summed, 1)

                def copy_tail(b):
                    pool.wait_ge(sem.multiplied, at(n, 8, b, 8))
                    pool.wait_ge(sem.qk_read, at(n, 4, b, 4))
                    tail = raw_k[:, :, BT:BT + PREV]
                    pool.tensor_tensor(raw_k[:, :, 0:PREV], tail, r.zeros[:, :, :], ALU.add).then_inc(sem.tail_copied, 1)

                def copy_norm_tail(b):
                    pool.wait_ge(sem.inverted_norms, at(n, 2, b, 2))
                    pool.wait_ge(sem.rotated, at(n, 4, b, 4))
                    tail = r.inv_k[:, BT:BT + PREV]
                    pool.tensor_tensor(r.inv_k[:, 0:PREV], tail, r.zeros[:, 0, :], ALU.add).then_inc(sem.norm_tail_copied, 1)

                def normalise(b, a):
                    pool.wait_ge(sem.sums_inverted, at(n, 4, b, a + 1))
                    probs = r.probs[:, a, :].rearrange("p (j k) -> p j k", j=4)
                    pool.tensor_tensor(probs, probs, r.inv_sums[:, a, :].unsqueeze(2).to_broadcast([P, 4, KC]), ALU.mult
                                       ).then_inc(sem.normalised, 1)

                def first_blocks():
                    sum_squares(0)
                    sum_products(0)
                    copy_tail(0)
                    copy_norm_tail(0)
                    sum_squares(1)
                    sum_products(1)
                    copy_tail(1)

                def step(b):
                    for a in range(4):
                        normalise(b, a)
                    if exists(b + 1, last):
                        copy_norm_tail(b + 1)
                    if exists(b + 2, last):
                        sum_squares(b + 2)
                        sum_products(b + 2)
                        copy_tail(b + 2)

                return first_blocks, step

            run(pool, heads)


def output_and_ffn(nc, L, r, sem):
    banks = r.banks
    y = r.y
    lay = bass.ds(L, 1)
    MID = ((0, P), (P, P), (2 * P, INNER2 - 2 * P))

    def at(per_block, b, k):
        return L * (BLOCKS * per_block) + (b * per_block + k + PRIMED)

    with nc.Block() as block:

        def moments(pe, b):
            pe.wait_ge(sem.ffn_shifted, at(2, b, 2))
            pe.matmul(banks[2 + b % 2][:, :], r.ones_mean[:, :], r.shifted[:, b % 2, :], start=True, stop=True
                      ).then_inc(sem.mean_made, 1)
            pe.wait_ge(sem.centred_squared, at(1, b, 1))
            if b >= 2:
                pe.wait_ge(sem.logged, at(1, b, -1))
            pe.matmul(banks[4 + b % 2][:, :], r.ones_mean[:, :], r.centred_sq[:, b % 2, :], start=True, stop=True
                      ).then_inc(sem.variance_made, 1)

        def down(pe, b):
            pe.wait_ge(sem.gate_applied, at(3, b, 3))
            if b >= 1:
                pe.wait_ge(sem.ffn_added, at(1, b, 0))
            for m, (first, size) in enumerate(MID):
                mm = pe.matmul(banks[6][:, :], r.w2[0:size, m, :], r.inner[0:size, b % 2, m, :], start=m == 0, stop=m == 2)
            mm.then_inc(sem.ffn_made, 1)

        @block.tensor
        def _(pe):
            pe.wait_ge(sem.ffn_loaded, L * 64 + 64)
            for b in range(BLOCKS):
                cols = slice(b * BT, (b + 1) * BT)
                if b >= 2:
                    pe.wait_ge(sem.residual_added, at(1, b, -1))
                for c in range(8):
                    mm = pe.matmul(banks[b % 2][:, :], r.wo[:, c, :], r.attn[:, c, cols], start=c == 0, stop=c == 7)
                mm.then_inc(sem.projected_out, 1)
                if b >= 1:
                    moments(pe, b - 1)
            moments(pe, BLOCKS - 1)
            for b in range(BLOCKS):
                pe.wait_ge(sem.ffn_normed, at(1, b, 1))
                if b == 0:
                    pe.wait_ge(sem.residual_added, at(1, 0, BLOCKS))
                    pe.wait_ge(sem.centred, at(1, 0, BLOCKS))
                    pe.wait_ge(sem.logged, at(1, 0, BLOCKS))
                for m, (first, size) in enumerate(MID):
                    for gate in (1, 0):
                        u = 6 * b + 2 * m + (1 - gate)
                        if b >= 1 and gate:
                            pe.wait_ge(sem.gated, at(3, b, m - 2))
                        elif b >= 1:
                            pe.wait_ge(sem.gate_applied, at(3, b, m - 2))
                        bank = banks[2 * m + gate]
                        pe.matmul(bank[0:size, :], r.w1[:, gate * INNER2 + first:gate * INNER2 + first + size],
                                  r.normed[:, b, :], start=True, stop=True).then_inc(sem.gate_made if gate else sem.value_made, 1)
                if b >= 1:
                    down(pe, b - 1)
            down(pe, BLOCKS - 1)

        def add_ffn(dve, b):
            cols = slice(1 + b * BT, 1 + (b + 1) * BT)
            dve.wait_ge(sem.ffn_made, at(1, b, 1))
            dve.scalar_tensor_tensor(y[:, cols], banks[6][:, :], r.b2[:, lay], y[:, cols], ALU.add, ALU.add
                                     ).then_inc(sem.ffn_added, 1)

        @block.vector
        def _(dve):
            for b in range(BLOCKS + 1):
                if b < BLOCKS:
                    cols = slice(1 + b * BT, 1 + (b + 1) * BT)
                    dve.wait_ge(sem.projected_out, at(1, b, 1))
                    dve.tensor_tensor(y[:, cols], banks[b % 2][:, :], y[:, cols], ALU.add).then_inc(sem.residual_added, 1)
                    dve.wait_ge(sem.residual_added, at(1, b, 1))
                    if b >= 2:
                        dve.wait_ge(sem.mean_made, at(1, b, -1))
                    dve.tensor_copy(r.shifted[0:64, b % 2, :], y[0:64, cols]).then_inc(sem.ffn_shifted, 1)
                    dve.tensor_copy(r.shifted[64:128, b % 2, :], y[64:128, b * BT:(b + 1) * BT]).then_inc(sem.ffn_shifted, 1)
                    dve.wait_ge(sem.ffn_shifted, at(2, b, 2))
                    dve.wait_ge(sem.mean_made, at(1, b, 1))
                    dve.tensor_tensor(r.centred[:, b % 2, :], r.shifted[:, b % 2, :], banks[2 + b % 2][:, :], ALU.subtract
                                      ).then_inc(sem.centred, 1)
                if b >= 1:
                    c = b - 1
                    dve.wait_ge(sem.inverse_std, at(1, c, 1))
                    dve.tensor_tensor(r.scaled[:, c % 2, :], r.centred[:, c % 2, :], r.inv_std[:, :], ALU.mult).then_inc(sem.scaled, 1)
                    dve.wait_ge(sem.scaled, at(1, c, 1))
                    dve.tensor_scalar(r.normed[:, c, :], r.scaled[:, c % 2, :], r.ln_gb[:, lay, 0], r.ln_gb[:, lay, 1],
                                      ALU.mult, ALU.add).then_inc(sem.ffn_normed, 1)
            for b in range(BLOCKS):
                for m, (first, size) in enumerate(MID):
                    dve.wait_ge(sem.gated, at(3, b, m + 1))
                    dve.wait_ge(sem.value_made, at(3, b, m + 1))
                    if b >= 2:
                        dve.wait_ge(sem.ffn_made, at(1, b, -1))
                    dve.scalar_tensor_tensor(r.inner[0:size, b % 2, m, :], banks[2 * m][0:size, :], r.b1_now[0:size, m:m + 1],
                                             r.gate[0:size, m, :], ALU.add, ALU.mult).then_inc(sem.gate_applied, 1)
                if b >= 1:
                    add_ffn(dve, b - 1)
            add_ffn(dve, BLOCKS - 1)
            dve.wait_ge(sem.ffn_added, at(1, 3, 1))
            dve.tensor_copy(r.ys[0:64, PREV:], y[0:64, 1:]).then_inc(sem.attn_shifted, 1)
            dve.tensor_copy(r.ys[64:128, PREV:], y[64:128, 0:T]).then_inc(sem.attn_shifted, 1)

        @block.scalar
        def _(act):
            act.preload_act_table_set("natural_log_exp_and_others")
            act.copy(r.b1_now[:, :], r.b1[:, lay, :].rearrange("p l n -> p (l n)")).then_inc(sem.b1_copied, 1)
            for b in range(BLOCKS):
                act.wait_ge(sem.centred, at(1, b, 1))
                if b >= 2:
                    act.wait_ge(sem.variance_made, at(1, b, -1))
                act.activation(r.centred_sq[:, b % 2, :], r.centred[:, b % 2, :], ACT.Square).then_inc(sem.centred_squared, 1)
                act.wait_ge(sem.variance_made, at(1, b, 1))
                act.activation(r.log_var[:, :], banks[4 + b % 2][:, :], ACT.Ln, bias=r.eps[:, 0:1]).then_inc(sem.logged, 1)
                act.wait_ge(sem.logged, at(1, b, 1))
                if b >= 1:
                    act.wait_ge(sem.scaled, at(1, b, 0))
                act.activation(r.inv_std[:, :], r.log_var[:, :], ACT.Exp, scale=-0.5).then_inc(sem.inverse_std, 1)
            for b in range(BLOCKS):
                for m, (first, size) in enumerate(MID):
                    if b == 0 and m == 0:
                        act.wait_ge(sem.b1_copied, L + 1)
                    act.wait_ge(sem.gate_made, at(3, b, m + 1))
                    if b >= 1:
                        act.wait_ge(sem.gate_applied, at(3, b, m - 2))
                    act.activation(r.gate[0:size, m, :], banks[2 * m + 1][0:size, :], ACT.Gelu,
                                   bias=r.b1_now[0:size, 3 + m:4 + m]).then_inc(sem.gated, 1)
def semaphores(nc, ctx):
    sem = Record()
    sem.consts_loaded = ctx.enter_context(nc.semaphore("consts_loaded"))
    sem.x_loaded = ctx.enter_context(nc.semaphore("x_loaded"))
    sem.small_loaded = ctx.enter_context(nc.semaphore("small_loaded"))
    sem.cleared = ctx.enter_context(nc.semaphore("cleared"))
    sem.stats = ctx.enter_context(nc.semaphore("stats"))
    sem.aggregated = ctx.enter_context(nc.semaphore("aggregated"))
    sem.std_ready = ctx.enter_context(nc.semaphore("std_ready"))
    sem.rstd_ready = ctx.enter_context(nc.semaphore("rstd_ready"))
    sem.x_normed = ctx.enter_context(nc.semaphore("x_normed"))
    sem.x_transposed = ctx.enter_context(nc.semaphore("x_transposed"))
    sem.x_copied = ctx.enter_context(nc.semaphore("x_copied"))
    sem.wA_loaded = ctx.enter_context(nc.semaphore("wA_loaded"))
    sem.colsA_loaded = ctx.enter_context(nc.semaphore("colsA_loaded"))
    sem.powered = ctx.enter_context(nc.semaphore("powered"))
    sem.wA_turned = ctx.enter_context(nc.semaphore("wA_turned"))
    sem.bc_split = ctx.enter_context(nc.semaphore("bc_split"))
    sem.wA_ready = ctx.enter_context(nc.semaphore("wA_ready"))
    sem.xi_made = ctx.enter_context(nc.semaphore("xi_made"))
    sem.xi_copied = ctx.enter_context(nc.semaphore("xi_copied"))
    sem.bu_made = ctx.enter_context(nc.semaphore("bu_made"))
    sem.bu_copied = ctx.enter_context(nc.semaphore("bu_copied"))
    sem.diag_ready = ctx.enter_context(nc.semaphore("diag_ready"))
    sem.og_made = ctx.enter_context(nc.semaphore("og_made"))
    sem.o_gated = ctx.enter_context(nc.semaphore("o_gated"))
    sem.oT_copied = ctx.enter_context(nc.semaphore("oT_copied"))
    sem.aT_added = ctx.enter_context(nc.semaphore("aT_added"))
    sem.o_turned = ctx.enter_context(nc.semaphore("o_turned"))
    sem.aout_made = ctx.enter_context(nc.semaphore("aout_made"))
    sem.dt_exp = ctx.enter_context(nc.semaphore("dt_exp"))
    sem.sig_ready = ctx.enter_context(nc.semaphore("sig_ready"))
    sem.colchain = ctx.enter_context(nc.semaphore("colchain"))
    sem.coefs_ready = ctx.enter_context(nc.semaphore("coefs_ready"))
    sem.state_zeroed = ctx.enter_context(nc.semaphore("state_zeroed"))
    sem.osc1 = ctx.enter_context(nc.semaphore("osc1"))
    sem.osc2 = ctx.enter_context(nc.semaphore("osc2"))
    sem.osc_kept = ctx.enter_context(nc.semaphore("osc_kept"))
    sem.doubled = ctx.enter_context(nc.semaphore("doubled"))
    sem.silu_ready = ctx.enter_context(nc.semaphore("silu_ready"))
    sem.o_std = ctx.enter_context(nc.semaphore("o_std"))
    sem.o_rstd = ctx.enter_context(nc.semaphore("o_rstd"))
    sem.wB_loaded = ctx.enter_context(nc.semaphore("wB_loaded"))
    sem.router_exp = ctx.enter_context(nc.semaphore("router_exp"))
    sem.routed = ctx.enter_context(nc.semaphore("routed"))
    sem.experts_scaled = ctx.enter_context(nc.semaphore("experts_scaled"))
    sem.experts_made = ctx.enter_context(nc.semaphore("experts_made"))
    sem.top_found = ctx.enter_context(nc.semaphore("top_found"))
    sem.top_neg = ctx.enter_context(nc.semaphore("top_neg"))
    sem.index_found = ctx.enter_context(nc.semaphore("index_found"))
    sem.expert_found = ctx.enter_context(nc.semaphore("expert_found"))
    sem.expert_cast = ctx.enter_context(nc.semaphore("expert_cast"))
    sem.prob_ready = ctx.enter_context(nc.semaphore("prob_ready"))
    sem.selected = ctx.enter_context(nc.semaphore("selected"))
    sem.experts_summed = ctx.enter_context(nc.semaphore("experts_summed"))
    sem.moe_added = ctx.enter_context(nc.semaphore("moe_added"))
    sem.wC_loaded = ctx.enter_context(nc.semaphore("wC_loaded"))
    sem.parts_ready = ctx.enter_context(nc.semaphore("parts_ready"))
    sem.stacked = ctx.enter_context(nc.semaphore("stacked"))
    sem.qkC_made = ctx.enter_context(nc.semaphore("qkC_made"))
    sem.qkC_read = ctx.enter_context(nc.semaphore("qkC_read"))
    sem.vC_made = ctx.enter_context(nc.semaphore("vC_made"))
    sem.v_cleared = ctx.enter_context(nc.semaphore("v_cleared"))
    sem.vC_copied = ctx.enter_context(nc.semaphore("vC_copied"))
    sem.ones3_set = ctx.enter_context(nc.semaphore("ones3_set"))
    sem.ones_placed = ctx.enter_context(nc.semaphore("ones_placed"))
    sem.stack_loaded = ctx.enter_context(nc.semaphore("stack_loaded"))
    sem.max_split = ctx.enter_context(nc.semaphore("max_split"))
    sem.max_placed = ctx.enter_context(nc.semaphore("max_placed"))
    sem.taken = ctx.enter_context(nc.semaphore("taken"))
    sem.v_taken = ctx.enter_context(nc.semaphore("v_taken"))
    sem.part_max_done = ctx.enter_context(nc.semaphore("part_max_done"))
    sem.max_scored = ctx.enter_context(nc.semaphore("max_scored"))
    sem.max_ready_c = ctx.enter_context(nc.semaphore("max_ready_c"))
    sem.outputs_taken = ctx.enter_context(nc.semaphore("outputs_taken"))
    sem.max_turned = ctx.enter_context(nc.semaphore("max_turned"))
    sem.exp_done = ctx.enter_context(nc.semaphore("exp_done"))
    sem.weights_scored = ctx.enter_context(nc.semaphore("weights_scored"))
    sem.acc_copied = ctx.enter_context(nc.semaphore("acc_copied"))
    sem.valued = ctx.enter_context(nc.semaphore("valued"))
    sem.outputs_turned = ctx.enter_context(nc.semaphore("outputs_turned"))
    sem.max_reduced = ctx.enter_context(nc.semaphore("max_reduced"))
    sem.max_cut = ctx.enter_context(nc.semaphore("max_cut"))
    sem.den_inverted = ctx.enter_context(nc.semaphore("den_inverted"))
    sem.aC_copied = ctx.enter_context(nc.semaphore("aC_copied"))
    sem.aC_turned = ctx.enter_context(nc.semaphore("aC_turned"))
    sem.c_added = ctx.enter_context(nc.semaphore("c_added"))
    sem.c_out = ctx.enter_context(nc.semaphore("c_out"))
    sem.ffn_loaded = ctx.enter_context(nc.semaphore("ffn_loaded"))
    sem.weights_copied = ctx.enter_context(nc.semaphore("weights_copied"))
    sem.weights_loaded = ctx.enter_context(nc.semaphore("weights_loaded"))
    sem.squared = ctx.enter_context(nc.semaphore("squared"))
    sem.rotated = ctx.enter_context(nc.semaphore("rotated"))
    sem.scored = ctx.enter_context(nc.semaphore("scored"))
    sem.normalised = ctx.enter_context(nc.semaphore("normalised"))
    sem.turned_copied = ctx.enter_context(nc.semaphore("turned_copied"))
    sem.turned = ctx.enter_context(nc.semaphore("turned"))
    sem.out_copied = ctx.enter_context(nc.semaphore("out_copied"))
    sem.attended = ctx.enter_context(nc.semaphore("attended"))
    sem.multiplied = ctx.enter_context(nc.semaphore("multiplied"))
    sem.tail_copied = ctx.enter_context(nc.semaphore("tail_copied"))
    sem.inverted_norms = ctx.enter_context(nc.semaphore("inverted_norms"))
    sem.neg_max_ready = ctx.enter_context(nc.semaphore("neg_max_ready"))
    sem.max_ready = ctx.enter_context(nc.semaphore("max_ready"))
    sem.exponentiated = ctx.enter_context(nc.semaphore("exponentiated"))
    sem.tables_ready = ctx.enter_context(nc.semaphore("tables_ready"))
    sem.summed = ctx.enter_context(nc.semaphore("summed"))
    sem.sums_inverted = ctx.enter_context(nc.semaphore("sums_inverted"))
    sem.residual_added = ctx.enter_context(nc.semaphore("residual_added"))
    sem.tables_loaded = ctx.enter_context(nc.semaphore("tables_loaded"))
    sem.qk_made = ctx.enter_context(nc.semaphore("qk_made"))
    sem.qk_read = ctx.enter_context(nc.semaphore("qk_read"))
    sem.v_made = ctx.enter_context(nc.semaphore("v_made"))
    sem.v_read = ctx.enter_context(nc.semaphore("v_read"))
    sem.norm_made = ctx.enter_context(nc.semaphore("norm_made"))
    sem.norm_read = ctx.enter_context(nc.semaphore("norm_read"))
    sem.norm_tail_copied = ctx.enter_context(nc.semaphore("norm_tail_copied"))
    sem.placed = ctx.enter_context(nc.semaphore("placed"))
    sem.squares_summed = ctx.enter_context(nc.semaphore("squares_summed"))
    sem.projected_out = ctx.enter_context(nc.semaphore("projected_out"))
    sem.ffn_normed = ctx.enter_context(nc.semaphore("ffn_normed"))
    sem.gated = ctx.enter_context(nc.semaphore("gated"))
    sem.gate_applied = ctx.enter_context(nc.semaphore("gate_applied"))
    sem.gate_made = ctx.enter_context(nc.semaphore("gate_made"))
    sem.value_made = ctx.enter_context(nc.semaphore("value_made"))
    sem.ffn_shifted = ctx.enter_context(nc.semaphore("ffn_shifted"))
    sem.mean_made = ctx.enter_context(nc.semaphore("mean_made"))
    sem.centred_squared = ctx.enter_context(nc.semaphore("centred_squared"))
    sem.variance_made = ctx.enter_context(nc.semaphore("variance_made"))
    sem.ffn_added = ctx.enter_context(nc.semaphore("ffn_added"))
    sem.ffn_made = ctx.enter_context(nc.semaphore("ffn_made"))
    sem.centred = ctx.enter_context(nc.semaphore("centred"))
    sem.inverse_std = ctx.enter_context(nc.semaphore("inverse_std"))
    sem.scaled = ctx.enter_context(nc.semaphore("scaled"))
    sem.attn_shifted = ctx.enter_context(nc.semaphore("attn_shifted"))
    sem.logged = ctx.enter_context(nc.semaphore("logged"))
    sem.b1_copied = ctx.enter_context(nc.semaphore("b1_copied"))
    sem.b1_cleared = ctx.enter_context(nc.semaphore("b1_cleared"))
    sem.y_turned = ctx.enter_context(nc.semaphore("y_turned"))
    sem.out_summed = ctx.enter_context(nc.semaphore("out_summed"))
    sem.out_stored = ctx.enter_context(nc.semaphore("out_stored"))
    sem.y_shifted = ctx.enter_context(nc.semaphore("y_shifted"))
    return sem


def looped(sem):
    return (sem.qk_made, sem.qk_read, sem.v_made, sem.v_read, sem.norm_made, sem.norm_read, sem.norm_tail_copied,
            sem.placed, sem.squares_summed, sem.acc_copied, sem.attended, sem.centred, sem.centred_squared, sem.den_inverted, sem.exp_done,
            sem.exponentiated, sem.ffn_added, sem.ffn_made, sem.ffn_normed, sem.ffn_shifted, sem.gate_applied,
            sem.gate_made, sem.gated, sem.inverse_std, sem.inverted_norms, sem.logged, sem.max_cut, sem.max_placed,
            sem.max_ready, sem.max_ready_c, sem.max_reduced, sem.max_scored, sem.max_split, sem.max_turned,
            sem.mean_made, sem.multiplied, sem.neg_max_ready, sem.normalised, sem.osc1, sem.osc2, sem.out_copied,
            sem.outputs_taken, sem.outputs_turned, sem.part_max_done, sem.projected_out, sem.residual_added,
            sem.rotated, sem.scaled, sem.scored, sem.squared, sem.stack_loaded, sem.summed, sem.sums_inverted,
            sem.tail_copied, sem.taken, sem.turned, sem.turned_copied, sem.v_taken, sem.value_made, sem.valued,
            sem.variance_made, sem.weights_copied, sem.weights_scored)



def program(nc, ins, const, out):
    ctx = ExitStack()
    with ctx:
        r = Record()
        sem = semaphores(nc, ctx)

        def sb(name, shape, dt=fp32, within=None):
            return (within or ctx).enter_context(nc.sbuf_tensor(name, shape, dt))

        psum = ctx.enter_context(nc.psum_tensor("psum", [P, 8, BT], fp32))
        r.banks = [psum[:, i, :] for i in range(8)]
        r.pairs = [psum[:, 0:2, :], psum[:, 2:4, :]]
        r.d = ins

        r.x = sb("x", [P, TILES, P])
        r.ident = sb("ident", [P, P])
        r.ones32 = sb("ones32", [P, P])
        r.ones_mean = sb("ones_mean", [P, P])
        r.ident_bf = sb("ident_bf", [P, P], bf16)
        r.mask_bf = sb("mask_bf", [P, 2, 4 * KC], bf16)
        r.eps = sb("eps", [P, 1])
        r.tiny = sb("tiny", [P, 1])
        r.half_shift = sb("half_shift", [P, 1])
        r.stats = sb("stats", [P, TILES, 6])
        r.moments = sb("moments", [P, TILES, 2])
        r.std = sb("std", [P, TILES])
        r.rstd = sb("rstd", [P, TILES])
        early = ctx.enter_context(ExitStack())
        r.iota8 = sb("iota8", [P, 8], within=early)
        r.causal_bf = sb("causal_bf", [P, 2, P], bf16, within=early)
        r.ones_row = sb("ones_row", [1, P], within=early)
        first = {}
        k = 0
        for name, cols in CONSTS:
            first[name] = k
            k += cols

        with ExitStack() as own:
            mask_f = sb("mask_f", [P, 2, 4 * KC], within=own)
            causal_f = sb("causal_f", [P, 2, P], within=own)
            with nc.Block() as block:

                @block.sync
                def _(sp):
                    sp.dma_start(r.x[:, :, :], ins['L0_attn_hidden_states'].rearrange("o (t p) c -> p (o t) c", p=P)).then_inc(sem.x_loaded, 16)
                    for name, to in (("ident", r.ident[:, :]), ("ones32", r.ones32[:, :]), ("ones_mean", r.ones_mean[:, :]),
                                     ("mask", mask_f[:, :, :].rearrange("p a n -> p (a n)")),
                                     ("causal", causal_f[:, :, :].rearrange("p a n -> p (a n)")), ("iota8", r.iota8[:, :])):
                        n = dict(CONSTS)[name]
                        sp.dma_start(to, const[:, first[name]:first[name] + n]).then_inc(sem.consts_loaded, 16)
                    for semaphore in looped(sem):
                        sp.sem_inc(semaphore, PRIMED)
                    sp.wait_ge(sem.x_loaded, 16)

                @block.vector
                def _(dve):
                    dve.memset(r.ones_row[:, :], 1.0)
                    dve.memset(r.eps[:, :], EPS)
                    dve.memset(r.tiny[:, :], 2.0 ** -64)
                    dve.memset(r.half_shift[:, :], LN_2_10)
                    dve.wait_ge(sem.consts_loaded, 16 * (len(CONSTS) - 1))
                    dve.tensor_copy(r.ident_bf[:, :], r.ident[:, :])
                    dve.tensor_copy(r.mask_bf[:, :, :], mask_f[:, :, :])
                    dve.tensor_copy(r.causal_bf[:, :, :], causal_f[:, :, :])

        with ExitStack() as own:
            r.x_norm = sb("x_norm", [P, TILES, P], within=own)
            r.hT = sb("hT", [P, T], within=own)

            with ExitStack() as a:
                r.ST, r.CH, r.LOG_ST, r.LOG_CH = 32, T // 32, 5, 6
                r.N_POW = r.LOG_ST + r.LOG_CH
                r.wA = sb("wA", [P, 3, P], within=a)
                r.wAT = sb("wAT", [P, 3, P], within=a)
                r.bc_raw = sb("bc_raw", [P, 2, 2 * P], within=a)
                r.bc = sb("bc", [P, 4, P], within=a)
                r.bcT = sb("bcT", [P, 4, P], within=a)
                r.colsA = sb("colsA", [P, 4], within=a)
                r.colt = sb("colt", [P, 4], within=a)
                r.coef = sb("coef", [P, 4], within=a)
                r.powers = sb("powers", [P, r.N_POW, 4], within=a)
                r.pw_tmp = sb("pw_tmp", [P, 4], within=a)
                r.diag_d = sb("diag_d", [P, P], within=a)
                r.xiT = sb("xiT", [P, T], within=a)
                r.bu = sb("bu", [P, 2, T], within=a)
                r.y_osc = sb("y_osc", [P, 2, T], within=a)
                r.state = sb("state", [P, 2, 2, 2, r.CH], within=a)
                r.drive = sb("drive", [P, 2, r.CH], within=a)
                r.sq_junk = sb("sq_junk", [P, P], within=a)
                r.o_ss = sb("o_ss", [P, TILES], within=a)
                r.sig = sb("sig", [P, 2, P], within=a)
                r.silu = sb("silu", [P, P], within=a)
                r.gated = sb("gated", [P, 2, P], within=a)
                r.gatedT = sb("gatedT", [P, 2, P], within=a)
                r.a_out = sb("a_out", [P, TILES, P], within=a)
                normalise_and_transpose(nc, r, sem, 0, r.hT, 0)
                oscillators(nc, r, sem)

            with ExitStack() as b:
                r.N_EXP = 8
                r.wgate = sb("wgate", [P, P], within=b)
                r.wexp = sb("wexp", [P, r.N_EXP, P], within=b)
                r.row_bg = sb("row_bg", [1, P], within=b)
                r.row_be = sb("row_be", [1, r.N_EXP * P], within=b)
                r.top8 = sb("top8", [P, 2, 8], within=b)
                r.top_neg = sb("top_neg", [P, 2, 1], within=b)
                r.top_at = sb("top_at", [P, 2, 8], u32, within=b)
                r.expert_u = sb("expert_u", [P, 2, 1], u32, within=b)
                r.expert_f = sb("expert_f", [P, 2, 1], within=b)
                r.top_p = sb("top_p", [P, 2, 1], within=b)
                r.router_sum = sb("router_sum", [P, 2, 1], within=b)
                r.select = sb("select", [P, 2, 8], within=b)
                r.junk = sb("junk", [P, P], within=b)
                r.scaled_exp = sb("scaled_exp", [P, 2, r.N_EXP, P], within=b)
                r.moe = sb("moe", [P, 2, P], within=b)
                normalise_and_transpose(nc, r, sem, 1, r.hT, 0)
                experts(nc, r, sem)

            with ExitStack() as c:
                d_stack = nc.dram_tensor("stacks", (2, HEADS, len(PRODUCTS), 8, T), bf16, kind="Internal").ap()
                r.d_stack = d_stack
                r.woC = sb("woC", [P, P], within=c)
                r.row_bo = sb("row_bo", [1, P], within=c)
                r.v_aug = sb("v_aug", [P, TILES, HEADS, 32], within=c)
                r.part_max = sb("part_max", [P, 4, TILES, BLOCKS], within=c)
                r.k_next = sb("k_next", [KPROD + 3, 4, T], bf16, within=c)
                r.ones3 = sb("ones3", [3, 4 * T], bf16, within=c)
                r.attn_tok = sb("attn_tok", [P, TILES, P], within=c)
                r.aC_T = sb("aC_T", [P, 2, P], within=c)
                normalise_and_transpose(nc, r, sem, 2, r.hT, 0)
                with ExitStack() as proj:
                    r.wqkvC = sb("wqkvC", [P, 3 * P], within=proj)
                    r.cols_bqk = sb("cols_bqk", [P, 2], within=proj)
                    r.row_bv = sb("row_bv", [1, P], within=proj)
                    r.qkf = sb("qkf", [P, 2, T], within=proj)
                    r.rest = sb("rest", [P, T], within=proj)
                    r.parts = sb("parts", [P, 2, 3, T], bf16, within=proj)
                    causal_projections(nc, r, sem)
                with ExitStack() as att:
                    r.q_next = sb("q_next", [KPROD + 3, 4, T], bf16, within=att)
                    r.q_now = sb("q_now", [KPROD + 3, 4, T], bf16, within=att)
                    r.k_now = sb("k_now", [KPROD + 3, 4, T], bf16, within=att)
                    r.v_now = sb("v_now", [P, TILES, 4, 32], within=att)
                    r.weights = sb("weights", [P, 2, 2, BT], within=att)
                    r.max_c = sb("max_c", [P, 4 * TILES], within=att)
                    r.neg_max_c = sb("neg_max_c", [P, P], within=att)
                    r.max_rows = sb("max_rows", [4 * TILES, 2, P], within=att)
                    r.max_parts = sb("max_parts", [4 * TILES, 3, P], bf16, within=att)
                    r.acc_sb = sb("acc_sb", [P, BT], within=att)
                    r.inv_den = sb("inv_den", [P, 4, 4], within=att)
                    causal_attention(nc, r, sem)
                causal_output(nc, r, sem)

        early.close()

        r.d_tab = const[:, first["base_tab"]:]
        r.y = sb("y", [P, 1 + T])
        with ExitStack() as d:
            r.ys = sb("ys", [P, PREV + T], within=d)
            r.attn = sb("attn", [P, 8, T], within=d)
            r.wo = sb("wo", [P, 8, P], within=d)
            r.w1 = sb("w1", [P, 2 * INNER2], within=d)
            r.w2 = sb("w2", [P, 3, P], within=d)
            r.b1 = sb("b1", [P, DEPTH, 6], within=d)
            r.zeros = sb("zeros", [P, 2, PREV], within=d)
            r.b1_now = sb("b1_now", [P, 6], within=d)
            r.b2 = sb("b2", [P, DEPTH], within=d)
            r.ln_gb = sb("ln_gb", [P, DEPTH, 2], within=d)
            r.qk_scale = sb("qk_scale", [P, DEPTH, 4], within=d)
            r.d_wqkv, r.d_wo, r.d_w1, r.d_w2 = (ins['L1_ffn_' + w] for w in ('Wqkv', 'Wo', 'W1', 'W2'))
            with ExitStack() as own:
                r.x_norm = sb("x_norm_d", [P, TILES, P], within=own)
                normalise_and_transpose(nc, r, sem, 3, r.y, 1)
            with nc.Block() as block:

                @block.sync
                def _(sp):
                  with nc.allow_non_contiguous_dma(reason="columns of parameters, a few thousand elements"):
                    for h in range(2):
                        for a in range(4):
                            rows = slice(32 * a, 32 * a + 32)
                            for s, name in enumerate(('L1_ffn_q_scale', 'L1_ffn_k_scale')):
                                sp.dma_start(r.qk_scale[rows, :, 2 * s + h],
                                             ins[name][:, 32 * h:32 * h + 32].rearrange("l d -> d l")).then_inc(sem.small_loaded, 16)
                    for i, name in enumerate(('L1_ffn_ln_g', 'L1_ffn_ln_b')):
                        sp.dma_start(r.ln_gb[:, :, i], ins[name].rearrange("l d -> d l")).then_inc(sem.small_loaded, 16)
                    sp.dma_start(r.b2[:, :], ins['L1_ffn_b2'].rearrange("l d -> d l")).then_inc(sem.small_loaded, 16)
                    sp.wait_ge(sem.b1_cleared, 1)
                    for h in range(2):
                        for m in range(3):
                            size = min(P, INNER2 - m * P)
                            f = h * INNER2 + m * P
                            sp.dma_start(r.b1[0:size, :, 3 * h + m], ins['L1_ffn_b1'][:, f:f + size].rearrange("l d -> d l")).then_inc(sem.small_loaded, 16)
                    sp.wait_ge(sem.small_loaded, 16 * (16 + 3 + 6))

                @block.vector
                def _(dve):
                    dve.memset(r.b1[:, :, :], 0.0).then_inc(sem.b1_cleared, 1)
                    dve.memset(r.y[:, 0:1], 0.0).then_inc(sem.cleared, 1)
                    dve.memset(r.ys[:, 0:PREV], 0.0)
                    dve.memset(r.zeros[:, :, :], 0.0)
                    dve.wait_ge(sem.cleared, 1)
                    dve.tensor_copy(r.ys[0:64, PREV:], r.y[0:64, 1:]).then_inc(sem.y_shifted, 1)
                    dve.tensor_copy(r.ys[64:128, PREV:], r.y[64:128, 0:T]).then_inc(sem.y_shifted, 1)

            layers(nc, r, sem, sb)

        with ExitStack() as own:
            out_sb = sb("out_sb", [P, TILES, P], within=own)
            with nc.Block() as block:

                @block.tensor
                def _(pe):
                    for t in range(TILES):
                        mm = pe.transpose(r.banks[t // 4][:, (t % 4) * P:(t % 4 + 1) * P], r.y[:, 1 + t * P:1 + (t + 1) * P], r.ident[:, :])
                        if t % 4 == 3:
                            mm.then_inc(sem.y_turned, 1)

                @block.vector
                def _(dve):
                    for q in range(4):
                        dve.wait_ge(sem.y_turned, q + 1)
                        dve.tensor_tensor(out_sb[:, 4 * q:4 * q + 4, :].rearrange("p t c -> p (t c)"),
                                          r.x[:, 4 * q:4 * q + 4, :].rearrange("p t c -> p (t c)"), r.banks[q][:, :], ALU.add
                                          ).then_inc(sem.out_summed, 1)

                @block.sync
                def _(sp):
                    to = out.rearrange("o (t p) c -> p (o t) c", p=P)
                    for q in range(4):
                        sp.wait_ge(sem.out_summed, q + 1)
                        sp.dma_start(to[:, 4 * q:4 * q + 4, :], out_sb[:, 4 * q:4 * q + 4, :]).then_inc(sem.out_stored, 16)
                    sp.wait_ge(sem.out_stored, 64)


LN_2_10 = 6.931471805599453


def layers(nc, r, sem, sb):
    r.work_ps = [r.banks[4], r.banks[5]]
    r.scores_ps = r.banks[0:4]
    r.pt_ps, r.out_ps = r.banks[6], r.banks[7]
    with nc.Fori(0, DEPTH) as L:
        with ExitStack() as a:
            r.w_stage = sb("w_stage", [P, 3, GW], within=a)
            r.w_qk = sb("w_qk", [P, 4, P], within=a)
            r.w_v = sb("w_v", [P, GW], within=a)
            r.tab_q = sb("tab_q", [P, 4, BT], within=a)
            r.tab_k = sb("tab_k", [P, 4, BT + PREV], within=a)
            r.raw_q = sb("raw_q", [P, 2, BT], within=a)
            r.raw_k = sb("raw_k", [P, 2, BT + PREV], within=a)
            r.squares = sb("squares", [P, 4, BT], within=a)
            r.inv_q = sb("inv_q", [P, BT], within=a)
            r.inv_k = sb("inv_k", [P, BT + PREV], within=a)
            r.prod_q = sb("prod_q", [P, 4, BT], within=a)
            r.prod_k = sb("prod_k", [P, 4, BT + PREV], within=a)
            r.rot_q = sb("rot_q", [P, 2, BT], within=a)
            r.rot_k = sb("rot_k", [P, 2, BT + PREV], within=a)
            r.q_pair = sb("q_pair", [P, 2, BT], within=a)
            r.k_pair = sb("k_pair", [P, 2, 2, BT + PREV], within=a)
            r.v_win = sb("v_win", [P, 2, 8, GW], within=a)
            r.probs = sb("probs", [P, 4, 4 * KC], within=a)
            r.turned_sb = sb("turned_sb", [P, 2, BT], within=a)
            r.row_max = sb("row_max", [P, 4, 4], within=a)
            r.neg_max = sb("neg_max", [P, 4, 4], within=a)
            r.sums = sb("sums", [P, 4, 4], within=a)
            r.inv_sums = sb("inv_sums", [P, 4, 4], within=a)
            windowed_attention(nc, L, r, sem)
        with ExitStack() as f:
            r.shifted = sb("shifted", [P, 2, BT], within=f)
            r.centred = sb("centred", [P, 2, BT], within=f)
            r.centred_sq = sb("centred_sq", [P, 2, BT], within=f)
            r.log_var = sb("log_var", [P, BT], within=f)
            r.inv_std = sb("inv_std", [P, BT], within=f)
            r.scaled = sb("scaled", [P, 2, BT], within=f)
            r.normed = sb("normed", [P, BLOCKS, BT], within=f)
            r.gate = sb("gate", [P, 3, BT], within=f)
            r.inner = sb("inner", [P, 2, 3, BT], within=f)
            output_and_ffn(nc, L, r, sem)


def constants():
    import numpy as np
    c = {}
    c["ident"] = np.eye(P)
    c["ones32"] = np.kron(np.eye(4), np.ones((32, 32)))
    c["ones_mean"] = np.full((P, P), 1.0 / P)
    q = np.arange(P)[:, None] % QC
    key = np.arange(KC)[None, :] - PREV
    allowed = (key <= q) & (q <= key + WINDOW)
    mask = np.where(allowed, 0.0, -1e30)
    later = np.tile(mask, (1, 4))
    first = later.copy()
    for head in range(2):
        first[:QC, head * KC:head * KC + PREV] = -1e30
    c["mask"] = np.concatenate([first, later], 1)
    tri = np.where(np.arange(P)[None, :] > np.arange(P)[:, None], -1e30, 0.0)
    c["causal"] = np.concatenate([tri, tri.T], 1)
    c["iota8"] = np.tile(np.arange(8.0), (P, 1))
    half = np.arange(0, DH, 2, dtype=np.float64)[:, None]
    pos = np.arange(-PREV, BT, dtype=np.float64)[None, :]
    angle = pos / 10000.0 ** (half / DH)
    scale = ((half + 0.4 * DH) / (1.4 * DH)) ** ((pos - BT // 2) / (WINDOW // 2))
    tabs = [np.cos(angle) * scale, np.sin(angle) * scale, np.cos(angle) / scale, np.sin(angle) / scale]
    c["base_tab"] = np.concatenate([np.tile(t, (4, 1)) for t in tabs], 1)
    return np.concatenate([c[n] for n, _ in CONSTS], 1).astype(np.float32)


def kernel(**inputs):
    import numpy as np
    import concourse.bacc as bacc
    from concourse.bass_utils import run_bass_kernel_spmd
    nc = bacc.Bacc("TRN2", target_bir_lowering=False, num_devices=1)
    arrays, aps = {}, {}
    for name in INPUTS:
        a = np.ascontiguousarray(inputs[name])
        arrays["in_" + name] = a
        aps[name] = nc.dram_tensor("in_" + name, a.shape, mybir.dt.from_np(a.dtype), kind="ExternalInput").ap()
    arrays["constants"] = constants()
    const = nc.dram_tensor("constants", arrays["constants"].shape, fp32, kind="ExternalInput").ap()
    out = nc.dram_tensor("out", (1, T, P), fp32, kind="ExternalOutput").ap()
    program(nc, aps, const, out)
    got = run_bass_kernel_spmd(nc, [arrays], core_ids=[0])
    return got.results[0]["out"]
```

```python
import concourse.bass as bass
import concourse.mybir as mybir
from contextlib import ExitStack

fp32, bf16, u32 = mybir.dt.float32, mybir.dt.bfloat16, mybir.dt.uint32
ACT = mybir.ActivationFunctionType
ALU = mybir.AluOpType
AX = mybir.AxisListType

P = 128
T = 2048
TILES = T // P
BT = 512
BLOCKS = T // BT
DEPTH = 6
HEADS, DH = 16, 64
INNER = HEADS * DH
GROUPS = 4
GW = 4 * DH
WINDOW = 32
PREV = WINDOW
QC = 64
KC = QC + PREV
QK_SCALE = 8.0
PRIMED = 1
INNER2 = int(P * 4 * 2 / 3)
EPS = 1e-5
PRODUCTS = ((0, 0), (0, 1), (1, 0), (0, 2), (2, 0), (1, 1))
KPROD = 8 * len(PRODUCTS)
MAX_ROW = 96

CONSTS = (("ident", P), ("ones32", P), ("ones_mean", P), ("mask", 2 * 4 * KC), ("causal", 2 * P), ("iota8", 8),
          ("base_tab", 4 * (BT + PREV)))

INPUTS = ('L0_attn_hidden_states', 'L0_attn_Wi', 'L0_attn_Wg', 'L0_attn_Wo', 'L0_attn_A_diag', 'L0_attn_B_param',
          'L0_attn_C_param', 'L0_attn_D', 'L0_attn_dt', 'L0_attn_norm_weight', 'L0_ffn_Wg', 'L0_ffn_bg', 'L0_ffn_We',
          'L0_ffn_be', 'L1_attn_W_qkv', 'L1_attn_b_qkv', 'L1_attn_W_o', 'L1_attn_b_o', 'L1_ffn_Wqkv', 'L1_ffn_q_scale',
          'L1_ffn_k_scale', 'L1_ffn_Wo', 'L1_ffn_ln_g', 'L1_ffn_ln_b', 'L1_ffn_W1', 'L1_ffn_b1', 'L1_ffn_W2', 'L1_ffn_b2')


class Record:
    pass


def normalise_and_transpose(nc, r, sem, k, to, to_first):
    with nc.Block() as block:

        @block.vector
        def _(dve):
            if k < 2:
                for t in range(TILES):
                    dve.bn_stats(r.stats[:, t, :], r.x[:, t, :]).then_inc(sem.stats, 1)
            dve.wait_ge(sem.stats, (k + 1) * TILES)
            for t in range(TILES):
                dve.bn_aggr(r.moments[:, t, :], r.stats[:, t, :]).then_inc(sem.aggregated, 1)
            dve.wait_ge(sem.std_ready, k + 1)
            dve.reciprocal(r.rstd[:, :], r.std[:, :]).then_inc(sem.rstd_ready, 1)
            dve.wait_ge(sem.rstd_ready, k + 1)
            for t in range(TILES):
                dve.tensor_scalar(r.x_norm[:, t, :], r.x[:, t, :], r.moments[:, t, 0:1], r.rstd[:, t:t + 1],
                                  ALU.subtract, ALU.mult).then_inc(sem.x_normed, 1)

        @block.scalar
        def _(act):
            act.wait_ge(sem.aggregated, (k + 1) * TILES)
            act.activation(r.std[:, :], r.moments[:, :, 1], ACT.Sqrt, bias=r.eps[:, 0:1]).then_inc(sem.std_ready, 1)
            for q in range(TILES // 4):
                act.wait_ge(sem.x_transposed, k * 4 + q + 1)
                act.copy(to[:, to_first + q * BT:to_first + (q + 1) * BT], r.banks[q][:, :]).then_inc(sem.x_copied, 1)

        @block.tensor
        def _(pe):
            for t in range(TILES):
                pe.wait_ge(sem.x_normed, k * TILES + t + 1)
                mm = pe.transpose(r.banks[t // 4][:, (t % 4) * P:(t % 4 + 1) * P], r.x_norm[:, t, :], r.ident[:, :])
                if t % 4 == 3:
                    mm.then_inc(sem.x_transposed, 1)


BIASES = ((0, 8 * P), (8 * P, P), (9 * P, P), (10 * P, P))
EXPERTS_BIAS, GATE_BIAS, V_BIAS, OUT_BIAS = BIASES


def bias(r, which, skip=0, n=P):
    return r.bias3[:, which[0] + skip:which[0] + skip + n]


def oscillators(nc, r, sem):
    CH, ST = r.CH, r.ST
    hT, xiT, bu, ys2 = r.hT, r.xiT, r.bu, r.y_osc
    banks = r.banks

    with nc.Block() as block:

        @block.sync
        def _(sp):
            for i, (dst, src) in enumerate(((r.wA[:, 0, :], r.d['L0_attn_Wi']), (r.wA[:, 1, :], r.d['L0_attn_Wg']),
                                            (r.wA[:, 2, :], r.d['L0_attn_Wo']),
                                            (r.bc_raw[:, 0, :], r.d['L0_attn_B_param'].rearrange("p h c -> p (h c)")),
                                            (r.bc_raw[:, 1, :], r.d['L0_attn_C_param'].rearrange("p h c -> p (h c)")))):
                sp.dma_start(dst, src).then_inc(sem.wA_loaded, 16)
            for i, name in enumerate(('L0_attn_A_diag', 'L0_attn_dt', 'L0_attn_D', 'L0_attn_norm_weight')):
                sp.dma_start(r.colsA[:, i:i + 1], r.d[name].rearrange("(p o) -> p o", o=1)).then_inc(sem.colsA_loaded, 16)
            for (first, n), src in zip(BIASES, (r.d['L0_ffn_be'].rearrange("(o e) f -> o (e f)", o=1),
                                                r.d['L0_ffn_bg'].rearrange("(o n) -> o n", o=1),
                                                r.d['L1_attn_b_qkv'][2 * P:3 * P].rearrange("(o n) -> o n", o=1),
                                                r.d['L1_attn_b_o'].rearrange("(o n) -> o n", o=1))):
                sp.dma_start(r.bias_raw[0:1, first:first + n], src).then_inc(sem.bias_loaded, 16)
            sp.dma_start(r.wgate[:, :], r.d['L0_ffn_Wg']).then_inc(sem.wB_loaded, 16)
            sp.dma_start(r.wexp[:, :, :], r.d['L0_ffn_We'].rearrange("e d f -> d e f")).then_inc(sem.wB_loaded, 16)
            sp.dma_start(r.wqkvC[:, :], r.d['L1_attn_W_qkv']).then_inc(sem.wC_loaded, 16)
            sp.dma_start(r.woC[:, :], r.d['L1_attn_W_o']).then_inc(sem.wC_loaded, 16)
            for i in range(2):
                sp.dma_start(r.cols_bqk[:, i:i + 1], r.d['L1_attn_b_qkv'][i * P:(i + 1) * P].rearrange("(p o) -> p o", o=1)).then_inc(sem.wC_loaded, 16)
            with nc.allow_non_contiguous_dma(reason="columns of parameters, a few thousand elements"):
                for h in range(2):
                    for a in range(4):
                        rows = slice(32 * a, 32 * a + 32)
                        for s, name in enumerate(('L1_ffn_q_scale', 'L1_ffn_k_scale')):
                            sp.dma_start(r.qk_scale[rows, 0:DEPTH, 2 * s + h],
                                     r.d[name][:, 32 * h:32 * h + 32].rearrange("l d -> d l")).then_inc(sem.small_loaded, 16)
                for i, name in enumerate(('L1_ffn_ln_g', 'L1_ffn_ln_b')):
                    sp.dma_start(r.ln_gb[:, :, i], r.d[name].rearrange("l d -> d l")).then_inc(sem.small_loaded, 16)
                sp.dma_start(r.b2[:, :], r.d['L1_ffn_b2'].rearrange("l d -> d l")).then_inc(sem.small_loaded, 16)
                sp.wait_ge(sem.b1_cleared, 1)
                for h in range(2):
                    for m in range(3):
                        size = min(P, INNER2 - m * P)
                        f = h * INNER2 + m * P
                        sp.dma_start(r.b1[0:size, :, 3 * h + m], r.d['L1_ffn_b1'][:, f:f + size].rearrange("l d -> d l")).then_inc(sem.small_loaded, 16)
            sp.wait_ge(sem.bias_cut, 5)
            for i in range(3):
                sp.dma_start(r.bias3[i:i + 1, :], r.bias_parts[0:1, i, :]).then_inc(sem.bias_placed, 16)
            sp.wait_ge(sem.bias_placed, 48)
            sp.wait_ge(sem.small_loaded, 16 * (16 + 3 + 6))

        @block.gpsimd
        def _(pool):
            pool.wait_ge(sem.coefs_ready, 6)
            k = 0
            for s in range(r.N_POW - 1):
                m = r.powers[:, s, :]
                nxt = r.powers[:, s + 1, :]
                pool.tensor_tensor(r.pw_tmp[:, 0:1], m[:, 2:3], m[:, 3:4], ALU.mult).then_inc(sem.powered, 1)
                pool.tensor_tensor(r.pw_tmp[:, 1:2], m[:, 0:1], m[:, 1:2], ALU.add).then_inc(sem.powered, 1)
                pool.tensor_tensor(r.pw_tmp[:, 2:4], m[:, 0:2], m[:, 0:2], ALU.mult).then_inc(sem.powered, 1)
                k += 3
                pool.wait_ge(sem.powered, k)
                pool.tensor_scalar(nxt[:, 0:2], r.pw_tmp[:, 2:4], r.pw_tmp[:, 0:1], None, ALU.add).then_inc(sem.powered, 1)
                pool.tensor_scalar(nxt[:, 2:4], m[:, 2:4], r.pw_tmp[:, 1:2], None, ALU.mult).then_inc(sem.powered, 1)
                k += 2
                pool.wait_ge(sem.powered, k)
            pool.wait_ge(sem.bias_loaded, 64)
            full, rest = r.bias_raw[0:1, :], r.bias_rest[0:1, :]
            hi, mid, lo = (r.bias_parts[0:1, i, :] for i in range(3))
            pool.tensor_copy(hi, full).then_inc(sem.bias_cut, 1)
            pool.wait_ge(sem.bias_cut, 1)
            pool.tensor_tensor(rest, full, hi, ALU.subtract).then_inc(sem.bias_cut, 1)
            pool.wait_ge(sem.bias_cut, 2)
            pool.tensor_copy(mid, rest).then_inc(sem.bias_cut, 1)
            pool.wait_ge(sem.bias_cut, 3)
            pool.tensor_tensor(lo, rest, mid, ALU.subtract).then_inc(sem.bias_cut, 2)
            pool.memset(r.v_aug[:, :, :, :], 0.0).then_inc(sem.v_cleared, 1)
            pool.wait_ge(sem.v_cleared, 1)
            pool.memset(r.v_aug[:, :, :, 8:9], 1.0).then_inc(sem.v_cleared, 1)
            pool.memset(r.part_max[:, :, :, :], -3e38).then_inc(sem.v_cleared, 1)
            pool.memset(r.ones3[:, :], 1.0).then_inc(sem.ones3_set, 1)
            pool.wait_ge(sem.ones3_set, 1)
            pool.dma_start(r.k_next[MAX_ROW:MAX_ROW + 3, :, :].rearrange("p a t -> p (a t)"), r.ones3[:, :]).then_inc(sem.ones_placed, 16)
            pool.memset(r.q_next[0:MAX_ROW, :, :], 0.0).then_inc(sem.rows_cleared, 1)
            pool.memset(r.k_next[0:MAX_ROW, :, :], 0.0).then_inc(sem.rows_cleared, 1)
            pool.wait_ge(sem.ones_placed, 16)

        @block.tensor
        def _(pe):
            pe.wait_ge(sem.wA_loaded, 80)
            for i in range(3):
                mm = pe.transpose(banks[4][:, i * P:(i + 1) * P], r.wA[:, i, :], r.ident[:, :])
            mm.then_inc(sem.wA_turned, 1)
            pe.wait_ge(sem.bc_split, 4)
            for i in range(4):
                mm = pe.transpose(banks[5][:, i * P:(i + 1) * P], r.bc[:, i, :], r.ident[:, :])
            mm.then_inc(sem.wA_turned, 1)
            pe.wait_ge(sem.wA_ready, 4)
            for b in range(BLOCKS):
                pe.matmul(banks[b][:, :], r.wAT[:, 0, :], hT[:, b * BT:(b + 1) * BT], start=True, stop=True
                          ).then_inc(sem.xi_made, 1)
            for c in range(2):
                for b in range(BLOCKS):
                    u = c * BLOCKS + b
                    bank = banks[6 + u % 2]
                    pe.wait_ge(sem.xi_copied, b + 1)
                    if u >= 2:
                        pe.wait_ge(sem.bu_copied, u - 1)
                    pe.matmul(bank[:, :], r.bcT[:, c, :], xiT[:, b * BT:(b + 1) * BT], start=True, stop=True
                              ).then_inc(sem.bu_made, 1)
            pe.wait_ge(sem.diag_ready, 1)
            for t in range(TILES + 2):
                if t < TILES:
                    tok = slice(t * P, (t + 1) * P)
                    if t == 0:
                        pe.wait_ge(sem.osc_kept, ST)
                    if t >= 4:
                        pe.wait_ge(sem.o_gated, t - 3)
                    bank = banks[t % 4]
                    pe.matmul(bank[:, 0:P], ys2[:, 0, tok], r.bcT[:, 2, :], start=True, stop=False)
                    pe.matmul(bank[:, 0:P], ys2[:, 1, tok], r.bcT[:, 3, :], start=False, stop=False)
                    pe.matmul(bank[:, 0:P], xiT[:, tok], r.diag_d[:, :], start=False, stop=True)
                    pe.matmul(bank[:, P:2 * P], hT[:, tok], r.wAT[:, 1, :], start=True, stop=True).then_inc(sem.og_made, 1)
                if 1 <= t <= TILES:
                    u = t - 1
                    pe.wait_ge(sem.o_gated, u + 1)
                    if u >= 2:
                        pe.wait_ge(sem.oT_copied, u - 1)
                    pe.transpose(banks[4 + u % 2][:, 0:P], r.gated[:, u % 2, :], r.ident[:, :]).then_inc(sem.o_turned, 1)
                if t >= 2:
                    u = t - 2
                    pe.wait_ge(sem.oT_copied, u + 1)
                    if u >= 2:
                        pe.wait_ge(sem.aT_added, u - 1)
                    pe.matmul(banks[6 + u % 2][:, 0:P], r.gatedT[:, u % 2, :], r.wAT[:, 2, :], start=True, stop=True
                              ).then_inc(sem.aout_made, 1)

        @block.scalar
        def _(act):
            act.wait_ge(sem.colsA_loaded, 64)
            act.activation(r.colt[:, 0:1], r.colsA[:, 1:2], ACT.Exp, scale=-1.0).then_inc(sem.dt_exp, 1)
            act.wait_ge(sem.wA_turned, 1)
            act.copy(r.wAT[:, 0:2, :].rearrange("p a n -> p (a n)"), banks[4][:, 0:2 * P]).then_inc(sem.wA_ready, 1)
            act.mul(r.wAT[:, 2, :], banks[4][:, 2 * P:3 * P], r.colsA[:, 3:4]).then_inc(sem.wA_ready, 1)
            act.wait_ge(sem.wA_turned, 2)
            act.copy(r.bcT[:, 0:3, :].rearrange("p a n -> p (a n)"), banks[5][:, 0:3 * P]).then_inc(sem.wA_ready, 1)
            act.mul(r.bcT[:, 3, :], banks[5][:, 3 * P:4 * P], -1.0).then_inc(sem.wA_ready, 1)
            for b in range(BLOCKS):
                act.wait_ge(sem.xi_made, b + 1)
                act.copy(xiT[:, b * BT:(b + 1) * BT], banks[b][:, :]).then_inc(sem.xi_copied, 1)
            act.wait_ge(sem.coefs_ready, 6)
            for u in range(2 * BLOCKS):
                act.wait_ge(sem.bu_made, u + 1)
                act.mul(bu[:, u // BLOCKS, (u % BLOCKS) * BT:(u % BLOCKS + 1) * BT], banks[6 + u % 2][:, :],
                        r.coef[:, 3:4]).then_inc(sem.bu_copied, 1)
            for t in range(TILES):
                act.wait_ge(sem.og_made, t + 1)
                act.activation(r.sq_junk[:, :], banks[t % 4][:, 0:P], ACT.Square, accum_out=r.o_ss[:, t:t + 1])
                if t >= 2:
                    act.wait_ge(sem.o_gated, t - 1)
                act.activation(r.sig[:, t % 2, :], banks[t % 4][:, P:2 * P], ACT.Sigmoid).then_inc(sem.sig_ready, 1)
                act.wait_ge(sem.o_turned, t + 1)
                if t >= 2:
                    act.wait_ge(sem.aout_made, t - 1)
                act.copy(r.gatedT[:, t % 2, :], banks[4 + t % 2][:, 0:P]).then_inc(sem.oT_copied, 1)

        @block.vector
        def _(dve):
            co, ca, ct = r.coef, r.colsA, r.colt
            dve.wait_ge(sem.dt_exp, 1)
            k = 0

            def link(ins):
                nonlocal k
                k += 1
                ins.then_inc(sem.colchain, 1)
                dve.wait_ge(sem.colchain, k)

            link(dve.tensor_scalar(ct[:, 1:2], ct[:, 0:1], 1.0, None, ALU.add))
            link(dve.reciprocal(co[:, 2:3], ct[:, 1:2]))
            link(dve.tensor_scalar(ct[:, 2:3], ca[:, 0:1], 0.0, co[:, 2:3], ALU.max, ALU.mult))
            link(dve.tensor_scalar(ct[:, 3:4], ct[:, 2:3], co[:, 2:3], 1.0, ALU.mult, ALU.add))
            link(dve.reciprocal(co[:, 0:1], ct[:, 3:4]))
            dve.tensor_scalar(co[:, 3:4], co[:, 0:1], co[:, 2:3], None, ALU.mult).then_inc(sem.coefs_ready, 1)
            dve.tensor_scalar(co[:, 1:2], ct[:, 2:3], co[:, 0:1], -1.0, ALU.mult, ALU.mult).then_inc(sem.coefs_ready, 1)
            dve.tensor_copy(r.powers[:, 0, 0:1], co[:, 0:1]).then_inc(sem.coefs_ready, 1)
            dve.tensor_copy(r.powers[:, 0, 1:2], co[:, 0:1]).then_inc(sem.coefs_ready, 1)
            dve.tensor_scalar(r.powers[:, 0, 2:3], ct[:, 2:3], co[:, 0:1], -1.0, ALU.mult, ALU.mult).then_inc(sem.coefs_ready, 1)
            dve.tensor_scalar(r.powers[:, 0, 3:4], co[:, 0:1], co[:, 2:3], None, ALU.mult).then_inc(sem.coefs_ready, 1)
            dve.tensor_scalar(r.diag_d[:, :], r.ident[:, :], ca[:, 2:3], None, ALU.mult).then_inc(sem.diag_ready, 1)
            dve.wait_ge(sem.wA_loaded, 80)
            for i in range(4):
                dve.tensor_copy(r.bc[:, i, :], r.bc_raw[:, i // 2, :].rearrange("p (h c) -> p h c", c=2)[:, :, i % 2]
                                ).then_inc(sem.bc_split, 1)

            steps = bu[:, :, :].rearrange("p c (n s) -> p c n s", s=ST)
            outs = ys2[:, :, :].rearrange("p c (n s) -> p c n s", s=ST)
            dve.memset(r.state[:, 0, :, :, :], 0.0).then_inc(sem.state_zeroed, 1)
            dve.wait_ge(sem.state_zeroed, 1)
            dve.wait_ge(sem.bu_copied, 2 * BLOCKS)

            def run(z, y, counter, keep):
                with dve.Fori(0, ST // 4) as j4:
                    for i in range(4):
                        done = j4 * 12 + (3 * i + PRIMED)
                        now = steps[:, :, :, bass.ds(j4 * 4 + i, 1)].rearrange("p c n s -> p c (n s)")
                        y_old = y
                        dve.wait_ge(counter, done)
                        dve.scalar_tensor_tensor(r.drive[:, :, :], y_old, co[:, 1:2], now, ALU.mult, ALU.add).then_inc(counter, 1)
                        dve.wait_ge(counter, done + 1)
                        dve.scalar_tensor_tensor(z, z, co[:, 0:1], r.drive[:, :, :], ALU.mult, ALU.add).then_inc(counter, 1)
                        dve.wait_ge(counter, done + 2)
                        dve.scalar_tensor_tensor(y, z, co[:, 2:3], y_old, ALU.mult, ALU.add).then_inc(counter, 1)
                        if keep:
                            dve.wait_ge(counter, done + 3)
                            dve.tensor_copy(outs[:, :, :, bass.ds(j4 * 4 + i, 1)].rearrange("p c n s -> p c (n s)"), y
                                            ).then_inc(sem.osc_kept, 1)

            run(r.state[:, 0, 0, :, :], r.state[:, 0, 1, :, :], sem.osc1, False)
            dve.wait_ge(sem.osc1, 3 * ST + PRIMED)
            dve.wait_ge(sem.powered, 5 * (r.N_POW - 1))
            k2 = 0
            cur = 0
            for s in range(r.LOG_CH):
                d = 1 << s
                g = r.powers[:, r.LOG_ST + s, :]
                src, dst = r.state[:, cur], r.state[:, 1 - cur]
                zs, ysrc = src[:, 0, :, 0:CH - d], src[:, 1, :, 0:CH - d]
                dve.tensor_copy(dst[:, :, :, 0:d], src[:, :, :, 0:d]).then_inc(sem.doubled, 1)
                dve.scalar_tensor_tensor(dst[:, 0, :, d:CH], zs, g[:, 0:1], src[:, 0, :, d:CH], ALU.mult, ALU.add).then_inc(sem.doubled, 1)
                dve.scalar_tensor_tensor(dst[:, 1, :, d:CH], zs, g[:, 3:4], src[:, 1, :, d:CH], ALU.mult, ALU.add).then_inc(sem.doubled, 1)
                k2 += 3
                dve.wait_ge(sem.doubled, k2)
                dve.scalar_tensor_tensor(dst[:, 0, :, d:CH], ysrc, g[:, 2:3], dst[:, 0, :, d:CH], ALU.mult, ALU.add).then_inc(sem.doubled, 1)
                dve.scalar_tensor_tensor(dst[:, 1, :, d:CH], ysrc, g[:, 1:2], dst[:, 1, :, d:CH], ALU.mult, ALU.add).then_inc(sem.doubled, 1)
                k2 += 2
                dve.wait_ge(sem.doubled, k2)
                cur = 1 - cur
            src, dst = r.state[:, cur], r.state[:, 1 - cur]
            dve.memset(dst[:, :, :, 0:1], 0.0).then_inc(sem.doubled, 1)
            dve.tensor_copy(dst[:, 0, :, 1:CH], src[:, 0, :, 0:CH - 1]).then_inc(sem.doubled, 1)
            dve.tensor_copy(dst[:, 1, :, 1:CH], src[:, 1, :, 0:CH - 1]).then_inc(sem.doubled, 1)
            dve.wait_ge(sem.doubled, k2 + 3)
            run(dst[:, 0], dst[:, 1], sem.osc2, True)

            for t in range(TILES + 2):
                if t < TILES:
                    dve.wait_ge(sem.sig_ready, t + 1)
                    if t >= 2:
                        dve.wait_ge(sem.o_turned, t - 1)
                    dve.tensor_tensor(r.silu[:, :], banks[t % 4][:, P:2 * P], r.sig[:, t % 2, :], ALU.mult).then_inc(sem.silu_ready, 1)
                    dve.wait_ge(sem.silu_ready, t + 1)
                    dve.tensor_tensor(r.gated[:, t % 2, :], banks[t % 4][:, 0:P], r.silu[:, :], ALU.mult).then_inc(sem.o_gated, 1)
                if t >= 2:
                    u = t - 2
                    dve.wait_ge(sem.aout_made, u + 1)
                    dve.tensor_copy(r.a_out[:, u, :], banks[6 + u % 2][:, 0:P]).then_inc(sem.aT_added, 1)

    with nc.Block() as block:
        @block.scalar
        def _(act):
            act.activation(r.std[:, :], r.o_ss[:, :], ACT.Sqrt, bias=r.eps[:, 0:1], scale=1.0 / P).then_inc(sem.o_std, 1)

        @block.vector
        def _(dve):
            dve.wait_ge(sem.o_std, 1)
            dve.reciprocal(r.rstd[:, :], r.std[:, :]).then_inc(sem.o_rstd, 1)
            dve.wait_ge(sem.o_rstd, 1)
            for t in range(TILES):
                dve.scalar_tensor_tensor(r.x[:, t, :], r.a_out[:, t, :], r.rstd[:, t:t + 1], r.x[:, t, :], ALU.mult, ALU.add)


def experts(nc, r, sem):
    hT, banks = r.hT, r.banks
    with nc.Block() as block:

        @block.tensor
        def _(pe):
            pe.wait_ge(sem.wB_loaded, 32)
            for t in range(TILES):
                tok = slice(t * P, (t + 1) * P)
                if t >= 2:
                    pe.wait_ge(sem.router_exp, t - 1)
                bank = banks[t % 2]
                pe.matmul(bank[:, 0:P], hT[:, tok], r.wgate[:, :], start=True, stop=False)
                pe.matmul(bank[:, 0:P], r.ones3b[:, :], bias(r, GATE_BIAS), start=False, stop=True).then_inc(sem.routed, 1)
                if t >= 2:
                    pe.wait_ge(sem.experts_scaled, t - 1)
                for h in range(2):
                    bank = banks[2 + 2 * (t % 2) + h]
                    pe.matmul(bank[:, :], hT[:, tok], r.wexp[:, 4 * h:4 * h + 4, :].rearrange("p e f -> p (e f)"), start=True, stop=False)
                    mm = pe.matmul(bank[:, :], r.ones3b[:, :], bias(r, EXPERTS_BIAS, h * BT, BT), start=False, stop=True)
                mm.then_inc(sem.experts_made, 1)

        @block.vector
        def _(dve):
            def take_statistics(t):
                dve.wait_ge(sem.moe_added, t + 1)
                dve.bn_stats(r.stats[:, t, :], r.x[:, t, :]).then_inc(sem.stats, 1)

            for t in range(TILES + 1):
                if t < TILES:
                    p = t % 2
                    dve.wait_ge(sem.routed, t + 1)
                    dve.max(r.top8[:, p, :], banks[p][:, 0:P]).then_inc(sem.top_found, 1)
                    dve.wait_ge(sem.top_found, t + 1)
                    if t >= 2:
                        dve.wait_ge(sem.router_exp, t - 1)
                    dve.tensor_scalar(r.top_neg[:, p, :], r.top8[:, p, 0:1], -1.0, None, ALU.mult).then_inc(sem.top_neg, 1)
                    dve.max_index(r.top_at[:, p, :], r.top8[:, p, :], banks[p][:, 0:P]).then_inc(sem.index_found, 1)
                    dve.wait_ge(sem.index_found, t + 1)
                    dve.tensor_scalar(r.expert_u[:, p, :], r.top_at[:, p, 0:1], r.N_EXP - 1, None, ALU.bitwise_and).then_inc(sem.expert_found, 1)
                    dve.wait_ge(sem.expert_found, t + 1)
                    dve.tensor_copy(r.expert_f[:, p, :], r.expert_u[:, p, :]).then_inc(sem.expert_cast, 1)
                    dve.wait_ge(sem.router_exp, t + 1)
                    dve.reciprocal(r.top_p[:, p, :], r.router_sum[:, p, :]).then_inc(sem.prob_ready, 1)
                    dve.wait_ge(sem.expert_cast, t + 1)
                    dve.wait_ge(sem.prob_ready, t + 1)
                    if t >= 2:
                        dve.wait_ge(sem.experts_scaled, t - 1)
                    dve.tensor_scalar(r.select[:, p, :], r.iota8[:, :], r.expert_f[:, p, :], r.top_p[:, p, :], ALU.is_equal, ALU.mult
                                      ).then_inc(sem.selected, 1)
                if t >= 1:
                    u = t - 1
                    dve.wait_ge(sem.experts_scaled, u + 1)
                    dve.tensor_reduce(r.moe[:, u % 2, :], r.scaled_exp[:, u % 2, :, :].rearrange("p e f -> p f e"), AX.X, ALU.add
                                      ).then_inc(sem.experts_summed, 1)
                    dve.wait_ge(sem.experts_summed, u + 1)
                    dve.tensor_tensor(r.x[:, u, :], r.x[:, u, :], r.moe[:, u % 2, :], ALU.add).then_inc(sem.moe_added, 1)
                    if u >= 1:
                        take_statistics(u - 1)
            take_statistics(TILES - 1)

        @block.scalar
        def _(act):
            for t in range(TILES):
                p = t % 2
                act.wait_ge(sem.index_found, t + 1)
                act.wait_ge(sem.top_neg, t + 1)
                if t >= 2:
                    act.wait_ge(sem.prob_ready, t - 1)
                act.activation(r.junk[:, :], banks[p][:, 0:P], ACT.Exp, bias=r.top_neg[:, p, :], accum_out=r.router_sum[:, p, :]
                               ).then_inc(sem.router_exp, 1)
                act.wait_ge(sem.selected, t + 1)
                act.wait_ge(sem.experts_made, t + 1)
                if t >= 2:
                    act.wait_ge(sem.experts_summed, t - 1)
                for e in range(r.N_EXP):
                    a = act.activation(r.scaled_exp[:, p, e, :], banks[2 + 2 * p + e // 4][:, (e % 4) * P:(e % 4 + 1) * P], ACT.Relu,
                                       scale=r.select[:, p, e:e + 1])
                a.then_inc(sem.experts_scaled, 1)


def causal_projections(nc, r, sem):
    hT, banks = r.hT, r.banks
    with nc.Block() as block:

        @block.sync
        def _(sp):
            for part in range(3):
                for s in range(2):
                    if part < 2:
                        sp.wait_ge(sem.parts_cast, 2 * part + s + 1)
                    else:
                        sp.wait_ge(sem.parts_subtracted, s + 3)
                    for i, pair in enumerate(PRODUCTS):
                        if pair[s] == part:
                            sp.dma_start(r.d_stack[s, :, i], r.parts[:, s, part, :]).then_inc(sem.stacked, 16)
            sp.wait_ge(sem.stacked, 2 * len(PRODUCTS) * 16)

        @block.tensor
        def _(pe):
            pe.wait_ge(sem.wC_loaded, 64)
            for s in range(2):
                for b in range(BLOCKS):
                    pe.matmul(banks[4 * s + b][:, :], r.wqkvC[:, s * P:(s + 1) * P], hT[:, b * BT:(b + 1) * BT], start=True, stop=True
                              ).then_inc(sem.qkC_made, 1)
            for t in range(TILES):
                if t % 4 == 0:
                    pe.wait_ge(sem.qkC_read, t // 4 + 1)
                bank = banks[t // 4]
                pe.matmul(bank[:, (t % 4) * P:(t % 4 + 1) * P], hT[:, t * P:(t + 1) * P], r.wqkvC[:, 2 * P:3 * P], start=True, stop=False)
                mm = pe.matmul(bank[:, (t % 4) * P:(t % 4 + 1) * P], r.ones3b[:, :], bias(r, V_BIAS), start=False, stop=True)
                if t % 4 == 3:
                    mm.then_inc(sem.vC_made, 1)

        @block.vector
        def _(dve):
            dve.wait_ge(sem.wC_loaded, 64)
            for b in range(BLOCKS):
                dve.wait_ge(sem.qkC_made, b + 1)
                dve.tensor_scalar(r.qkf[:, 0, b * BT:(b + 1) * BT], banks[b][:, :], r.cols_bqk[:, 0:1],
                                  8 ** -0.5, ALU.add, ALU.mult).then_inc(sem.qkC_read, 1)
            for s in range(2):
                dve.wait_ge(sem.parts_cast, s + 1)
                dve.tensor_tensor(r.rest[:, s, :], r.qkf[:, s, :], r.parts[:, s, 0, :], ALU.subtract).then_inc(sem.parts_subtracted, 1)
            for s in range(2):
                dve.wait_ge(sem.parts_cast, s + 3)
                dve.tensor_tensor(r.parts[:, s, 2, :], r.rest[:, s, :], r.parts[:, s, 1, :], ALU.subtract).then_inc(sem.parts_subtracted, 1)

        @block.scalar
        def _(act):
            act.wait_ge(sem.qkC_read, BLOCKS)
            act.copy(r.parts[:, 0, 0, :], r.qkf[:, 0, :]).then_inc(sem.parts_cast, 1)
            for b in range(BLOCKS):
                act.wait_ge(sem.qkC_made, BLOCKS + b + 1)
                act.activation(r.qkf[:, 1, b * BT:(b + 1) * BT], banks[4 + b][:, :], ACT.Identity, bias=r.cols_bqk[:, 1:2]
                               ).then_inc(sem.kC_read, 1)
            act.wait_ge(sem.kC_read, BLOCKS)
            act.copy(r.parts[:, 1, 0, :], r.qkf[:, 1, :]).then_inc(sem.parts_cast, 1)
            for s in range(2):
                act.wait_ge(sem.parts_subtracted, s + 1)
                act.copy(r.parts[:, s, 1, :], r.rest[:, s, :]).then_inc(sem.parts_cast, 1)
            act.wait_ge(sem.v_cleared, 2)
            for q in range(4):
                act.wait_ge(sem.vC_made, q + 1)
                for j in range(4):
                    act.copy(r.v_aug[:, 4 * q + j, :, 0:8], banks[q][:, j * P:(j + 1) * P].rearrange("p (h d) -> p h d", d=8)
                             ).then_inc(sem.vC_copied, 1)


def causal_attention(nc, r, sem):
    banks = r.banks
    maxb = (banks[5], banks[6])
    misc, acc = banks[7], banks[4]
    NH = 4
    MAXES = [(a, qt, kb) for qt in range(TILES) for a in range(NH) for kb in range(qt // 4 + 1)]
    STEPS = [(b, kt, pair) for b in range(BLOCKS) for kt in range(4 * b + 4) for pair in range(2)]
    NM, NSTEP = len(MAXES), len(STEPS)
    NTILE = NSTEP // 2

    def maxima_by(i):
        return min(NM, max(0, i - 5) * 5 // 2)

    LAST_MAXIMA = min(i for i in range(NSTEP) if maxima_by(i) == NM)

    def at(n, per_group, k):
        return n * per_group + (k + PRIMED)

    def max_bank(m, i):
        turns = [*maxb, *banks[0:4]] if isinstance(m, int) and m == 0 else maxb
        return len(turns), turns[i % len(turns)]

    def first_query(b, kt):
        return max(0, kt - 4 * b) * P

    with nc.Block() as block:

        @block.sync
        def _(sp):
            def load(m):
                heads = bass.ds(m * NH, NH)
                for s, to in ((0, r.q_next), (1, r.k_next)):
                    sp.dma_start(to[0:KPROD, :, :], r.d_stack[s, heads].rearrange("h i d t -> (i d) h t")).then_inc(sem.stack_loaded, 16)

            def place_maxima(m):
                sp.wait_ge(sem.max_split, at(m, 4, 4))
                for i in range(3):
                    sp.dma_start(r.q_next[MAX_ROW + i:MAX_ROW + i + 1, :, :].rearrange("p a (q t) -> p (a q) t", t=P),
                                 r.max_parts[:, i, :]).then_inc(sem.max_placed, 16)

            sp.wait_ge(sem.rows_cleared, 2)
            load(0)
            place_maxima(0)
            with sp.Fori(0, GROUPS - 1) as n:
                sp.wait_ge(sem.taken, at(n, 2, 2))
                load(n + 1)
                place_maxima(n + 1)

        @block.tensor
        def _(pe):
            def maxima(m, i):
                a, qt, kb = MAXES[i]
                keys = min(BT, (qt + 1) * P - kb * BT)
                deep, bank = max_bank(m, i)
                if i < deep:
                    pe.wait_ge(sem.part_max_done, at(m, NM, 0))
                else:
                    pe.wait_ge(sem.part_max_done, at(m, NM, i - deep + 1))
                diag = kb == qt // 4
                mm = pe.matmul(bank[:, 0:keys], r.q_next[0:MAX_ROW, a, qt * P:(qt + 1) * P], r.k_next[0:MAX_ROW, a, kb * BT:kb * BT + keys],
                               start=True, stop=not diag, skip_group_check=True)
                if diag:
                    mm = pe.matmul(bank[:, keys - P:keys], r.ident_bf[:, :], r.causal_bf[:, 0, :], start=False, stop=True, skip_group_check=True)
                mm.then_inc(sem.max_scored, 1)

            def turn_maxima(m, outputs):
                pe.wait_ge(sem.max_ready_c, at(m, 1, 1))
                pe.wait_ge(sem.outputs_taken, outputs)
                pe.wait_ge(sem.max_split, at(m, 4, 0))
                pe.transpose(misc[:, 0:P], r.neg_max_c[:, :], r.ident[:, :]).then_inc(sem.max_turned, 1)

            def weights(n, i, h):
                b, kt, pair = STEPS[i]
                q0 = first_query(b, kt)
                if h == 0 and i < 2:
                    pe.wait_ge(sem.exp_done, at(n, NSTEP, 0))
                elif h == 0:
                    pe.wait_ge(sem.exp_done, at(n, NSTEP, i - 1))
                a = 2 * pair + h
                bank = banks[2 * (i % 2) + h]
                diag = kt >= 4 * b
                mm = pe.matmul(bank[:, q0:BT], r.k_now[:, a, kt * P:(kt + 1) * P], r.q_now[:, a, b * BT + q0:(b + 1) * BT],
                               start=True, stop=not diag, skip_group_check=True)
                if diag:
                    mm = pe.matmul(bank[:, q0:q0 + P], r.ident_bf[:, :], r.causal_bf[:, 1, :], start=False, stop=True, skip_group_check=True)
                if h == 1:
                    mm.then_inc(sem.weights_scored, 1)

            def values(n, j):
                b, kt, _ = STEPS[2 * j]
                q0 = first_query(b, kt)
                pe.wait_ge(sem.exp_done, at(n, NSTEP, 2 * j + 2))
                if kt == 0:
                    pe.wait_ge(sem.acc_copied, at(n, BLOCKS, b))
                for a in range(NH):
                    mm = pe.matmul(acc[32 * a:32 * a + 32, q0:BT], r.v_now[:, kt, a, :],
                                   r.weights[:, (2 * j + a // 2) % 4, a % 2, q0:BT],
                                   start=kt == 0, stop=kt == 4 * b + 3, skip_group_check=True)
                mm.then_inc(sem.valued, 1)

            def turn_outputs(n, b, more):
                if b == BLOCKS - 1 and more:
                    pe.wait_ge(sem.max_split, at(n + 1, 4, 1))
                pe.wait_ge(sem.acc_copied, at(n, BLOCKS, b + 1))
                pe.wait_ge(sem.outputs_taken, at(n, BLOCKS, b))
                for j in range(4):
                    mm = pe.transpose(misc[:, j * P:(j + 1) * P], r.acc_sb[:, j * P:(j + 1) * P], r.ident[:, :])
                mm.then_inc(sem.outputs_turned, 1)

            pe.wait_ge(sem.rows_cleared, 2)
            pe.wait_ge(sem.stack_loaded, 32 + PRIMED)
            for i in range(NM):
                maxima(0, i)
            turn_maxima(0, PRIMED)

            def body(n, more):
                pe.wait_ge(sem.taken, at(n, 2, 2))
                pe.wait_ge(sem.v_taken, at(n, 1, 1))
                mi = 0

                def next_maxima(last):
                    nonlocal mi
                    while more and mi < last:
                        if mi == 0:
                            pe.wait_ge(sem.stack_loaded, at(n, 32, 64))
                        maxima(n + 1, mi)
                        mi += 1

                for i in range(NSTEP + 2):
                    for h in range(2):
                        next_maxima(min(maxima_by(i - 1) + h + 1, maxima_by(i)))
                        if i < NSTEP:
                            weights(n, i, h)
                    next_maxima(maxima_by(i))
                    if i >= 3 and i % 2 == 1:
                        values(n, (i - 3) // 2)
                        b, kt, _ = STEPS[i - 3]
                        if b >= 1 and kt == 0:
                            turn_outputs(n, b - 1, more)
                    if more and i == LAST_MAXIMA + 3:
                        turn_maxima(n + 1, at(n, BLOCKS, BLOCKS - 1))
                turn_outputs(n, BLOCKS - 1, more)

            with pe.Fori(0, GROUPS - 1) as n:
                body(n, True)
            body(GROUPS - 1, False)

        @block.scalar
        def _(act):
            def body(n):
                for i, (b, kt, pair) in enumerate(STEPS):
                    q0 = first_query(b, kt)
                    act.wait_ge(sem.weights_scored, at(n, NSTEP, i + 1))
                    if i >= 4:
                        act.wait_ge(sem.valued, at(n, NTILE, i // 2 - 1))
                    else:
                        act.wait_ge(sem.valued, at(n, NTILE, 0))
                    act.activation(r.weights[:, i % 4, :, q0:BT], r.pairs[i % 2][:, :, q0:BT], ACT.Exp).then_inc(sem.exp_done, 1)
            with act.Fori(0, GROUPS) as n:
                body(n)

        @block.vector
        def _(dve):
            def part_maxima(m, i):
                a, qt, kb = MAXES[i]
                keys = min(BT, (qt + 1) * P - kb * BT)
                dve.wait_ge(sem.max_scored, at(m, NM, i + 1))
                dve.tensor_reduce(r.part_max[:, a, qt, kb:kb + 1], max_bank(m, i)[1][:, 0:keys], AX.X, ALU.max).then_inc(sem.part_max_done, 1)

            def finish_maxima(m):
                dve.wait_ge(sem.part_max_done, at(m, NM, NM))
                dve.tensor_reduce(r.max_c[:, :], r.part_max[:, :, :, :].rearrange("p a q k -> p (a q) k"), AX.X, ALU.max
                                  ).then_inc(sem.max_reduced, 1)
                dve.wait_ge(sem.max_reduced, at(m, 1, 1))
                dve.tensor_scalar(r.neg_max_c[:, 0:NH * TILES], r.max_c[:, :], -1.0, None, ALU.mult).then_inc(sem.max_ready_c, 1)
                dve.wait_ge(sem.max_turned, at(m, 1, 1))
                dve.wait_ge(sem.max_placed, at(m, 48, 0))
                full, rest = r.max_rows[:, 0, :], r.max_rows[:, 1, :]
                dve.tensor_copy(full, misc[0:NH * TILES, 0:P]).then_inc(sem.max_split, 1)
                dve.wait_ge(sem.max_split, at(m, 4, 1))
                dve.tensor_copy(r.max_parts[:, 0, :], full).then_inc(sem.max_cut, 1)
                dve.wait_ge(sem.max_cut, at(m, 2, 1))
                dve.tensor_tensor(rest, full, r.max_parts[:, 0, :], ALU.subtract).then_inc(sem.max_split, 1)
                dve.wait_ge(sem.max_split, at(m, 4, 2))
                dve.tensor_copy(r.max_parts[:, 1, :], rest).then_inc(sem.max_cut, 1)
                dve.wait_ge(sem.max_cut, at(m, 2, 2))
                dve.tensor_tensor(r.max_parts[:, 2, :], rest, r.max_parts[:, 1, :], ALU.subtract).then_inc(sem.max_split, 2)

            def take(n):
                dve.wait_ge(sem.max_placed, at(n, 48, 48))
                dve.wait_ge(sem.valued, at(n, NTILE, 0))
                dve.tensor_copy(r.q_now[:, :, :], r.q_next[:, :, :]).then_inc(sem.taken, 1)
                dve.tensor_copy(r.k_now[:, :, :], r.k_next[:, :, :]).then_inc(sem.taken, 1)
                dve.tensor_copy(r.v_now[:, :, :, :], r.v_aug[:, :, bass.ds(n * NH, NH), :]).then_inc(sem.v_taken, 1)

            def copy_sums(n, b):
                dve.wait_ge(sem.valued, at(n, NTILE, 2 * (b + 1) * (b + 2)))
                dve.wait_ge(sem.outputs_turned, at(n, BLOCKS, b))
                dve.tensor_copy(r.acc_sb[:, :], acc[:, :]).then_inc(sem.acc_copied, 1)

            def take_outputs(n, b):
                dve.wait_ge(sem.outputs_turned, at(n, BLOCKS, b + 1))
                v = misc[:, :].rearrange("p (j a c) -> p j a c", j=4, a=NH)
                dve.reciprocal(r.inv_den[:, :, :], v[:, :, :, 8]).then_inc(sem.den_inverted, 1)
                dve.wait_ge(sem.den_inverted, at(n, BLOCKS, b + 1))
                for j in range(4):
                    o = dve.tensor_tensor(r.attn_tok[:, 4 * b + j, bass.ds(n * 4 * 8, 32)].rearrange("p (a d) -> p a d", d=8),
                                          v[:, j, :, 0:8], r.inv_den[:, j, :].unsqueeze(2).to_broadcast([P, NH, 8]), ALU.mult)
                o.then_inc(sem.outputs_taken, 1)

            dve.wait_ge(sem.v_cleared, 3)
            dve.memset(r.neg_max_c[:, NH * TILES:P], 0.0)
            for i in range(NM):
                part_maxima(0, i)
            finish_maxima(0)

            def body(n, more):
                take(n)
                mi = 0
                for i in range(NSTEP + 2):
                    if more:
                        while mi < maxima_by(i):
                            part_maxima(n + 1, mi)
                            mi += 1
                        if i == LAST_MAXIMA + 1:
                            finish_maxima(n + 1)
                    if i >= 2:
                        b, kt, pair = STEPS[i - 2]
                        if kt == 4 * b + 3 and pair == 1:
                            copy_sums(n, b)
                        if b >= 1 and kt == 1 and pair == 0:
                            take_outputs(n, b - 1)
                take_outputs(n, BLOCKS - 1)

            with dve.Fori(0, GROUPS - 1) as n:
                body(n, True)
            body(GROUPS - 1, False)


def causal_output(nc, r, sem):
    banks = r.banks
    with nc.Block() as block:

        @block.tensor
        def _(pe):
            for t in range(TILES + 1):
                if t < TILES:
                    if t >= 2:
                        pe.wait_ge(sem.aC_copied, t - 1)
                    pe.transpose(banks[t % 2][:, 0:P], r.attn_tok[:, t, :], r.ident[:, :]).then_inc(sem.aC_turned, 1)
                if t >= 1:
                    u = t - 1
                    pe.wait_ge(sem.aC_copied, u + 1)
                    if u >= 2:
                        pe.wait_ge(sem.c_added, u - 1)
                    pe.matmul(banks[2 + u % 2][:, 0:P], r.aC_T[:, u % 2, :], r.woC[:, :], start=True, stop=False)
                    pe.matmul(banks[2 + u % 2][:, 0:P], r.ones3b[:, :], bias(r, OUT_BIAS), start=False, stop=True).then_inc(sem.c_out, 1)

        @block.scalar
        def _(act):
            for t in range(TILES):
                act.wait_ge(sem.aC_turned, t + 1)
                if t >= 2:
                    act.wait_ge(sem.c_out, t - 1)
                act.copy(r.aC_T[:, t % 2, :], banks[t % 2][:, 0:P]).then_inc(sem.aC_copied, 1)

        @block.vector
        def _(dve):
            def take_statistics(t):
                dve.wait_ge(sem.c_added, t + 1)
                dve.bn_stats(r.stats[:, t, :], r.x[:, t, :]).then_inc(sem.stats, 1)

            for t in range(TILES):
                dve.wait_ge(sem.c_out, t + 1)
                dve.tensor_tensor(r.x[:, t, :], r.x[:, t, :], banks[2 + t % 2][:, 0:P], ALU.add).then_inc(sem.c_added, 1)
                if t >= 1:
                    take_statistics(t - 1)
            take_statistics(TILES - 1)
def load_tables(sp, r, sem):
    base = r.d_tab.rearrange("p (a n) -> p a n", a=4)
    for twice in range(2):
        sp.dma_start(r.tab_q[:, 2 * twice:2 * twice + 2, :], base[:, 0:2, PREV:]).then_inc(sem.tables_loaded, 16)
        sp.dma_start(r.tab_k[:, 2 * twice:2 * twice + 2, :], base[:, 2:4, :]).then_inc(sem.tables_loaded, 16)


def windowed_attention(nc, L, r, sem):
    ys, raw_q, raw_k, squares = r.ys, r.raw_q, r.raw_k, r.squares
    work, scores, pt_ps, out_ps = r.work_ps, r.scores_ps, r.pt_ps, r.out_ps

    def at(n, per_block, b, k):
        return n * (BLOCKS * per_block) + (b * per_block + k + PRIMED)

    def squares_at(g, b, k):
        return L * (GROUPS * BLOCKS * 2 - 2) + (g * (BLOCKS * 2) + (2 * b + k - 2 + PRIMED))

    PLACED = 16 * 12

    def exists(c, last):
        return c < BLOCKS or not last

    def run(engine, heads):
        first_blocks, _ = heads(L * GROUPS, 0, False)
        first_blocks()
        with engine.Fori(0, GROUPS - 1) as g:
            _, step = heads(L * GROUPS + g, g, False)
            for b in range(BLOCKS):
                step(b)
        _, step = heads(L * GROUPS + (GROUPS - 1), GROUPS - 1, True)
        for b in range(BLOCKS):
            step(b)

    def place_heads(sp, n, b):
        for half in range(2):
            sp.wait_ge(sem.rotated, at(n, 4, b, half + 1))
            for a in range(4):
                to = 64 * half + 32 * (a % 2)
                sp.dma_start(r.k_pair[to:to + 32, a // 2, a % 2, :], r.rot_k[32 * a:32 * a + 32, half, :]
                             ).then_inc(sem.placed, 16)
        for half in range(2):
            sp.wait_ge(sem.rotated, at(n, 4, b, half + 3))
            for hp in range(2):
                sp.dma_start(r.q_pair[64 * half:64 * half + 64, hp, :], r.rot_q[64 * hp:64 * hp + 64, half, :]
                             ).then_inc(sem.placed, 16)

    with nc.Block() as block:

        @block.sync
        def _(sp):
            lay = bass.ds(L, 1)

            def load_weights(n, g):
                sp.wait_ge(sem.weights_copied, n * 3 + PRIMED)
                for s in range(3):
                    sp.dma_start(r.w_stage[:, s, :],
                                 r.d_wqkv[lay, :, bass.ds(g * GW + s * INNER, GW)].rearrange("l p n -> p (l n)")
                                 ).then_inc(sem.weights_loaded, 16)

            load_weights(L * GROUPS, 0)
            sp.dma_start(r.wo[:, :, :], r.d_wo[lay].rearrange("l (c p) n -> p (l c) n", p=P)).then_inc(sem.ffn_loaded, 16)
            sp.dma_start(r.w1[:, :], r.d_w1[lay].rearrange("l p n -> p (l n)")).then_inc(sem.ffn_loaded, 16)
            sp.dma_start(r.w2[:, 0:2, :], r.d_w2[lay, 0:2 * P].rearrange("l (c p) n -> p (l c) n", p=P)).then_inc(sem.ffn_loaded, 16)
            sp.dma_start(r.w2[0:INNER2 - 2 * P, 2, :], r.d_w2[lay, 2 * P:INNER2].rearrange("l p n -> p (l n)")).then_inc(sem.ffn_loaded, 16)
            place_heads(sp, L * GROUPS, 0)
            with sp.Fori(0, GROUPS - 1) as g:
                n = L * GROUPS + g
                load_weights(n + 1, g + 1)
                for b in range(BLOCKS):
                    place_heads(sp, n, b + 1)
            for b in range(BLOCKS - 1):
                place_heads(sp, L * GROUPS + (GROUPS - 1), b + 1)

        @block.tensor
        def _(pe):
            def heads(n, g, last):
                def project(c, u):
                    tokens = slice(PREV + c % BLOCKS * BT, PREV + (c % BLOCKS + 1) * BT)
                    if c % BLOCKS == 0 and u == 0:
                        pe.wait_ge(sem.weights_copied, (n + c // BLOCKS) * 3 + (2 + PRIMED))
                    if u < 2:
                        pe.wait_ge(sem.norm_read, at(n, 2, c, 0))
                    else:
                        pe.wait_ge(sem.qk_read, at(n, 4, c, u - 1))
                    pe.matmul(work[u % 2][:, :], r.w_qk[:, u, :], ys[:, tokens],
                              start=True, stop=True).then_inc(sem.qk_made, 1)

                def project_v(c, v):
                    if c % BLOCKS == 0 and v == 0:
                        pe.wait_ge(sem.weights_copied, (n + c // BLOCKS) * 3 + (3 + PRIMED))
                    if v >= 2:
                        pe.wait_ge(sem.v_read, at(n, 4, c, v - 1))
                    elif last and c == BLOCKS - 1:
                        pe.wait_ge(sem.norm_read, at(n, 2, c, 2))
                    else:
                        pe.wait_ge(sem.qk_read, at(n, 4, c + 1, v + 3))
                    for half in range(2):
                        chunk = 2 * v + half
                        first = c % BLOCKS * BT + chunk * QC
                        mm = pe.matmul(work[v % 2][0:KC, half * GW:(half + 1) * GW], ys[:, first:first + KC], r.w_v[:, :],
                                       start=True, stop=True)
                    mm.then_inc(sem.v_made, 1)

                def norms(b):
                    for s in range(2):
                        if b == 0:
                            pe.wait_ge(sem.qk_read, at(n, 4, b, s + 3))
                        else:
                            pe.wait_ge(sem.v_read, at(n, 4, b - 1, s + 3))
                        if b == 0:
                            pe.wait_ge(sem.squared, at(n, 4, b, 2 * s + 2))
                            pe.matmul(work[s][:, :], r.ones32[:, :], squares[:, 2 * s + 1, :], start=True, stop=False)
                        else:
                            pe.wait_ge(sem.squares_summed, squares_at(g, b, s + 1))
                        pe.matmul(work[s][:, :], r.ones32[:, :], squares[:, 2 * s, :], start=b > 0, stop=True
                                  ).then_inc(sem.norm_made, 1)

                def score(b, u):
                    if u == 0:
                        pe.wait_ge(sem.placed, at(n, PLACED, b, PLACED))
                    hp, jh = u // 2, u % 2
                    bank = scores[u]
                    pe.matmul(bank[:, 0:4 * KC], r.ident_bf[:, :], r.mask_bf[:, 0 if b == 0 and jh == 0 else 1, :],
                              start=True, stop=False, skip_group_check=True)
                    for jj in range(2):
                        for odd in range(2):
                            c = 4 * jh + 2 * jj + odd
                            mm = pe.matmul(bank[64 * odd:64 * odd + 64, jj * 2 * KC:(jj + 1) * 2 * KC],
                                           r.q_pair[:, hp, c * QC:(c + 1) * QC],
                                           r.k_pair[:, hp, :, c * QC:c * QC + KC],
                                           start=False, stop=True, skip_group_check=True)
                    mm.then_inc(sem.scored, 1)

                def turn(b, a):
                    pe.wait_ge(sem.normalised, at(n, 4, b, a + 1))
                    if b or a:
                        pe.wait_ge(sem.turned_copied, at(n, 4, b, a))
                    else:
                        pe.wait_ge(sem.turned_copied, at(n, 4, 0, 0))
                    for j in range(4):
                        mm = pe.transpose(pt_ps[0:KC, j * P:(j + 1) * P], r.probs[:, a, j * KC:(j + 1) * KC], r.ident[:, :])
                    mm.then_inc(sem.turned, 1)

                def attend(b, a):
                    pe.wait_ge(sem.turned_copied, at(n, 4, b, a + 1))
                    if a % 2 == 0:
                        pe.wait_ge(sem.out_copied, at(n, 2, b, a // 2))
                    hp, jh = a // 2, a % 2
                    for jj in range(2):
                        for odd in range(2):
                            c = 4 * jh + 2 * jj + odd
                            for hh in range(2):
                                first = (2 * jj + hh) * P + odd * QC
                                head = 2 * hp + hh
                                mm = pe.matmul(out_ps[64 * hh:64 * hh + 64, c * QC:(c + 1) * QC],
                                               r.v_win[0:KC, b % 2, c, head * DH:(head + 1) * DH],
                                               r.turned_sb[0:KC, a % 2, first:first + QC],
                                               start=True, stop=True)
                    mm.then_inc(sem.attended, 1)

                def first_blocks():
                    for u in range(4):
                        project(0, u)
                    norms(0)
                    for u in range(4):
                        project(1, u)
                    for v in range(4):
                        project_v(0, v)
                    norms(1)

                def project_out(b, pairs):
                    if 0 in pairs:
                        pe.wait_ge(sem.out_copied, at(n, 2, b, 2))
                        pe.wait_ge(sem.v_read, at(n, 4, BLOCKS - 1, b + 3))
                    for c in pairs:
                        mm = pe.matmul(work[b][:, :], r.wo[:, c, :], r.attn[:, c, b * BT:(b + 1) * BT], start=c == 0, stop=c == 7)
                    if 7 in pairs:
                        mm.then_inc(sem.projected_out, 1)

                def step(b):
                    score(b, 0)
                    for u in range(3):
                        score(b, u + 1)
                        if exists(b + 2, last):
                            project(b + 2, u)
                    if exists(b + 2, last):
                        project(b + 2, 3)
                    if last and b == BLOCKS - 1:
                        pe.wait_ge(sem.ffn_loaded, L * 64 + 64)
                        project_out(0, range(8))
                    turn(b, 0)
                    for a in range(4):
                        if a < 3:
                            if exists(b + 1, last):
                                project_v(b + 1, a)
                            turn(b, a + 1)
                        if a == 2 and exists(b + 1, last):
                            project_v(b + 1, 3)
                        if a == 3 and exists(b + 2, last):
                            norms(b + 2)
                        if last and b == BLOCKS - 1:
                            project_out(1, range(2 * a, 2 * a + 2))
                        attend(b, a)

                return first_blocks, step

            run(pe, heads)

        @block.scalar
        def _(act):
            act.preload_act_table_set("natural_log_exp_and_others")

            def heads(n, g, last):
                def copy_raw(b, u):
                    if u == 0:
                        act.wait_ge(sem.multiplied, at(n, 8, b, 0))
                        act.wait_ge(sem.tail_copied, at(n, 1, b, 0))
                    act.wait_ge(sem.qk_made, at(n, 4, b, u + 1))
                    to = raw_q[:, u, :] if u < 2 else raw_k[:, u - 2, PREV:]
                    act.copy(to, work[u % 2][:, :]).then_inc(sem.qk_read, 1)

                def square(b, u):
                    act.wait_ge(sem.qk_read, at(n, 4, b, u + 1))
                    src = raw_q[:, u, :] if u < 2 else raw_k[:, u - 2, PREV:]
                    act.activation(squares[:, u, :], src, ACT.Square).then_inc(sem.squared, 1)

                def copy_v(b, v):
                    act.wait_ge(sem.v_made, at(n, 4, b, v + 1))
                    act.copy(r.v_win[0:KC, b % 2, 2 * v:2 * v + 2, :].rearrange("p c n -> p (c n)"),
                             work[v % 2][0:KC, :]).then_inc(sem.v_read, 1)

                def inverse_norms(b):
                    act.wait_ge(sem.rotated, at(n, 4, b, 0))
                    act.wait_ge(sem.norm_tail_copied, at(n, 1, b, 0))
                    to = (r.inv_q[:, :], r.inv_k[:, PREV:])
                    for s in range(2):
                        act.wait_ge(sem.norm_made, at(n, 2, b, s + 1))
                        act.activation(to[s], work[s][:, :], ACT.Ln, bias=r.tiny[:, 0:1],
                                       scale=float(2 ** 20)).then_inc(sem.norm_read, 1)
                    for s in range(2):
                        act.wait_ge(sem.norm_read, at(n, 2, b, s + 1))
                        act.activation(to[s], to[s], ACT.Exp, bias=r.half_shift[:, 0:1], scale=-0.5
                                       ).then_inc(sem.inverted_norms, 1)

                def exponentials(b, a):
                    act.wait_ge(sem.neg_max_ready, at(n, 4, b, a + 1))
                    for j in range(4):
                        e = act.activation(r.probs[:, a, j * KC:(j + 1) * KC], scores[a][:, j * KC:(j + 1) * KC], ACT.Exp,
                                           bias=r.neg_max[:, a, j:j + 1], scale=QK_SCALE,
                                           accum_out=r.sums[:, a, j:j + 1])
                    e.then_inc(sem.exponentiated, 1)

                def copy_out(b, pair):
                    act.wait_ge(sem.attended, at(n, 4, b, 2 * pair + 2))
                    act.copy(r.attn[:, bass.ds(g * 2 + pair, 1), b * BT:(b + 1) * BT].rearrange("p c n -> p (c n)"),
                             out_ps[:, :]).then_inc(sem.out_copied, 1)

                def first_blocks():
                    for u in range(4):
                        copy_raw(0, u)
                    for u in range(4):
                        square(0, u)
                    inverse_norms(0)
                    for u in range(4):
                        copy_raw(1, u)
                    for v in range(4):
                        copy_v(0, v)
                    for u in range(4):
                        square(1, u)
                    inverse_norms(1)

                def step(b):
                    projects, values = exists(b + 2, last), exists(b + 1, last)
                    for a in range(4):
                        exponentials(b, a)
                        if projects:
                            copy_raw(b + 2, a)
                    if values:
                        copy_v(b + 1, 0)
                    if projects:
                        for u in range(4):
                            square(b + 2, u)
                    if values:
                        copy_v(b + 1, 1)
                        copy_v(b + 1, 2)
                    copy_out(b, 0)
                    if values:
                        copy_v(b + 1, 3)
                    if projects:
                        inverse_norms(b + 2)
                    copy_out(b, 1)

                return first_blocks, step

            run(act, heads)

        @block.vector
        def _(dve):
            dve.memset(raw_k[:, :, 0:PREV], 0.0).then_inc(sem.tables_ready, 1)
            dve.memset(r.inv_k[:, 0:PREV], 0.0).then_inc(sem.tables_ready, 1)
            lay = bass.ds(L, 1)

            def scale_tables():
                dve.wait_ge(sem.tables_loaded, L * 64 + 64)
                for s, col in enumerate((0, 1, 1, 0)):
                    dve.tensor_scalar(r.tab_q[:, s, :], r.tab_q[:, s, :], r.qk_scale[:, lay, col], None, ALU.mult
                                      ).then_inc(sem.tables_ready, 1)
                    dve.tensor_scalar(r.tab_k[:, s, :], r.tab_k[:, s, :], r.qk_scale[:, lay, 2 + col], None, ALU.mult
                                      ).then_inc(sem.tables_ready, 1)
                dve.wait_ge(sem.tables_ready, L * 10 + 10)

            def heads(n, g, last):
                def take_weights(m):
                    dve.wait_ge(sem.weights_loaded, m * 48 + 48)
                    dve.wait_ge(sem.qk_read, at(m, 4, 0, 0))
                    for s in range(2):
                        dve.tensor_copy(r.w_qk[:, 2 * s:2 * s + 2, :].rearrange("p h (a d) -> p h a d", a=4),
                                        r.w_stage[:, s, :].rearrange("p (a h d) -> p h a d", a=4, h=2)
                                        ).then_inc(sem.weights_copied, 1)

                def take_v_weights(m):
                    dve.wait_ge(sem.v_read, at(m, 4, 0, 0))
                    dve.tensor_copy(r.w_v[:, :], r.w_stage[:, 2, :]).then_inc(sem.weights_copied, 1)

                def multiply(b, steps):
                    for step in steps:
                        s, plane = step % 4, (0, 1, 1, 0)[step % 4]
                        if step == 0:
                            dve.wait_ge(sem.summed, at(n, 4, b, 0))
                            dve.wait_ge(sem.rotated, at(n, 4, b, 0))
                        if step < 4:
                            dve.wait_ge(sem.qk_read, at(n, 4, b, plane + 1))
                            dve.tensor_tensor(r.prod_q[:, s, :], raw_q[:, plane, :], r.tab_q[:, s, :], ALU.mult
                                              ).then_inc(sem.multiplied, 1)
                        else:
                            if step == 4:
                                dve.wait_ge(sem.tail_copied, at(n, 1, b, 0))
                            dve.wait_ge(sem.qk_read, at(n, 4, b, plane + 3))
                            dve.tensor_tensor(r.prod_k[:, s, :], raw_k[:, plane, :], r.tab_k[:, s, :], ALU.mult
                                              ).then_inc(sem.multiplied, 1)

                def finish_rotation(b, half):
                    if half == 0:
                        dve.wait_ge(sem.placed, at(n, PLACED, b, 0))
                        dve.wait_ge(sem.inverted_norms, at(n, 2, b, 2))
                        dve.wait_ge(sem.norm_tail_copied, at(n, 1, b, 0))
                        dve.wait_ge(sem.summed, at(n, 4, b, 4))
                    to, inv, prod = (r.rot_k, r.inv_k, r.prod_k) if half < 2 else (r.rot_q, r.inv_q, r.prod_q)
                    dve.scalar_tensor_tensor(to[:, half % 2, :], inv[:, :], 1e12, prod[:, 2 * (half % 2), :],
                                             ALU.min, ALU.mult).then_inc(sem.rotated, 1)

                def maximum(b, a):
                    dve.wait_ge(sem.scored, at(n, 4, b, a + 1))
                    dve.tensor_reduce(r.row_max[:, a, :], scores[a][:, 0:4 * KC].rearrange("p (j k) -> p j k", j=4),
                                      AX.X, ALU.max).then_inc(sem.max_ready, 1)
                    dve.wait_ge(sem.max_ready, at(n, 4, b, a + 1))
                    dve.tensor_scalar(r.neg_max[:, a, :], r.row_max[:, a, :], -QK_SCALE, None, ALU.mult
                                      ).then_inc(sem.neg_max_ready, 1)

                def invert_sums(b, a):
                    dve.wait_ge(sem.exponentiated, at(n, 4, b, a + 1))
                    dve.reciprocal(r.inv_sums[:, a, :], r.sums[:, a, :]).then_inc(sem.sums_inverted, 1)

                def copy_turned(b, a):
                    dve.wait_ge(sem.turned, at(n, 4, b, a + 1))
                    if a >= 2:
                        dve.wait_ge(sem.attended, at(n, 4, b, a - 1))
                    else:
                        dve.wait_ge(sem.attended, at(n, 4, b, 0))
                    dve.tensor_copy(r.turned_sb[0:KC, a % 2, :], pt_ps[0:KC, :]).then_inc(sem.turned_copied, 1)

                def first_blocks():
                    take_weights(n)
                    take_v_weights(n)
                    scale_tables()
                    multiply(0, range(8))
                    for half in range(4):
                        finish_rotation(0, half)
                    multiply(1, range(8))

                def step(b):
                    maximum(b, 0)
                    maximum(b, 1)
                    maximum(b, 2)
                    invert_sums(b, 0)
                    maximum(b, 3)
                    for a in range(4):
                        if exists(b + 1, last):
                            finish_rotation(b + 1, a)
                        if a < 3:
                            invert_sums(b, a + 1)
                        if a == 3 and exists(b + 2, last):
                            multiply(b + 2, range(0, 2))
                        copy_turned(b, a)
                    if exists(b + 2, last):
                        multiply(b + 2, range(2, 8))
                    if not last and b == 1:
                        take_weights(n + 1)
                    if not last and b == 2:
                        take_v_weights(n + 1)

                return first_blocks, step

            run(dve, heads)

        @block.gpsimd
        def _(pool):
            def heads(n, g, last):
                def sum_products(b):
                    for x, prod in enumerate((r.prod_q, r.prod_k)):
                        for half, op in ((0, ALU.subtract), (1, ALU.add)):
                            pool.wait_ge(sem.multiplied, at(n, 8, b, 4 * x + 2 * half + 2))
                            pool.tensor_tensor(prod[:, 2 * half, :], prod[:, 2 * half, :], prod[:, 2 * half + 1, :], op
                                               ).then_inc(sem.summed, 1)

                def sum_squares(b):
                    for s in range(2):
                        pool.wait_ge(sem.squared, at(n, 4, b, 2 * s + 2))
                        pool.tensor_tensor(squares[:, 2 * s, :], squares[:, 2 * s, :], squares[:, 2 * s + 1, :], ALU.add
                                           ).then_inc(sem.squares_summed, 1)

                def copy_tail(b):
                    pool.wait_ge(sem.multiplied, at(n, 8, b, 8))
                    pool.wait_ge(sem.qk_read, at(n, 4, b, 4))
                    tail = raw_k[:, :, BT:BT + PREV]
                    pool.tensor_tensor(raw_k[:, :, 0:PREV], tail, r.zeros[:, :, :], ALU.add).then_inc(sem.tail_copied, 1)

                def copy_norm_tail(b):
                    pool.wait_ge(sem.inverted_norms, at(n, 2, b, 2))
                    pool.wait_ge(sem.rotated, at(n, 4, b, 4))
                    tail = r.inv_k[:, BT:BT + PREV]
                    pool.tensor_tensor(r.inv_k[:, 0:PREV], tail, r.zeros[:, 0, :], ALU.add).then_inc(sem.norm_tail_copied, 1)

                def normalise(b, a):
                    pool.wait_ge(sem.sums_inverted, at(n, 4, b, a + 1))
                    probs = r.probs[:, a, :].rearrange("p (j k) -> p j k", j=4)
                    pool.tensor_tensor(probs, probs, r.inv_sums[:, a, :].unsqueeze(2).to_broadcast([P, 4, KC]), ALU.mult
                                       ).then_inc(sem.normalised, 1)

                def first_blocks():
                    sum_products(0)
                    copy_tail(0)
                    copy_norm_tail(0)
                    sum_squares(1)
                    sum_products(1)
                    copy_tail(1)

                def step(b):
                    for a in range(4):
                        normalise(b, a)
                    if exists(b + 1, last):
                        copy_norm_tail(b + 1)
                    if exists(b + 2, last):
                        sum_squares(b + 2)
                        sum_products(b + 2)
                        copy_tail(b + 2)

                return first_blocks, step

            run(pool, heads)


def output_and_ffn(nc, L, r, sem):
    banks = r.banks
    y = r.y
    lay = bass.ds(L, 1)
    MID = ((0, P), (P, P), (2 * P, INNER2 - 2 * P))

    def at(per_block, b, k):
        return L * (BLOCKS * per_block) + (b * per_block + k + PRIMED)

    with nc.Block() as block:

        def project_out(pe, b):
            for c in range(8):
                mm = pe.matmul(banks[b - 2][:, :], r.wo[:, c, :], r.attn[:, c, b * BT:(b + 1) * BT], start=c == 0, stop=c == 7)
            mm.then_inc(sem.projected_out, 1)

        def mean(pe, b):
            pe.wait_ge(sem.ffn_shifted, at(2, b, 2))
            if b >= 1:
                pe.wait_ge(sem.centred, at(1, b, 0))
            pe.matmul(banks[7][:, :], r.ones_mean[:, :], r.shifted[:, b % 2, :], start=True, stop=True
                      ).then_inc(sem.mean_made, 1)

        def variance(pe, b):
            pe.wait_ge(sem.centred_squared, at(1, b, 1))
            if b >= 1:
                pe.wait_ge(sem.logged, at(1, b, 0))
            pe.matmul(banks[6][:, :], r.ones_mean[:, :], r.centred_sq[:, b % 2, :], start=True, stop=True
                      ).then_inc(sem.variance_made, 1)

        def up(pe, b, m):
            first, size = MID[m]
            if m == 0:
                pe.wait_ge(sem.ffn_normed, at(1, b, 1))
                if b == 0:
                    pe.wait_ge(sem.residual_added, at(1, 0, BLOCKS))
            for gate in (1, 0):
                if b >= 1 and gate:
                    pe.wait_ge(sem.gated, at(3, b, m - 2))
                elif b >= 1:
                    pe.wait_ge(sem.gate_applied, at(3, b, m - 2))
                pe.matmul(banks[2 * m + gate][0:size, :], r.w1[:, gate * INNER2 + first:gate * INNER2 + first + size],
                          r.normed[:, b, :], start=True, stop=True).then_inc(sem.gate_made if gate else sem.value_made, 1)

        def down(pe, b):
            pe.wait_ge(sem.gate_applied, at(3, b, 3))
            if b >= 1:
                pe.wait_ge(sem.ffn_added, at(1, b, 0))
            else:
                pe.wait_ge(sem.logged, at(1, 0, BLOCKS))
            for m, (first, size) in enumerate(MID):
                mm = pe.matmul(banks[6][:, :], r.w2[0:size, m, :], r.inner[0:size, b % 2, m, :], start=m == 0, stop=m == 2)
            mm.then_inc(sem.ffn_made, 1)

        @block.sync
        def _(sp):
            load_tables(sp, r, sem)

        @block.tensor
        def _(pe):
            mean(pe, 0)
            project_out(pe, 2)
            variance(pe, 0)
            mean(pe, 1)
            project_out(pe, 3)
            variance(pe, 1)
            mean(pe, 2)
            variance(pe, 2)
            mean(pe, 3)
            for m in range(2):
                up(pe, 0, m)
            variance(pe, 3)
            up(pe, 0, 2)
            for b in range(1, BLOCKS):
                for m in range(3):
                    up(pe, b, m)
                down(pe, b - 1)
            down(pe, BLOCKS - 1)

        def add_ffn(dve, b):
            cols = slice(1 + b * BT, 1 + (b + 1) * BT)
            dve.wait_ge(sem.ffn_made, at(1, b, 1))
            dve.scalar_tensor_tensor(y[:, cols], banks[6][:, :], r.b2[:, lay], y[:, cols], ALU.add, ALU.add
                                     ).then_inc(sem.ffn_added, 1)

        def shift_for_attention(dve, b):
            dve.wait_ge(sem.ffn_added, at(1, b, 1))
            for rows, back in ((slice(0, 64), 0), (slice(64, 128), 1)):
                dve.tensor_copy(r.ys[rows, PREV + b * BT:PREV + (b + 1) * BT],
                                y[rows, 1 - back + b * BT:1 - back + (b + 1) * BT]).then_inc(sem.attn_shifted, 1)

        @block.vector
        def _(dve):
            for b in range(BLOCKS + 1):
                if b < BLOCKS:
                    cols = slice(1 + b * BT, 1 + (b + 1) * BT)
                    dve.wait_ge(sem.projected_out, at(1, b, 1))
                    dve.tensor_tensor(y[:, cols], banks[4 + b if b < 2 else b - 2][:, :], y[:, cols], ALU.add
                                      ).then_inc(sem.residual_added, 1)
                    dve.wait_ge(sem.residual_added, at(1, b, 1))
                    if b >= 2:
                        dve.wait_ge(sem.mean_made, at(1, b, -1))
                    dve.tensor_copy(r.shifted[0:64, b % 2, :], y[0:64, cols]).then_inc(sem.ffn_shifted, 1)
                    dve.tensor_copy(r.shifted[64:128, b % 2, :], y[64:128, b * BT:(b + 1) * BT]).then_inc(sem.ffn_shifted, 1)
                    dve.wait_ge(sem.ffn_shifted, at(2, b, 2))
                    dve.wait_ge(sem.mean_made, at(1, b, 1))
                    dve.tensor_tensor(r.centred[:, b % 2, :], r.shifted[:, b % 2, :], banks[7][:, :], ALU.subtract
                                      ).then_inc(sem.centred, 1)
                if b >= 1:
                    c = b - 1
                    dve.wait_ge(sem.inverse_std, at(1, c, 1))
                    dve.tensor_tensor(r.scaled[:, c % 2, :], r.centred[:, c % 2, :], r.inv_std[:, :], ALU.mult).then_inc(sem.scaled, 1)
                    dve.wait_ge(sem.scaled, at(1, c, 1))
                    dve.tensor_scalar(r.normed[:, c, :], r.scaled[:, c % 2, :], r.ln_gb[:, lay, 0], r.ln_gb[:, lay, 1],
                                      ALU.mult, ALU.add).then_inc(sem.ffn_normed, 1)
            for b in range(BLOCKS):
                for m, (first, size) in enumerate(MID):
                    dve.wait_ge(sem.gated, at(3, b, m + 1))
                    dve.wait_ge(sem.value_made, at(3, b, m + 1))
                    if b >= 2:
                        dve.wait_ge(sem.ffn_made, at(1, b, -1))
                    dve.scalar_tensor_tensor(r.inner[0:size, b % 2, m, :], banks[2 * m][0:size, :], r.b1_now[0:size, m:m + 1],
                                             r.gate[0:size, m, :], ALU.add, ALU.mult).then_inc(sem.gate_applied, 1)
                if b >= 1:
                    add_ffn(dve, b - 1)
                    shift_for_attention(dve, b - 1)
            add_ffn(dve, BLOCKS - 1)
            shift_for_attention(dve, BLOCKS - 1)

        @block.scalar
        def _(act):
            act.preload_act_table_set("natural_log_exp_and_others")
            act.copy(r.b1_now[:, :], r.b1[:, lay, :].rearrange("p l n -> p (l n)")).then_inc(sem.b1_copied, 1)
            for b in range(BLOCKS):
                act.wait_ge(sem.centred, at(1, b, 1))
                if b >= 2:
                    act.wait_ge(sem.variance_made, at(1, b, -1))
                act.activation(r.centred_sq[:, b % 2, :], r.centred[:, b % 2, :], ACT.Square).then_inc(sem.centred_squared, 1)
                act.wait_ge(sem.variance_made, at(1, b, 1))
                act.activation(r.log_var[:, :], banks[6][:, :], ACT.Ln, bias=r.eps[:, 0:1]).then_inc(sem.logged, 1)
                act.wait_ge(sem.logged, at(1, b, 1))
                if b >= 1:
                    act.wait_ge(sem.scaled, at(1, b, 0))
                act.activation(r.inv_std[:, :], r.log_var[:, :], ACT.Exp, scale=-0.5).then_inc(sem.inverse_std, 1)
            for b in range(BLOCKS):
                for m, (first, size) in enumerate(MID):
                    if b == 0 and m == 0:
                        act.wait_ge(sem.b1_copied, L + 1)
                    act.wait_ge(sem.gate_made, at(3, b, m + 1))
                    if b >= 1:
                        act.wait_ge(sem.gate_applied, at(3, b, m - 2))
                    act.activation(r.gate[0:size, m, :], banks[2 * m + 1][0:size, :], ACT.Gelu,
                                   bias=r.b1_now[0:size, 3 + m:4 + m]).then_inc(sem.gated, 1)
def semaphores(nc, ctx):
    sem = Record()
    sem.consts_loaded = ctx.enter_context(nc.semaphore("consts_loaded"))
    sem.x_loaded = ctx.enter_context(nc.semaphore("x_loaded"))
    sem.small_loaded = ctx.enter_context(nc.semaphore("small_loaded"))
    sem.cleared = ctx.enter_context(nc.semaphore("cleared"))
    sem.stats = ctx.enter_context(nc.semaphore("stats"))
    sem.aggregated = ctx.enter_context(nc.semaphore("aggregated"))
    sem.std_ready = ctx.enter_context(nc.semaphore("std_ready"))
    sem.rstd_ready = ctx.enter_context(nc.semaphore("rstd_ready"))
    sem.x_normed = ctx.enter_context(nc.semaphore("x_normed"))
    sem.x_transposed = ctx.enter_context(nc.semaphore("x_transposed"))
    sem.x_copied = ctx.enter_context(nc.semaphore("x_copied"))
    sem.wA_loaded = ctx.enter_context(nc.semaphore("wA_loaded"))
    sem.colsA_loaded = ctx.enter_context(nc.semaphore("colsA_loaded"))
    sem.powered = ctx.enter_context(nc.semaphore("powered"))
    sem.wA_turned = ctx.enter_context(nc.semaphore("wA_turned"))
    sem.bc_split = ctx.enter_context(nc.semaphore("bc_split"))
    sem.wA_ready = ctx.enter_context(nc.semaphore("wA_ready"))
    sem.xi_made = ctx.enter_context(nc.semaphore("xi_made"))
    sem.xi_copied = ctx.enter_context(nc.semaphore("xi_copied"))
    sem.bu_made = ctx.enter_context(nc.semaphore("bu_made"))
    sem.bu_copied = ctx.enter_context(nc.semaphore("bu_copied"))
    sem.diag_ready = ctx.enter_context(nc.semaphore("diag_ready"))
    sem.og_made = ctx.enter_context(nc.semaphore("og_made"))
    sem.o_gated = ctx.enter_context(nc.semaphore("o_gated"))
    sem.oT_copied = ctx.enter_context(nc.semaphore("oT_copied"))
    sem.aT_added = ctx.enter_context(nc.semaphore("aT_added"))
    sem.o_turned = ctx.enter_context(nc.semaphore("o_turned"))
    sem.aout_made = ctx.enter_context(nc.semaphore("aout_made"))
    sem.dt_exp = ctx.enter_context(nc.semaphore("dt_exp"))
    sem.sig_ready = ctx.enter_context(nc.semaphore("sig_ready"))
    sem.colchain = ctx.enter_context(nc.semaphore("colchain"))
    sem.coefs_ready = ctx.enter_context(nc.semaphore("coefs_ready"))
    sem.state_zeroed = ctx.enter_context(nc.semaphore("state_zeroed"))
    sem.osc1 = ctx.enter_context(nc.semaphore("osc1"))
    sem.osc2 = ctx.enter_context(nc.semaphore("osc2"))
    sem.osc_kept = ctx.enter_context(nc.semaphore("osc_kept"))
    sem.doubled = ctx.enter_context(nc.semaphore("doubled"))
    sem.silu_ready = ctx.enter_context(nc.semaphore("silu_ready"))
    sem.o_std = ctx.enter_context(nc.semaphore("o_std"))
    sem.o_rstd = ctx.enter_context(nc.semaphore("o_rstd"))
    sem.wB_loaded = ctx.enter_context(nc.semaphore("wB_loaded"))
    sem.router_exp = ctx.enter_context(nc.semaphore("router_exp"))
    sem.routed = ctx.enter_context(nc.semaphore("routed"))
    sem.experts_scaled = ctx.enter_context(nc.semaphore("experts_scaled"))
    sem.experts_made = ctx.enter_context(nc.semaphore("experts_made"))
    sem.top_found = ctx.enter_context(nc.semaphore("top_found"))
    sem.top_neg = ctx.enter_context(nc.semaphore("top_neg"))
    sem.index_found = ctx.enter_context(nc.semaphore("index_found"))
    sem.expert_found = ctx.enter_context(nc.semaphore("expert_found"))
    sem.expert_cast = ctx.enter_context(nc.semaphore("expert_cast"))
    sem.prob_ready = ctx.enter_context(nc.semaphore("prob_ready"))
    sem.selected = ctx.enter_context(nc.semaphore("selected"))
    sem.experts_summed = ctx.enter_context(nc.semaphore("experts_summed"))
    sem.moe_added = ctx.enter_context(nc.semaphore("moe_added"))
    sem.wC_loaded = ctx.enter_context(nc.semaphore("wC_loaded"))
    sem.parts_cast = ctx.enter_context(nc.semaphore("parts_cast"))
    sem.parts_subtracted = ctx.enter_context(nc.semaphore("parts_subtracted"))
    sem.kC_read = ctx.enter_context(nc.semaphore("kC_read"))
    sem.stacked = ctx.enter_context(nc.semaphore("stacked"))
    sem.qkC_made = ctx.enter_context(nc.semaphore("qkC_made"))
    sem.qkC_read = ctx.enter_context(nc.semaphore("qkC_read"))
    sem.vC_made = ctx.enter_context(nc.semaphore("vC_made"))
    sem.v_cleared = ctx.enter_context(nc.semaphore("v_cleared"))
    sem.vC_copied = ctx.enter_context(nc.semaphore("vC_copied"))
    sem.ones3_set = ctx.enter_context(nc.semaphore("ones3_set"))
    sem.ones_placed = ctx.enter_context(nc.semaphore("ones_placed"))
    sem.stack_loaded = ctx.enter_context(nc.semaphore("stack_loaded"))
    sem.max_split = ctx.enter_context(nc.semaphore("max_split"))
    sem.max_placed = ctx.enter_context(nc.semaphore("max_placed"))
    sem.taken = ctx.enter_context(nc.semaphore("taken"))
    sem.v_taken = ctx.enter_context(nc.semaphore("v_taken"))
    sem.part_max_done = ctx.enter_context(nc.semaphore("part_max_done"))
    sem.max_scored = ctx.enter_context(nc.semaphore("max_scored"))
    sem.max_ready_c = ctx.enter_context(nc.semaphore("max_ready_c"))
    sem.outputs_taken = ctx.enter_context(nc.semaphore("outputs_taken"))
    sem.max_turned = ctx.enter_context(nc.semaphore("max_turned"))
    sem.exp_done = ctx.enter_context(nc.semaphore("exp_done"))
    sem.weights_scored = ctx.enter_context(nc.semaphore("weights_scored"))
    sem.acc_copied = ctx.enter_context(nc.semaphore("acc_copied"))
    sem.valued = ctx.enter_context(nc.semaphore("valued"))
    sem.outputs_turned = ctx.enter_context(nc.semaphore("outputs_turned"))
    sem.max_reduced = ctx.enter_context(nc.semaphore("max_reduced"))
    sem.max_cut = ctx.enter_context(nc.semaphore("max_cut"))
    sem.den_inverted = ctx.enter_context(nc.semaphore("den_inverted"))
    sem.aC_copied = ctx.enter_context(nc.semaphore("aC_copied"))
    sem.aC_turned = ctx.enter_context(nc.semaphore("aC_turned"))
    sem.c_added = ctx.enter_context(nc.semaphore("c_added"))
    sem.c_out = ctx.enter_context(nc.semaphore("c_out"))
    sem.ffn_loaded = ctx.enter_context(nc.semaphore("ffn_loaded"))
    sem.weights_copied = ctx.enter_context(nc.semaphore("weights_copied"))
    sem.weights_loaded = ctx.enter_context(nc.semaphore("weights_loaded"))
    sem.squared = ctx.enter_context(nc.semaphore("squared"))
    sem.rotated = ctx.enter_context(nc.semaphore("rotated"))
    sem.scored = ctx.enter_context(nc.semaphore("scored"))
    sem.normalised = ctx.enter_context(nc.semaphore("normalised"))
    sem.turned_copied = ctx.enter_context(nc.semaphore("turned_copied"))
    sem.turned = ctx.enter_context(nc.semaphore("turned"))
    sem.out_copied = ctx.enter_context(nc.semaphore("out_copied"))
    sem.attended = ctx.enter_context(nc.semaphore("attended"))
    sem.multiplied = ctx.enter_context(nc.semaphore("multiplied"))
    sem.tail_copied = ctx.enter_context(nc.semaphore("tail_copied"))
    sem.inverted_norms = ctx.enter_context(nc.semaphore("inverted_norms"))
    sem.neg_max_ready = ctx.enter_context(nc.semaphore("neg_max_ready"))
    sem.max_ready = ctx.enter_context(nc.semaphore("max_ready"))
    sem.exponentiated = ctx.enter_context(nc.semaphore("exponentiated"))
    sem.tables_ready = ctx.enter_context(nc.semaphore("tables_ready"))
    sem.summed = ctx.enter_context(nc.semaphore("summed"))
    sem.sums_inverted = ctx.enter_context(nc.semaphore("sums_inverted"))
    sem.residual_added = ctx.enter_context(nc.semaphore("residual_added"))
    sem.tables_loaded = ctx.enter_context(nc.semaphore("tables_loaded"))
    sem.qk_made = ctx.enter_context(nc.semaphore("qk_made"))
    sem.qk_read = ctx.enter_context(nc.semaphore("qk_read"))
    sem.v_made = ctx.enter_context(nc.semaphore("v_made"))
    sem.v_read = ctx.enter_context(nc.semaphore("v_read"))
    sem.norm_made = ctx.enter_context(nc.semaphore("norm_made"))
    sem.norm_read = ctx.enter_context(nc.semaphore("norm_read"))
    sem.norm_tail_copied = ctx.enter_context(nc.semaphore("norm_tail_copied"))
    sem.rows_cleared = ctx.enter_context(nc.semaphore("rows_cleared"))
    sem.bias_loaded = ctx.enter_context(nc.semaphore("bias_loaded"))
    sem.bias_cut = ctx.enter_context(nc.semaphore("bias_cut"))
    sem.bias_placed = ctx.enter_context(nc.semaphore("bias_placed"))
    sem.placed = ctx.enter_context(nc.semaphore("placed"))
    sem.squares_summed = ctx.enter_context(nc.semaphore("squares_summed"))
    sem.projected_out = ctx.enter_context(nc.semaphore("projected_out"))
    sem.ffn_normed = ctx.enter_context(nc.semaphore("ffn_normed"))
    sem.gated = ctx.enter_context(nc.semaphore("gated"))
    sem.gate_applied = ctx.enter_context(nc.semaphore("gate_applied"))
    sem.gate_made = ctx.enter_context(nc.semaphore("gate_made"))
    sem.value_made = ctx.enter_context(nc.semaphore("value_made"))
    sem.ffn_shifted = ctx.enter_context(nc.semaphore("ffn_shifted"))
    sem.mean_made = ctx.enter_context(nc.semaphore("mean_made"))
    sem.centred_squared = ctx.enter_context(nc.semaphore("centred_squared"))
    sem.variance_made = ctx.enter_context(nc.semaphore("variance_made"))
    sem.ffn_added = ctx.enter_context(nc.semaphore("ffn_added"))
    sem.ffn_made = ctx.enter_context(nc.semaphore("ffn_made"))
    sem.centred = ctx.enter_context(nc.semaphore("centred"))
    sem.inverse_std = ctx.enter_context(nc.semaphore("inverse_std"))
    sem.scaled = ctx.enter_context(nc.semaphore("scaled"))
    sem.attn_shifted = ctx.enter_context(nc.semaphore("attn_shifted"))
    sem.logged = ctx.enter_context(nc.semaphore("logged"))
    sem.b1_copied = ctx.enter_context(nc.semaphore("b1_copied"))
    sem.b1_cleared = ctx.enter_context(nc.semaphore("b1_cleared"))
    sem.y_turned = ctx.enter_context(nc.semaphore("y_turned"))
    sem.out_summed = ctx.enter_context(nc.semaphore("out_summed"))
    sem.out_stored = ctx.enter_context(nc.semaphore("out_stored"))
    sem.y_shifted = ctx.enter_context(nc.semaphore("y_shifted"))
    return sem


def looped(sem):
    return (sem.qk_made, sem.qk_read, sem.v_made, sem.v_read, sem.norm_made, sem.norm_read, sem.norm_tail_copied,
            sem.placed, sem.squares_summed, sem.acc_copied, sem.attended, sem.centred, sem.centred_squared, sem.den_inverted, sem.exp_done,
            sem.exponentiated, sem.ffn_added, sem.ffn_made, sem.ffn_normed, sem.ffn_shifted, sem.gate_applied,
            sem.gate_made, sem.gated, sem.inverse_std, sem.inverted_norms, sem.logged, sem.max_cut, sem.max_placed,
            sem.max_ready, sem.max_ready_c, sem.max_reduced, sem.max_scored, sem.max_split, sem.max_turned,
            sem.mean_made, sem.multiplied, sem.neg_max_ready, sem.normalised, sem.osc1, sem.osc2, sem.out_copied,
            sem.outputs_taken, sem.outputs_turned, sem.part_max_done, sem.projected_out, sem.residual_added,
            sem.rotated, sem.scaled, sem.scored, sem.squared, sem.stack_loaded, sem.summed, sem.sums_inverted,
            sem.tail_copied, sem.taken, sem.turned, sem.turned_copied, sem.v_taken, sem.value_made, sem.valued,
            sem.variance_made, sem.weights_copied, sem.weights_scored)



def program(nc, ins, const, out):
    ctx = ExitStack()
    with ctx:
        r = Record()
        sem = semaphores(nc, ctx)

        def sb(name, shape, dt=fp32, within=None):
            return (within or ctx).enter_context(nc.sbuf_tensor(name, shape, dt))

        psum = ctx.enter_context(nc.psum_tensor("psum", [P, 8, BT], fp32))
        r.banks = [psum[:, i, :] for i in range(8)]
        r.pairs = [psum[:, 0:2, :], psum[:, 2:4, :]]
        r.d = ins

        r.x = sb("x", [P, TILES, P])
        r.ident = sb("ident", [P, P])
        r.ones32 = sb("ones32", [P, P])
        r.ones_mean = sb("ones_mean", [P, P])
        r.ident_bf = sb("ident_bf", [P, P], bf16)
        r.mask_bf = sb("mask_bf", [P, 2, 4 * KC], bf16)
        r.eps = sb("eps", [P, 1])
        r.tiny = sb("tiny", [P, 1])
        r.half_shift = sb("half_shift", [P, 1])
        r.stats = sb("stats", [P, TILES, 6])
        r.moments = sb("moments", [P, TILES, 2])
        r.std = sb("std", [P, TILES])
        r.rstd = sb("rstd", [P, TILES])
        r.b1 = sb("b1", [P, DEPTH, 6])
        r.b2 = sb("b2", [P, DEPTH])
        r.ln_gb = sb("ln_gb", [P, DEPTH, 2])
        r.qk_scale = sb("qk_scale", [P, DEPTH, 4])
        early = ctx.enter_context(ExitStack())
        r.iota8 = sb("iota8", [P, 8], within=early)
        r.causal_bf = sb("causal_bf", [P, 2, P], bf16, within=early)
        r.ones3b = sb("ones3b", [3, P], bf16, within=early)
        r.bias3 = sb("bias3", [3, 11 * P], bf16, within=early)
        r.wgate = sb("wgate", [P, P], within=early)
        r.wexp = sb("wexp", [P, 8, P], within=early)
        r.wqkvC = sb("wqkvC", [P, 3 * P], within=early)
        r.woC = sb("woC", [P, P], within=early)
        r.cols_bqk = sb("cols_bqk", [P, 2], within=early)
        first = {}
        k = 0
        for name, cols in CONSTS:
            first[name] = k
            k += cols

        with ExitStack() as own:
            mask_f = sb("mask_f", [P, 2, 4 * KC], within=own)
            causal_f = sb("causal_f", [P, 2, P], within=own)
            with nc.Block() as block:

                @block.sync
                def _(sp):
                    sp.dma_start(r.x[:, :, :], ins['L0_attn_hidden_states'].rearrange("o (t p) c -> p (o t) c", p=P)).then_inc(sem.x_loaded, 16)
                    for name, to in (("ident", r.ident[:, :]), ("ones32", r.ones32[:, :]), ("ones_mean", r.ones_mean[:, :]),
                                     ("mask", mask_f[:, :, :].rearrange("p a n -> p (a n)")),
                                     ("causal", causal_f[:, :, :].rearrange("p a n -> p (a n)")), ("iota8", r.iota8[:, :])):
                        n = dict(CONSTS)[name]
                        sp.dma_start(to, const[:, first[name]:first[name] + n]).then_inc(sem.consts_loaded, 16)
                    for semaphore in looped(sem):
                        sp.sem_inc(semaphore, PRIMED)
                    sp.wait_ge(sem.x_loaded, 16)

                @block.vector
                def _(dve):
                    dve.memset(r.ones3b[:, :], 1.0)
                    dve.memset(r.b1[:, :, :], 0.0).then_inc(sem.b1_cleared, 1)
                    dve.memset(r.eps[:, :], EPS)
                    dve.memset(r.tiny[:, :], 2.0 ** -64)
                    dve.memset(r.half_shift[:, :], LN_2_10)
                    dve.wait_ge(sem.consts_loaded, 16 * (len(CONSTS) - 1))
                    dve.tensor_copy(r.ident_bf[:, :], r.ident[:, :])
                    dve.tensor_copy(r.mask_bf[:, :, :], mask_f[:, :, :])
                    dve.tensor_copy(r.causal_bf[:, :, :], causal_f[:, :, :])

        with ExitStack() as own:
            r.x_norm = sb("x_norm", [P, TILES, P], within=own)
            r.hT = sb("hT", [P, T], within=own)

            r.v_aug = sb("v_aug", [P, TILES, HEADS, 32], within=own)
            r.part_max = sb("part_max", [P, 4, TILES, BLOCKS], within=own)
            r.q_next = sb("q_next", [MAX_ROW + 3, 4, T], bf16, within=own)
            r.k_next = sb("k_next", [MAX_ROW + 3, 4, T], bf16, within=own)
            r.ones3 = sb("ones3", [3, 4 * T], bf16, within=own)

            with ExitStack() as a:
                r.ST, r.CH, r.LOG_ST, r.LOG_CH = 8, T // 8, 3, 8
                r.N_POW = r.LOG_ST + r.LOG_CH
                r.wA = sb("wA", [P, 3, P], within=a)
                r.wAT = sb("wAT", [P, 3, P], within=a)
                r.bc_raw = sb("bc_raw", [P, 2, 2 * P], within=a)
                r.bc = sb("bc", [P, 4, P], within=a)
                r.bcT = sb("bcT", [P, 4, P], within=a)
                r.colsA = sb("colsA", [P, 4], within=a)
                r.colt = sb("colt", [P, 4], within=a)
                r.coef = sb("coef", [P, 4], within=a)
                r.powers = sb("powers", [P, r.N_POW, 4], within=a)
                r.pw_tmp = sb("pw_tmp", [P, 4], within=a)
                r.diag_d = sb("diag_d", [P, P], within=a)
                r.xiT = sb("xiT", [P, T], within=a)
                r.bu = sb("bu", [P, 2, T], within=a)
                r.y_osc = sb("y_osc", [P, 2, T], within=a)
                r.state = sb("state", [P, 2, 2, 2, r.CH], within=a)
                r.drive = sb("drive", [P, 2, r.CH], within=a)
                r.sq_junk = sb("sq_junk", [P, P], within=a)
                r.o_ss = sb("o_ss", [P, TILES], within=a)
                r.sig = sb("sig", [P, 2, P], within=a)
                r.silu = sb("silu", [P, P], within=a)
                r.gated = sb("gated", [P, 2, P], within=a)
                r.gatedT = sb("gatedT", [P, 2, P], within=a)
                r.bias_raw = sb("bias_raw", [1, 11 * P], within=a)
                r.bias_rest = sb("bias_rest", [1, 11 * P], within=a)
                r.bias_parts = sb("bias_parts", [1, 3, 11 * P], bf16, within=a)
                r.a_out = r.x_norm
                normalise_and_transpose(nc, r, sem, 0, r.hT, 0)
                oscillators(nc, r, sem)

            with ExitStack() as b:
                r.N_EXP = 8
                r.top8 = sb("top8", [P, 2, 8], within=b)
                r.top_neg = sb("top_neg", [P, 2, 1], within=b)
                r.top_at = sb("top_at", [P, 2, 8], u32, within=b)
                r.expert_u = sb("expert_u", [P, 2, 1], u32, within=b)
                r.expert_f = sb("expert_f", [P, 2, 1], within=b)
                r.top_p = sb("top_p", [P, 2, 1], within=b)
                r.router_sum = sb("router_sum", [P, 2, 1], within=b)
                r.select = sb("select", [P, 2, 8], within=b)
                r.junk = sb("junk", [P, P], within=b)
                r.scaled_exp = sb("scaled_exp", [P, 2, r.N_EXP, P], within=b)
                r.moe = sb("moe", [P, 2, P], within=b)
                normalise_and_transpose(nc, r, sem, 1, r.hT, 0)
                experts(nc, r, sem)

            with ExitStack() as c:
                d_stack = nc.dram_tensor("stacks", (2, HEADS, len(PRODUCTS), 8, T), bf16, kind="Internal").ap()
                r.d_stack = d_stack
                r.attn_tok = sb("attn_tok", [P, TILES, P], within=c)
                r.aC_T = sb("aC_T", [P, 2, P], within=c)
                normalise_and_transpose(nc, r, sem, 2, r.hT, 0)
                with ExitStack() as proj:
                    r.qkf = sb("qkf", [P, 2, T], within=proj)
                    r.rest = sb("rest", [P, 2, T], within=proj)
                    r.parts = sb("parts", [P, 2, 3, T], bf16, within=proj)
                    causal_projections(nc, r, sem)
                with ExitStack() as att:
                    r.q_now = sb("q_now", [MAX_ROW + 3, 4, T], bf16, within=att)
                    r.k_now = sb("k_now", [MAX_ROW + 3, 4, T], bf16, within=att)
                    r.v_now = sb("v_now", [P, TILES, 4, 32], within=att)
                    r.weights = sb("weights", [P, 4, 2, BT], within=att)
                    r.max_c = sb("max_c", [P, 4 * TILES], within=att)
                    r.neg_max_c = sb("neg_max_c", [P, P], within=att)
                    r.max_rows = sb("max_rows", [4 * TILES, 2, P], within=att)
                    r.max_parts = sb("max_parts", [4 * TILES, 3, P], bf16, within=att)
                    r.acc_sb = sb("acc_sb", [P, BT], within=att)
                    r.inv_den = sb("inv_den", [P, 4, 4], within=att)
                    causal_attention(nc, r, sem)
                causal_output(nc, r, sem)

        early.close()

        r.d_tab = const[:, first["base_tab"]:]
        r.y = sb("y", [P, 1 + T])
        with ExitStack() as d:
            r.ys = sb("ys", [P, PREV + T], within=d)
            r.attn = sb("attn", [P, 8, T], within=d)
            r.wo = sb("wo", [P, 8, P], within=d)
            r.w1 = sb("w1", [P, 2 * INNER2], within=d)
            r.w2 = sb("w2", [P, 3, P], within=d)
            r.zeros = sb("zeros", [P, 2, PREV], within=d)
            r.b1_now = sb("b1_now", [P, 6], within=d)
            r.w_stage = sb("w_stage", [P, 3, GW], within=d)
            r.w_qk = sb("w_qk", [P, 4, P], within=d)
            r.w_v = sb("w_v", [P, GW], within=d)
            r.tab_q = sb("tab_q", [P, 4, BT], within=d)
            r.tab_k = sb("tab_k", [P, 4, BT + PREV], within=d)
            r.k_pair = sb("k_pair", [P, 2, 2, BT + PREV], within=d)
            r.d_wqkv, r.d_wo, r.d_w1, r.d_w2 = (ins['L1_ffn_' + w] for w in ('Wqkv', 'Wo', 'W1', 'W2'))
            with ExitStack() as own:
                r.x_norm = sb("x_norm_d", [P, TILES, P], within=own)
                normalise_and_transpose(nc, r, sem, 3, r.y, 1)
            with nc.Block() as block:

                @block.sync
                def _(sp):
                    load_tables(sp, r, sem)

                @block.vector
                def _(dve):
                    dve.memset(r.y[:, 0:1], 0.0).then_inc(sem.cleared, 1)
                    dve.memset(r.ys[:, 0:PREV], 0.0)
                    dve.memset(r.zeros[:, :, :], 0.0)
                    dve.memset(r.k_pair[:, :, :, :], 0.0)
                    dve.wait_ge(sem.cleared, 1)
                    dve.tensor_copy(r.ys[0:64, PREV:], r.y[0:64, 1:]).then_inc(sem.y_shifted, 1)
                    dve.tensor_copy(r.ys[64:128, PREV:], r.y[64:128, 0:T]).then_inc(sem.y_shifted, 1)

            layers(nc, r, sem, sb)

        with ExitStack() as own:
            out_sb = sb("out_sb", [P, TILES, P], within=own)
            with nc.Block() as block:

                @block.tensor
                def _(pe):
                    for t in range(TILES):
                        mm = pe.transpose(r.banks[t // 4][:, (t % 4) * P:(t % 4 + 1) * P], r.y[:, 1 + t * P:1 + (t + 1) * P], r.ident[:, :])
                        if t % 4 == 3:
                            mm.then_inc(sem.y_turned, 1)

                @block.vector
                def _(dve):
                    for q in range(4):
                        dve.wait_ge(sem.y_turned, q + 1)
                        dve.tensor_tensor(out_sb[:, 4 * q:4 * q + 4, :].rearrange("p t c -> p (t c)"),
                                          r.x[:, 4 * q:4 * q + 4, :].rearrange("p t c -> p (t c)"), r.banks[q][:, :], ALU.add
                                          ).then_inc(sem.out_summed, 1)

                @block.sync
                def _(sp):
                    to = out.rearrange("o (t p) c -> p (o t) c", p=P)
                    for q in range(4):
                        sp.wait_ge(sem.out_summed, q + 1)
                        sp.dma_start(to[:, 4 * q:4 * q + 4, :], out_sb[:, 4 * q:4 * q + 4, :]).then_inc(sem.out_stored, 16)
                    sp.wait_ge(sem.tables_loaded, 64 * (DEPTH + 1))
                    sp.wait_ge(sem.out_stored, 64)


LN_2_10 = 6.931471805599453


def layers(nc, r, sem, sb):
    r.work_ps = [r.banks[4], r.banks[5]]
    r.scores_ps = r.banks[0:4]
    r.pt_ps, r.out_ps = r.banks[6], r.banks[7]
    with nc.Fori(0, DEPTH) as L:
        with ExitStack() as a:
            r.raw_q = sb("raw_q", [P, 2, BT], within=a)
            r.raw_k = sb("raw_k", [P, 2, BT + PREV], within=a)
            r.squares = sb("squares", [P, 4, BT], within=a)
            r.inv_q = sb("inv_q", [P, BT], within=a)
            r.inv_k = sb("inv_k", [P, BT + PREV], within=a)
            r.prod_q = sb("prod_q", [P, 4, BT], within=a)
            r.prod_k = sb("prod_k", [P, 4, BT + PREV], within=a)
            r.rot_q = sb("rot_q", [P, 2, BT], within=a)
            r.rot_k = sb("rot_k", [P, 2, BT + PREV], within=a)
            r.q_pair = sb("q_pair", [P, 2, BT], within=a)
            r.v_win = sb("v_win", [P, 2, 8, GW], within=a)
            r.probs = sb("probs", [P, 4, 4 * KC], within=a)
            r.turned_sb = sb("turned_sb", [P, 2, BT], within=a)
            r.row_max = sb("row_max", [P, 4, 4], within=a)
            r.neg_max = sb("neg_max", [P, 4, 4], within=a)
            r.sums = sb("sums", [P, 4, 4], within=a)
            r.inv_sums = sb("inv_sums", [P, 4, 4], within=a)
            windowed_attention(nc, L, r, sem)
        with ExitStack() as f:
            r.shifted = sb("shifted", [P, 2, BT], within=f)
            r.centred = sb("centred", [P, 2, BT], within=f)
            r.centred_sq = sb("centred_sq", [P, 2, BT], within=f)
            r.log_var = sb("log_var", [P, BT], within=f)
            r.inv_std = sb("inv_std", [P, BT], within=f)
            r.scaled = sb("scaled", [P, 2, BT], within=f)
            r.normed = sb("normed", [P, BLOCKS, BT], within=f)
            r.gate = sb("gate", [P, 3, BT], within=f)
            r.inner = sb("inner", [P, 2, 3, BT], within=f)
            output_and_ffn(nc, L, r, sem)


def constants():
    import numpy as np
    c = {}
    c["ident"] = np.eye(P)
    c["ones32"] = np.kron(np.eye(4), np.ones((32, 32)))
    c["ones_mean"] = np.full((P, P), 1.0 / P)
    q = np.arange(P)[:, None] % QC
    key = np.arange(KC)[None, :] - PREV
    allowed = (key <= q) & (q <= key + WINDOW)
    mask = np.where(allowed, 0.0, -1e30)
    later = np.tile(mask, (1, 4))
    first = later.copy()
    for head in range(2):
        first[:QC, head * KC:head * KC + PREV] = -1e30
    c["mask"] = np.concatenate([first, later], 1)
    tri = np.where(np.arange(P)[None, :] > np.arange(P)[:, None], -1e30, 0.0)
    c["causal"] = np.concatenate([tri, tri.T], 1)
    c["iota8"] = np.tile(np.arange(8.0), (P, 1))
    half = np.arange(0, DH, 2, dtype=np.float64)[:, None]
    pos = np.arange(-PREV, BT, dtype=np.float64)[None, :]
    angle = pos / 10000.0 ** (half / DH)
    scale = ((half + 0.4 * DH) / (1.4 * DH)) ** ((pos - BT // 2) / (WINDOW // 2))
    tabs = [np.cos(angle) * scale, np.sin(angle) * scale, np.cos(angle) / scale, np.sin(angle) / scale]
    c["base_tab"] = np.concatenate([np.tile(t, (4, 1)) for t in tabs], 1)
    return np.concatenate([c[n] for n, _ in CONSTS], 1).astype(np.float32)


def kernel(**inputs):
    import numpy as np
    import concourse.bacc as bacc
    from concourse.bass_utils import run_bass_kernel_spmd
    nc = bacc.Bacc("TRN2", target_bir_lowering=False, num_devices=1)
    arrays, aps = {}, {}
    for name in INPUTS:
        a = np.ascontiguousarray(inputs[name])
        arrays["in_" + name] = a
        aps[name] = nc.dram_tensor("in_" + name, a.shape, mybir.dt.from_np(a.dtype), kind="ExternalInput").ap()
    arrays["constants"] = constants()
    const = nc.dram_tensor("constants", arrays["constants"].shape, fp32, kind="ExternalInput").ap()
    out = nc.dram_tensor("out", (1, T, P), fp32, kind="ExternalOutput").ap()
    program(nc, aps, const, out)
    got = run_bass_kernel_spmd(nc, [arrays], core_ids=[0])
    return got.results[0]["out"]
```
